# Optimizing a Trainium2 kernel written in Bass

```python
import numpy as np
import jax
import jax.numpy as jnp

def _softmax(x, axis=-1):
    return jax.nn.softmax(x, axis=axis)

def _gelu(x):
    return jax.nn.gelu(x, approximate=True)

def _silu(x):
    return jax.nn.silu(x)

def _sigmoid(x):
    return jax.nn.sigmoid(x)

def _layernorm(x, axis=-1, eps=1e-05):
    m = jnp.mean(x, axis=axis, keepdims=True)
    v = jnp.var(x, axis=axis, keepdims=True)
    return (x - m) / jnp.sqrt(v + eps)

def _scatter_add(tgt, idx, src, axis=0):
    return tgt.at[idx].add(src)

def _segment_sum(src, seg, n):
    return jax.ops.segment_sum(src, seg, n)
kernel_name = 'mk_pixart_seq_d4_seqx_r4_485b40'

def setup_inputs(seed: int=0):
    np.random.seed(seed)
    _w = jnp.asarray

    def _rec_inputs():
        import jax
        import jax.numpy as jnp
        _rk = jax.random.key(seed)
        x = -0.0003929 + 0.9999 * jax.random.normal(jax.random.fold_in(_rk, 1), (2, 1024, 256), jnp.float32)
        _lenS = 1024 - jax.random.randint(jax.random.fold_in(_rk, 7), (2,), 0, max(1, 1024 // 4) + 1, jnp.int32)
        _lenS2 = 77 - jax.random.randint(jax.random.fold_in(_rk, 8), (2,), 0, max(1, 77 // 4) + 1, jnp.int32)
        _ctx_1024P = jax.random.normal(jax.random.fold_in(_rk, 11), (2, 16, 256), jnp.float32)
        _ctx_1024c = jax.random.dirichlet(jax.random.fold_in(_rk, 511), 0.3 * jnp.ones((16,), jnp.float32), (2, 77))
        _ctx_1024t = jnp.einsum('bsk,bkd->bsd', _ctx_1024c, _ctx_1024P)
        _ctx_1024t = _ctx_1024t * jax.lax.rsqrt(jnp.mean(jnp.square(_ctx_1024t)) + 1e-12) * 0.953939
        ctx_1024 = -1.39393e-06 + 0.999914 * (_ctx_1024t + 0.3 * jax.random.normal(jax.random.fold_in(_rk, 611), (2, 77, 256), jnp.float32))
        cond_1024 = -0.00920427 + 1.00102 * jax.random.normal(jax.random.fold_in(_rk, 12), (2, 256), jnp.float32)
        return (x, ctx_1024, cond_1024)
    x, ctx_1024, cond_1024 = _rec_inputs()

    def _L0_xcond_setup():
        import jax, jax.numpy as jnp
        import numpy as np
        EPS = 1e-05

        def _ada_ln(x, c, W_ss, b_ss):
            mu = jnp.mean(x, axis=-1, keepdims=True)
            var = jnp.mean((x - mu) ** 2, axis=-1, keepdims=True)
            h = (x - mu) / jnp.sqrt(var + EPS)
            ss = jax.nn.silu(c) @ W_ss + b_ss
            scale, bias = jnp.split(ss, 2, axis=-1)
            return (1.0 + scale)[:, None, :] * h + bias[:, None, :]
        key = jax.random.key(seed)
        ks = jax.random.split(key, 12)
        B, Lq, Lkv, H = (8, 512, 128, 256)
        s = 0.02
        return {'x_q': jax.random.normal(ks[0], (B, Lq, H), jnp.float32), 'x_kv': jax.random.normal(ks[1], (B, Lkv, H), jnp.float32), 't_vec': jax.random.normal(ks[2], (B, H), jnp.float32), 'Wq': jax.random.normal(ks[3], (H, H), jnp.float32) * s, 'bq': jnp.zeros((H,), jnp.float32), 'Wkv': jax.random.normal(ks[4], (H, 2 * H), jnp.float32) * s, 'bkv': jnp.zeros((2 * H,), jnp.float32), 'Wp': jax.random.normal(ks[5], (H, H), jnp.float32) * s, 'bp': jnp.zeros((H,), jnp.float32), 'Wss_q': jax.random.normal(ks[6], (H, 2 * H), jnp.float32) * s, 'bss_q': jnp.zeros((2 * H,), jnp.float32), 'Wss_kv': jax.random.normal(ks[7], (H, 2 * H), jnp.float32) * s, 'bss_kv': jnp.zeros((2 * H,), jnp.float32)}
    _L0_xcond_all = _L0_xcond_setup()
    _L0_xcond_in = {k: v for k, v in _L0_xcond_all.items() if k in ('Wq', 'bq', 'Wkv', 'bkv', 'Wp', 'bp', 'Wss_q', 'bss_q', 'Wss_kv', 'bss_kv')}
    del _L0_xcond_all

    def _L1_xcond_setup():
        import jax, jax.numpy as jnp
        import numpy as np
        LN_EPS = 1e-06

        def _ln(x):
            mu = jnp.mean(x, axis=-1, keepdims=True)
            var = jnp.var(x, axis=-1, keepdims=True)
            return (x - mu) * jax.lax.rsqrt(var + LN_EPS)
        key = jax.random.key(seed)
        H, NH = (256, 16)
        B, N, S = (4, 256, 77)
        MLP = int(H * 4.0)
        ks = jax.random.split(key, 20)
        s = 1.0 / np.sqrt(H)
        return {'x': jax.random.normal(ks[0], (B, N, H), jnp.float32), 'c': jax.random.normal(ks[1], (B, H), jnp.float32), 'context': jax.random.normal(ks[2], (B, S, H), jnp.float32), 'W_mod': jax.random.normal(ks[3], (H, 6 * H), jnp.float32) * s, 'b_mod': jnp.zeros((6 * H,), jnp.float32), 'W_qkv': jax.random.normal(ks[4], (H, 3 * H), jnp.float32) * s, 'b_qkv': jnp.zeros((3 * H,), jnp.float32), 'W_proj': jax.random.normal(ks[5], (H, H), jnp.float32) * s, 'b_proj': jnp.zeros((H,), jnp.float32), 'W_qc': jax.random.normal(ks[6], (H, H), jnp.float32) * s, 'b_qc': jnp.zeros((H,), jnp.float32), 'W_kvc': jax.random.normal(ks[7], (H, 2 * H), jnp.float32) * s, 'b_kvc': jnp.zeros((2 * H,), jnp.float32), 'W_cproj': jax.random.normal(ks[8], (H, H), jnp.float32) * s, 'b_cproj': jnp.zeros((H,), jnp.float32), 'W_mlp1': jax.random.normal(ks[9], (H, MLP), jnp.float32) * s, 'b_mlp1': jnp.zeros((MLP,), jnp.float32), 'W_mlp2': jax.random.normal(ks[10], (MLP, H), jnp.float32) * (1.0 / np.sqrt(MLP)), 'b_mlp2': jnp.zeros((H,), jnp.float32)}
    _L1_xcond_all = _L1_xcond_setup()
    _L1_xcond_in = {k: v for k, v in _L1_xcond_all.items() if k in ('W_mod', 'b_mod', 'W_qkv', 'b_qkv', 'W_proj', 'b_proj', 'W_qc', 'b_qc', 'W_kvc', 'b_kvc', 'W_cproj', 'b_cproj', 'W_mlp1', 'b_mlp1', 'W_mlp2', 'b_mlp2')}
    del _L1_xcond_all

    def _L2_xcond_setup():
        import jax, jax.numpy as jnp
        import numpy as np
        C = 256
        H = 16
        D = C // H
        WIN = 128
        SHIFT = 64
        TOPK = 16
        HID = 1024
        EPS = 1e-06

        def _ln(x):
            x32 = x.astype(jnp.float32)
            m = x32.mean(-1, keepdims=True)
            v = jnp.mean((x32 - m) ** 2, axis=-1, keepdims=True)
            return ((x32 - m) * jax.lax.rsqrt(v + EPS)).astype(x.dtype)

        def _self_attn(h, w_qkv, b_qkv, w_so, b_so):
            B, L, _ = h.shape
            qkv = h @ w_qkv + b_qkv
            qkv = jnp.roll(qkv, -SHIFT, axis=1)
            nw = L // WIN
            qkv = qkv.reshape(B, nw, WIN, 3, H, D)
            q, k, v = (qkv[:, :, :, 0], qkv[:, :, :, 1], qkv[:, :, :, 2])
            scores = jnp.einsum('bnqhd,bnkhd->bnhqk', q, k) / jnp.sqrt(jnp.float32(D)).astype(h.dtype)
            attn = jax.nn.softmax(scores, axis=-1)
            o = jnp.einsum('bnhqk,bnkhd->bnqhd', attn, v).reshape(B, L, C)
            o = jnp.roll(o, SHIFT, axis=1)
            return o @ w_so + b_so

        def _topk_cross_attn(h, ctx, w_q, b_q, w_kv, b_kv, w_co, b_co):
            B, L, _ = h.shape
            Lc = ctx.shape[1]
            q = (h @ w_q + b_q).reshape(B, L, H, D)
            kv = (ctx @ w_kv + b_kv).reshape(B, Lc, 2, H, D)
            k, v = (kv[:, :, 0], kv[:, :, 1])
            scores = jnp.einsum('bqhd,bkhd->bhqk', q, k) / jnp.sqrt(jnp.float32(D)).astype(h.dtype)
            top_s, top_i = jax.lax.top_k(scores, TOPK)
            attn = jax.nn.softmax(top_s, axis=-1)
            v_bh = jnp.transpose(v, (0, 2, 1, 3))
            vg = jnp.take_along_axis(v_bh[:, :, None, :, :], top_i[..., None], axis=3)
            o = jnp.einsum('bhqk,bhqkd->bqhd', attn, vg).reshape(B, L, C)
            return o @ w_co + b_co

        def _swiglu(h, w_m1, b_m1, w_m2, b_m2):
            u = h @ w_m1 + b_m1
            a, b = (u[..., :HID], u[..., HID:])
            return jax.nn.silu(a) * b @ w_m2 + b_m2
        key = jax.random.key(seed)
        ks = jax.random.split(key, 24)
        s = 0.02
        inp = {'x': jax.random.normal(ks[0], (2, 1024, C), jnp.float32), 'mod': jax.random.normal(ks[1], (2, C), jnp.float32), 'context': jax.random.normal(ks[2], (2, 256, C), jnp.float32), 'w_ada': jax.random.normal(ks[3], (C, 9 * C), jnp.float32) * s, 'b_ada': jnp.zeros((9 * C,), jnp.float32), 'w_qkv': jax.random.normal(ks[4], (C, 3 * C), jnp.float32) * s, 'b_qkv': jnp.zeros((3 * C,), jnp.float32), 'w_so': jax.random.normal(ks[5], (C, C), jnp.float32) * s, 'b_so': jnp.zeros((C,), jnp.float32), 'w_q': jax.random.normal(ks[6], (C, C), jnp.float32) * s, 'b_q': jnp.zeros((C,), jnp.float32), 'w_kv': jax.random.normal(ks[7], (C, 2 * C), jnp.float32) * s, 'b_kv': jnp.zeros((2 * C,), jnp.float32), 'w_co': jax.random.normal(ks[8], (C, C), jnp.float32) * s, 'b_co': jnp.zeros((C,), jnp.float32), 'w_m1': jax.random.normal(ks[9], (C, 2 * HID), jnp.float32) * s, 'b_m1': jnp.zeros((2 * HID,), jnp.float32), 'w_m2': jax.random.normal(ks[10], (HID, C), jnp.float32) * s, 'b_m2': jnp.zeros((C,), jnp.float32)}
        return inp
    _L2_xcond_all = _L2_xcond_setup()
    _L2_xcond_in = {k: v for k, v in _L2_xcond_all.items() if k in ('w_ada', 'b_ada', 'w_qkv', 'b_qkv', 'w_so', 'b_so', 'w_q', 'b_q', 'w_kv', 'b_kv', 'w_co', 'b_co', 'w_m1', 'b_m1', 'w_m2', 'b_m2')}
    del _L2_xcond_all

    def _L3_xcond_setup():
        import jax, jax.numpy as jnp
        import numpy as np
        H = 256
        RH = 2 * H
        E = 3
        B, T, P = (8, 512, 64)
        LN_EPS = 1e-05

        def _layer_norm(x, gamma, beta):
            mu = jnp.mean(x, axis=-1, keepdims=True)
            var = jnp.mean(jnp.square(x - mu), axis=-1, keepdims=True)
            return (x - mu) * jax.lax.rsqrt(var + LN_EPS) * gamma + beta
        key = jax.random.key(seed)
        ks = jax.random.split(key, 24)
        s = lambda fan_in: 1.0 / np.sqrt(fan_in)
        inp = {'mix_hidden_states': jax.random.normal(ks[0], (B, T, H), jnp.float32), 'global_anchor': jax.random.normal(ks[1], (B, H), jnp.float32), 'prototype_bank': jax.random.normal(ks[2], (B, P, H), jnp.float32), 'ln_gamma': jnp.ones((H,), jnp.float32), 'ln_beta': jnp.zeros((H,), jnp.float32), 'Wq': jax.random.normal(ks[3], (H, H), jnp.float32) * s(H), 'Wk': jax.random.normal(ks[4], (H, H), jnp.float32) * s(H), 'Wv': jax.random.normal(ks[5], (H, H), jnp.float32) * s(H), 'router_W': jax.random.normal(ks[6], (3 * H, E), jnp.float32) * s(3 * H), 'router_b': jnp.zeros((E,), jnp.float32), 'e_w1': jax.random.normal(ks[7], (E, 3 * H, RH), jnp.float32) * s(3 * H), 'e_b1': jnp.zeros((E, RH), jnp.float32), 'e_w2': jax.random.normal(ks[8], (E, RH, H), jnp.float32) * s(RH), 'e_b2': jnp.zeros((E, H), jnp.float32), 'gate_w1': jax.random.normal(ks[9], (3 * H, H), jnp.float32) * s(3 * H), 'gate_b1': jnp.zeros((H,), jnp.float32), 'gate_w2': jax.random.normal(ks[10], (H, H), jnp.float32) * s(H), 'gate_b2': jnp.zeros((H,), jnp.float32), 'out_w': jax.random.normal(ks[11], (H, H), jnp.float32) * s(H), 'out_b': jnp.zeros((H,), jnp.float32)}
        return inp
    _L3_xcond_all = _L3_xcond_setup()
    _L3_xcond_in = {k: v for k, v in _L3_xcond_all.items() if k in ('ln_gamma', 'ln_beta', 'Wq', 'Wk', 'Wv', 'router_W', 'router_b', 'e_w1', 'e_b1', 'e_w2', 'e_b2', 'gate_w1', 'gate_b1', 'gate_w2', 'gate_b2', 'out_w', 'out_b')}
    del _L3_xcond_all
    return {'x': x, 'ctx_1024': ctx_1024, 'cond_1024': cond_1024, 'L0_xcond_Wq': _L0_xcond_in['Wq'], 'L0_xcond_bq': _L0_xcond_in['bq'], 'L0_xcond_Wkv': _L0_xcond_in['Wkv'], 'L0_xcond_bkv': _L0_xcond_in['bkv'], 'L0_xcond_Wp': _L0_xcond_in['Wp'], 'L0_xcond_bp': _L0_xcond_in['bp'], 'L0_xcond_Wss_q': _L0_xcond_in['Wss_q'], 'L0_xcond_bss_q': _L0_xcond_in['bss_q'], 'L0_xcond_Wss_kv': _L0_xcond_in['Wss_kv'], 'L0_xcond_bss_kv': _L0_xcond_in['bss_kv'], 'L1_xcond_W_mod': _L1_xcond_in['W_mod'], 'L1_xcond_b_mod': _L1_xcond_in['b_mod'], 'L1_xcond_W_qkv': _L1_xcond_in['W_qkv'], 'L1_xcond_b_qkv': _L1_xcond_in['b_qkv'], 'L1_xcond_W_proj': _L1_xcond_in['W_proj'], 'L1_xcond_b_proj': _L1_xcond_in['b_proj'], 'L1_xcond_W_qc': _L1_xcond_in['W_qc'], 'L1_xcond_b_qc': _L1_xcond_in['b_qc'], 'L1_xcond_W_kvc': _L1_xcond_in['W_kvc'], 'L1_xcond_b_kvc': _L1_xcond_in['b_kvc'], 'L1_xcond_W_cproj': _L1_xcond_in['W_cproj'], 'L1_xcond_b_cproj': _L1_xcond_in['b_cproj'], 'L1_xcond_W_mlp1': _L1_xcond_in['W_mlp1'], 'L1_xcond_b_mlp1': _L1_xcond_in['b_mlp1'], 'L1_xcond_W_mlp2': _L1_xcond_in['W_mlp2'], 'L1_xcond_b_mlp2': _L1_xcond_in['b_mlp2'], 'L2_xcond_w_ada': _L2_xcond_in['w_ada'], 'L2_xcond_b_ada': _L2_xcond_in['b_ada'], 'L2_xcond_w_qkv': _L2_xcond_in['w_qkv'], 'L2_xcond_b_qkv': _L2_xcond_in['b_qkv'], 'L2_xcond_w_so': _L2_xcond_in['w_so'], 'L2_xcond_b_so': _L2_xcond_in['b_so'], 'L2_xcond_w_q': _L2_xcond_in['w_q'], 'L2_xcond_b_q': _L2_xcond_in['b_q'], 'L2_xcond_w_kv': _L2_xcond_in['w_kv'], 'L2_xcond_b_kv': _L2_xcond_in['b_kv'], 'L2_xcond_w_co': _L2_xcond_in['w_co'], 'L2_xcond_b_co': _L2_xcond_in['b_co'], 'L2_xcond_w_m1': _L2_xcond_in['w_m1'], 'L2_xcond_b_m1': _L2_xcond_in['b_m1'], 'L2_xcond_w_m2': _L2_xcond_in['w_m2'], 'L2_xcond_b_m2': _L2_xcond_in['b_m2'], 'L3_xcond_ln_gamma': _L3_xcond_in['ln_gamma'], 'L3_xcond_ln_beta': _L3_xcond_in['ln_beta'], 'L3_xcond_Wq': _L3_xcond_in['Wq'], 'L3_xcond_Wk': _L3_xcond_in['Wk'], 'L3_xcond_Wv': _L3_xcond_in['Wv'], 'L3_xcond_router_W': _L3_xcond_in['router_W'], 'L3_xcond_router_b': _L3_xcond_in['router_b'], 'L3_xcond_e_w1': _L3_xcond_in['e_w1'], 'L3_xcond_e_b1': _L3_xcond_in['e_b1'], 'L3_xcond_e_w2': _L3_xcond_in['e_w2'], 'L3_xcond_e_b2': _L3_xcond_in['e_b2'], 'L3_xcond_gate_w1': _L3_xcond_in['gate_w1'], 'L3_xcond_gate_b1': _L3_xcond_in['gate_b1'], 'L3_xcond_gate_w2': _L3_xcond_in['gate_w2'], 'L3_xcond_gate_b2': _L3_xcond_in['gate_b2'], 'L3_xcond_out_w': _L3_xcond_in['out_w'], 'L3_xcond_out_b': _L3_xcond_in['out_b']}

def reference(x, ctx_1024, cond_1024, L0_xcond_Wq, L0_xcond_bq, L0_xcond_Wkv, L0_xcond_bkv, L0_xcond_Wp, L0_xcond_bp, L0_xcond_Wss_q, L0_xcond_bss_q, L0_xcond_Wss_kv, L0_xcond_bss_kv, L1_xcond_W_mod, L1_xcond_b_mod, L1_xcond_W_qkv, L1_xcond_b_qkv, L1_xcond_W_proj, L1_xcond_b_proj, L1_xcond_W_qc, L1_xcond_b_qc, L1_xcond_W_kvc, L1_xcond_b_kvc, L1_xcond_W_cproj, L1_xcond_b_cproj, L1_xcond_W_mlp1, L1_xcond_b_mlp1, L1_xcond_W_mlp2, L1_xcond_b_mlp2, L2_xcond_w_ada, L2_xcond_b_ada, L2_xcond_w_qkv, L2_xcond_b_qkv, L2_xcond_w_so, L2_xcond_b_so, L2_xcond_w_q, L2_xcond_b_q, L2_xcond_w_kv, L2_xcond_b_kv, L2_xcond_w_co, L2_xcond_b_co, L2_xcond_w_m1, L2_xcond_b_m1, L2_xcond_w_m2, L2_xcond_b_m2, L3_xcond_ln_gamma, L3_xcond_ln_beta, L3_xcond_Wq, L3_xcond_Wk, L3_xcond_Wv, L3_xcond_router_W, L3_xcond_router_b, L3_xcond_e_w1, L3_xcond_e_b1, L3_xcond_e_w2, L3_xcond_e_b2, L3_xcond_gate_w1, L3_xcond_gate_b1, L3_xcond_gate_w2, L3_xcond_gate_b2, L3_xcond_out_w, L3_xcond_out_b):
    import jax
    import jax.numpy as jnp

    def _L0_xcond_ref(x_q, x_kv, t_vec, Wq, bq, Wkv, bkv, Wp, bp, Wss_q, bss_q, Wss_kv, bss_kv):
        import jax, jax.numpy as jnp
        import numpy as np
        EPS = 1e-05

        def _ada_ln(x, c, W_ss, b_ss):
            mu = jnp.mean(x, axis=-1, keepdims=True)
            var = jnp.mean((x - mu) ** 2, axis=-1, keepdims=True)
            h = (x - mu) / jnp.sqrt(var + EPS)
            ss = jax.nn.silu(c) @ W_ss + b_ss
            scale, bias = jnp.split(ss, 2, axis=-1)
            return (1.0 + scale)[:, None, :] * h + bias[:, None, :]
        B, Lq, H = x_q.shape
        Lkv = x_kv.shape[1]
        nh = 16
        dh = H // nh
        xq = _ada_ln(x_q, t_vec, Wss_q, bss_q)
        xkv = _ada_ln(x_kv, t_vec, Wss_kv, bss_kv)
        q = (xq @ Wq + bq).reshape(B, Lq, nh, dh)
        kv = (xkv @ Wkv + bkv).reshape(B, Lkv, 2, nh, dh)
        k = kv[:, :, 0]
        v = kv[:, :, 1]
        scores = jnp.einsum('bqhd,bkhd->bhqk', q, k) / jnp.sqrt(jnp.float32(dh))
        attn = jax.nn.softmax(scores, axis=-1)
        out = jnp.einsum('bhqk,bkhd->bqhd', attn, v).reshape(B, Lq, H)
        return x_q + (out @ Wp + bp)

    def _L1_xcond_ref(x, c, context, W_mod, b_mod, W_qkv, b_qkv, W_proj, b_proj, W_qc, b_qc, W_kvc, b_kvc, W_cproj, b_cproj, W_mlp1, b_mlp1, W_mlp2, b_mlp2):
        import jax, jax.numpy as jnp
        import numpy as np
        LN_EPS = 1e-06

        def _ln(x):
            mu = jnp.mean(x, axis=-1, keepdims=True)
            var = jnp.var(x, axis=-1, keepdims=True)
            return (x - mu) * jax.lax.rsqrt(var + LN_EPS)
        B, N, H = x.shape
        NH = 16
        hd = H // NH
        scale = hd ** (-0.5)
        c_proj = jax.nn.silu(c) @ W_mod + b_mod
        shift_a, scale_a, gate_a, shift_m, scale_m, gate_m = jnp.split(c_proj, 6, axis=-1)

        def modulate(t, shift, sc):
            return t * (1 + sc[:, None]) + shift[:, None]
        x_norm = modulate(_ln(x), shift_a, scale_a)
        qkv = x_norm @ W_qkv + b_qkv
        q, k, v = jnp.split(qkv, 3, axis=-1)
        q = q.reshape(B, N, NH, hd).transpose(0, 2, 1, 3)
        k = k.reshape(B, N, NH, hd).transpose(0, 2, 1, 3)
        v = v.reshape(B, N, NH, hd).transpose(0, 2, 1, 3)
        attn_w = jax.nn.softmax(jnp.einsum('bhqd,bhkd->bhqk', q, k) * scale, axis=-1)
        attn_out = jnp.einsum('bhqk,bhkd->bhqd', attn_w, v)
        attn_out = attn_out.transpose(0, 2, 1, 3).reshape(B, N, H)
        attn_out = attn_out @ W_proj + b_proj
        x = x + gate_a[:, None] * attn_out
        S = context.shape[1]
        q_c = _ln(x) @ W_qc + b_qc
        kv_c = _ln(context) @ W_kvc + b_kvc
        k_c, v_c = jnp.split(kv_c, 2, axis=-1)
        q_c = q_c.reshape(B, N, NH, hd).transpose(0, 2, 1, 3)
        k_c = k_c.reshape(B, S, NH, hd).transpose(0, 2, 1, 3)
        v_c = v_c.reshape(B, S, NH, hd).transpose(0, 2, 1, 3)
        c_attn_w = jax.nn.softmax(jnp.einsum('bhqd,bhsd->bhqs', q_c, k_c) * scale, axis=-1)
        c_attn_out = jnp.einsum('bhqs,bhsd->bhqd', c_attn_w, v_c)
        c_attn_out = c_attn_out.transpose(0, 2, 1, 3).reshape(B, N, H)
        c_attn_out = c_attn_out @ W_cproj + b_cproj
        x = x + c_attn_out
        x_norm2 = modulate(_ln(x), shift_m, scale_m)
        h = jax.nn.gelu(x_norm2 @ W_mlp1 + b_mlp1)
        h = h @ W_mlp2 + b_mlp2
        x = x + gate_m[:, None] * h
        return x

    def _L2_xcond_ref(x, mod, context, w_ada, b_ada, w_qkv, b_qkv, w_so, b_so, w_q, b_q, w_kv, b_kv, w_co, b_co, w_m1, b_m1, w_m2, b_m2):
        import jax, jax.numpy as jnp
        import numpy as np
        C = 256
        H = 16
        D = C // H
        WIN = 128
        SHIFT = 64
        TOPK = 16
        HID = 1024
        EPS = 1e-06

        def _ln(x):
            x32 = x.astype(jnp.float32)
            m = x32.mean(-1, keepdims=True)
            v = jnp.mean((x32 - m) ** 2, axis=-1, keepdims=True)
            return ((x32 - m) * jax.lax.rsqrt(v + EPS)).astype(x.dtype)

        def _self_attn(h, w_qkv, b_qkv, w_so, b_so):
            B, L, _ = h.shape
            qkv = h @ w_qkv + b_qkv
            qkv = jnp.roll(qkv, -SHIFT, axis=1)
            nw = L // WIN
            qkv = qkv.reshape(B, nw, WIN, 3, H, D)
            q, k, v = (qkv[:, :, :, 0], qkv[:, :, :, 1], qkv[:, :, :, 2])
            scores = jnp.einsum('bnqhd,bnkhd->bnhqk', q, k) / jnp.sqrt(jnp.float32(D)).astype(h.dtype)
            attn = jax.nn.softmax(scores, axis=-1)
            o = jnp.einsum('bnhqk,bnkhd->bnqhd', attn, v).reshape(B, L, C)
            o = jnp.roll(o, SHIFT, axis=1)
            return o @ w_so + b_so

        def _topk_cross_attn(h, ctx, w_q, b_q, w_kv, b_kv, w_co, b_co):
            B, L, _ = h.shape
            Lc = ctx.shape[1]
            q = (h @ w_q + b_q).reshape(B, L, H, D)
            kv = (ctx @ w_kv + b_kv).reshape(B, Lc, 2, H, D)
            k, v = (kv[:, :, 0], kv[:, :, 1])
            scores = jnp.einsum('bqhd,bkhd->bhqk', q, k) / jnp.sqrt(jnp.float32(D)).astype(h.dtype)
            top_s, top_i = jax.lax.top_k(scores, TOPK)
            attn = jax.nn.softmax(top_s, axis=-1)
            v_bh = jnp.transpose(v, (0, 2, 1, 3))
            vg = jnp.take_along_axis(v_bh[:, :, None, :, :], top_i[..., None], axis=3)
            o = jnp.einsum('bhqk,bhqkd->bqhd', attn, vg).reshape(B, L, C)
            return o @ w_co + b_co

        def _swiglu(h, w_m1, b_m1, w_m2, b_m2):
            u = h @ w_m1 + b_m1
            a, b = (u[..., :HID], u[..., HID:])
            return jax.nn.silu(a) * b @ w_m2 + b_m2
        m = jax.nn.silu(mod) @ w_ada + b_ada
        sh_msa, sc_msa, g_msa, sh_mca, sc_mca, g_mca, sh_mlp, sc_mlp, g_mlp = [m[:, i * C:(i + 1) * C][:, None, :] for i in range(9)]
        h = _ln(x) * (1 + sc_msa) + sh_msa
        h = _self_attn(h, w_qkv, b_qkv, w_so, b_so)
        x = x + h * g_msa
        h = _ln(x) * (1 + sc_mca) + sh_mca
        h = _topk_cross_attn(h, context, w_q, b_q, w_kv, b_kv, w_co, b_co)
        x = x + h * g_mca
        h = _ln(x) * (1 + sc_mlp) + sh_mlp
        h = _swiglu(h, w_m1, b_m1, w_m2, b_m2)
        x = x + h * g_mlp
        return x

    def _L3_xcond_ref(mix_hidden_states, global_anchor, prototype_bank, ln_gamma, ln_beta, Wq, Wk, Wv, router_W, router_b, e_w1, e_b1, e_w2, e_b2, gate_w1, gate_b1, gate_w2, gate_b2, out_w, out_b):
        import jax, jax.numpy as jnp
        import numpy as np
        H = 256
        RH = 2 * H
        E = 3
        B, T, P = (8, 512, 64)
        LN_EPS = 1e-05

        def _layer_norm(x, gamma, beta):
            mu = jnp.mean(x, axis=-1, keepdims=True)
            var = jnp.mean(jnp.square(x - mu), axis=-1, keepdims=True)
            return (x - mu) * jax.lax.rsqrt(var + LN_EPS) * gamma + beta
        x = mix_hidden_states
        nx = _layer_norm(x, ln_gamma, ln_beta)
        q = nx @ Wq
        k = prototype_bank @ Wk
        v = prototype_bank @ Wv
        scores = jnp.einsum('bth,bph->btp', q, k) * H ** (-0.5)
        weights = jax.nn.softmax(scores, axis=-1)
        evidence = jnp.einsum('btp,bph->bth', weights, v)
        anchor = jnp.broadcast_to(global_anchor[:, None, :], nx.shape)
        combined = jnp.concatenate([nx, evidence, anchor], axis=-1)
        router_logits = combined @ router_W + router_b
        router_probs = jax.nn.softmax(router_logits, axis=-1)
        h = jax.nn.silu(jnp.einsum('btc,ecr->bter', combined, e_w1) + e_b1)
        expert_out = jnp.einsum('bter,erh->bteh', h, e_w2) + e_b2
        routed = jnp.sum(expert_out * router_probs[..., None], axis=-2)
        g = jax.nn.sigmoid(jax.nn.silu(combined @ gate_w1 + gate_b1) @ gate_w2 + gate_b2)
        refined_delta = g * (routed @ out_w + out_b)
        return x + refined_delta
    x = _L0_xcond_ref(x, ctx_1024, cond_1024, L0_xcond_Wq, L0_xcond_bq, L0_xcond_Wkv, L0_xcond_bkv, L0_xcond_Wp, L0_xcond_bp, L0_xcond_Wss_q, L0_xcond_bss_q, L0_xcond_Wss_kv, L0_xcond_bss_kv)
    x = _L1_xcond_ref(x, cond_1024, ctx_1024, L1_xcond_W_mod, L1_xcond_b_mod, L1_xcond_W_qkv, L1_xcond_b_qkv, L1_xcond_W_proj, L1_xcond_b_proj, L1_xcond_W_qc, L1_xcond_b_qc, L1_xcond_W_kvc, L1_xcond_b_kvc, L1_xcond_W_cproj, L1_xcond_b_cproj, L1_xcond_W_mlp1, L1_xcond_b_mlp1, L1_xcond_W_mlp2, L1_xcond_b_mlp2)
    x = _L2_xcond_ref(x, cond_1024, ctx_1024, L2_xcond_w_ada, L2_xcond_b_ada, L2_xcond_w_qkv, L2_xcond_b_qkv, L2_xcond_w_so, L2_xcond_b_so, L2_xcond_w_q, L2_xcond_b_q, L2_xcond_w_kv, L2_xcond_b_kv, L2_xcond_w_co, L2_xcond_b_co, L2_xcond_w_m1, L2_xcond_b_m1, L2_xcond_w_m2, L2_xcond_b_m2)
    x = _L3_xcond_ref(x, cond_1024, ctx_1024, L3_xcond_ln_gamma, L3_xcond_ln_beta, L3_xcond_Wq, L3_xcond_Wk, L3_xcond_Wv, L3_xcond_router_W, L3_xcond_router_b, L3_xcond_e_w1, L3_xcond_e_b1, L3_xcond_e_w2, L3_xcond_e_b2, L3_xcond_gate_w1, L3_xcond_gate_b1, L3_xcond_gate_w2, L3_xcond_gate_b2, L3_xcond_out_w, L3_xcond_out_b)
    return x

_drawn_inputs = setup_inputs


def setup_inputs(seed=0):
    import zlib

    import numpy as np

    out = dict(_drawn_inputs(seed))
    spreads = {'L0_xcond_bq': (0.0, 2.0),
     'L0_xcond_bkv': (0.0, 0.1),
     'L0_xcond_bp': (0.0, 0.1),
     'L0_xcond_bss_q': (0.0, 0.8),
     'L0_xcond_bss_kv': (0.0, 0.611),
     'L1_xcond_b_mod': (0.0, 0.1),
     'L1_xcond_b_qkv': (0.0, 0.1),
     'L1_xcond_b_proj': (0.0, 0.1),
     'L1_xcond_b_qc': (0.0, 0.52),
     'L1_xcond_b_kvc': (0.0, 0.1),
     'L1_xcond_b_cproj': (0.0, 0.1),
     'L1_xcond_b_mlp1': (0.0, 0.1),
     'L1_xcond_b_mlp2': (0.0, 0.1),
     'L2_xcond_b_ada': (0.0, 0.554),
     'L2_xcond_b_qkv': (0.0, 0.8),
     'L2_xcond_b_so': (0.0, 0.457),
     'L2_xcond_b_q': (0.0, 0.8),
     'L2_xcond_b_kv': (0.0, 0.8),
     'L2_xcond_b_co': (0.0, 0.488),
     'L2_xcond_b_m1': (0.0, 0.8),
     'L2_xcond_b_m2': (0.0, 2.0),
     'L3_xcond_ln_gamma': (1.0, 0.6),
     'L3_xcond_ln_beta': (0.0, 2.0),
     'L3_xcond_router_b': (0.0, 2.0),
     'L3_xcond_e_b1': (0.0, 2.0),
     'L3_xcond_e_b2': (0.0, 2.0),
     'L3_xcond_gate_b1': (0.0, 2.0),
     'L3_xcond_gate_b2': (0.0, 2.0),
     'L3_xcond_out_b': (0.0, 0.8)}
    factors = {'L0_xcond_Wq': 8.0,
     'L0_xcond_Wss_q': 8.0,
     'L2_xcond_w_qkv': 5.234,
     'L2_xcond_w_so': 4.561,
     'L2_xcond_w_q': 8.0,
     'L2_xcond_w_kv': 5.956,
     'L2_xcond_w_co': 5.246,
     'L2_xcond_w_m1': 8.0,
     'L2_xcond_w_m2': 8.0,
     'L3_xcond_Wq': 8.0,
     'L3_xcond_Wk': 8.0,
     'L3_xcond_Wv': 8.0,
     'L3_xcond_router_W': 6.683,
     'L3_xcond_e_w1': 4.779,
     'L3_xcond_e_w2': 3.897,
     'L3_xcond_gate_w1': 8.0,
     'L3_xcond_gate_w2': 8.0,
     'L3_xcond_out_w': 3.821}
    for name, (base, spread) in spreads.items():
        noise = np.random.default_rng([zlib.crc32(name.encode()), seed]).standard_normal(out[name].shape)
        drawn = base * np.exp(spread * noise) if base else spread * noise
        out[name] = jnp.asarray(drawn.astype(out[name].dtype))
    for name, factor in factors.items():
        out[name] = (out[name] * factor).astype(out[name].dtype)
    return out
```

```python
from contextlib import ExitStack

import concourse.bass as bass
from concourse import mybir

P = 128
ALU = mybir.AluOpType
ACT = mybir.ActivationFunctionType
AX = mybir.AxisListType
F32 = mybir.dt.float32
F16 = mybir.dt.float16
U32 = mybir.dt.uint32

B, L, C = 2, 1024, 256
TB = L // P
CC = C // P
H, D = 16, 16
S = 77
HP = H // 2
GH = 4
RP = 3
SCALE = 0.25
TOPK_GONE = -3.0e38
SHIFT = 64
N1, N2, NE = 8, 8, 3
RH = 2 * C
SLOT = 1024
ROWM = 32

COLUMN_ROWS = [
    ("cond_1024", 0, 4),
    ("L0_xcond_bq", 0, 2), ("L0_xcond_bkv", 0, 2), ("L0_xcond_bss_q", 0, 4), ("L0_xcond_bss_kv", 0, 4),
    ("L1_xcond_b_mod", 0, 12), ("L1_xcond_b_qkv", 0, 4), ("L1_xcond_b_qc", 0, 2), ("L1_xcond_b_kvc", 0, 2),
    ("L1_xcond_b_mlp1", 0, 8),
    ("L2_xcond_b_ada", 0, 18), ("L2_xcond_b_qkv", 0, 4), ("L2_xcond_b_q", 0, 2), ("L2_xcond_b_kv", 0, 2),
    ("L2_xcond_b_m1", 0, 16),
    ("L3_xcond_ln_gamma", 0, 2), ("L3_xcond_ln_beta", 0, 2), ("L3_xcond_e_b1", 0, 12), ("L3_xcond_gate_b1", 0, 2),
]
COL = {}
NCOL = 0
for _name, _, _n in COLUMN_ROWS:
    COL[_name] = NCOL
    NCOL += _n

ATT = {
    "x0": dict(kind="cross", half=0, w=["L0_xcond_Wq", "L0_xcond_Wkv", "L0_xcond_Wp"], n=[256, 512, 256],
               vb=("L0_xcond_bkv", 256), ob="L0_xcond_bp", qb=COL["L0_xcond_bq"], kb=COL["L0_xcond_bkv"], ln=0, gate=None),
    "s1": dict(kind="self", half=1, w=["L1_xcond_W_qkv", "L1_xcond_W_proj"], n=[768, 256],
               vb=("L1_xcond_b_qkv", 512), ob="L1_xcond_b_proj", qb=COL["L1_xcond_b_qkv"], kb=COL["L1_xcond_b_qkv"] + 2, ln=1, gate=0),
    "x1": dict(kind="cross", half=0, w=["L1_xcond_W_qc", "L1_xcond_W_kvc", "L1_xcond_W_cproj"], n=[256, 512, 256],
               vb=("L1_xcond_b_kvc", 256), ob="L1_xcond_b_cproj", qb=COL["L1_xcond_b_qc"], kb=COL["L1_xcond_b_kvc"], ln=2, gate=None),
    "w2": dict(kind="win", half=1, w=["L2_xcond_w_qkv", "L2_xcond_w_so"], n=[768, 256],
               vb=("L2_xcond_b_qkv", 512), ob="L2_xcond_b_so", qb=COL["L2_xcond_b_qkv"], kb=COL["L2_xcond_b_qkv"] + 2, ln=4, gate=2),
    "t2": dict(kind="top", half=0, w=["L2_xcond_w_q", "L2_xcond_w_kv", "L2_xcond_w_co"], n=[256, 512, 256],
               vb=("L2_xcond_b_kv", 256), ob="L2_xcond_b_co", qb=COL["L2_xcond_b_q"], kb=COL["L2_xcond_b_kv"], ln=5, gate=3),
}
ATT_ORDER = ["x0", "s1", "x1", "w2", "t2"]
MLP = {
    "m1": dict(ln=3, gate=1, w=["L1_xcond_W_mlp1", "L1_xcond_W_mlp2"], n=[1024, 256], ob="L1_xcond_b_mlp2", hb=COL["L1_xcond_b_mlp1"]),
    "m2": dict(ln=6, gate=4, w=["L2_xcond_w_m1", "L2_xcond_w_m2"], n=[2048, 256], ob="L2_xcond_b_m2", hb=COL["L2_xcond_b_m1"]),
}
LN_EPS = [1e-5, 1e-6, 1e-6, 1e-6, 1e-6, 1e-6, 1e-6, 1e-5]
GATES = [(1, 2), (1, 5), (2, 2), (2, 5), (2, 8)]
MODS = ([("ssq", i, i < 2) for i in range(4)] + [("sskv", i, i < 2) for i in range(4)]
        + [("mod1", i, i in (2, 3, 8, 9)) for i in (0, 1, 2, 3, 6, 7, 8, 9)]
        + [("ada2", i, i in (2, 3, 8, 9, 14, 15)) for i in (0, 1, 2, 3, 6, 7, 8, 9, 12, 13, 14, 15)])
MOD_AT = {(w, i): n for n, (w, i, _) in enumerate(MODS)}
MOD_COL = {"ssq": COL["L0_xcond_bss_q"], "sskv": COL["L0_xcond_bss_kv"], "mod1": COL["L1_xcond_b_mod"], "ada2": COL["L2_xcond_b_ada"]}
LN_MOD = {0: ("ssq", 0, 2), 1: ("mod1", 2, 0), 3: ("mod1", 8, 6), 4: ("ada2", 2, 0), 5: ("ada2", 8, 6), 6: ("ada2", 14, 12)}


def schedule(stop):
    out = [("prep",)]

    def attention(a):
        if ATT[a]["kind"] in ("cross", "top"):
            out.append(("ckv", a))
        for b in range(B):
            out.extend([("ln", ATT[a]["ln"], b), ("proj", a, b), ("attn", a, b), ("post", a, b)])

    def mlp(m):
        for b in range(B):
            out.extend([("ln", MLP[m]["ln"], b), ("mlp", m, b)])

    attention("x0")
    if stop == "x0":
        return out
    out.append(("mods2",))
    attention("s1")
    if stop == "s1":
        return out
    attention("x1")
    mlp("m1")
    if stop == "m1":
        return out
    attention("w2")
    if stop == "w2":
        return out
    attention("t2")
    if stop == "t2":
        return out
    mlp("m2")
    if stop == "m2":
        return out
    out.append(("prep3",))
    for b in range(B):
        out.extend([("ln", 7, b), ("moe", b)])
    return out


def steps_of(kind):
    n = TB if kind == "self" else 1
    return [(p, j, k) for p in range(HP) for j in range(2) for k in range(n)]


def first_pass_units(kind):
    return [(j, t) for j in range(2) for t in range(TB)] if kind == "self" else [(0, 0), (0, 1)]


def side_plan(kind):
    units, per = first_pass_units(kind), len(steps_of(kind)) // HP
    ahead = [[] for _ in range(per * HP)]
    start = []
    for p in range(HP):
        tasks = [("p1", p, u) for u in range(len(units))]
        if p < 2:
            start += tasks + ([] if kind == "top" else [("t", p)])
            continue
        for i, t in enumerate(tasks):
            ahead[(p - 2) * per + i * per // len(tasks)].append(t)
        if kind != "top":
            ahead[(p - 1) * per + (1 if per > 2 else 0)].insert(0, ("t", p))
    return start, ahead


def build(nc, ins, out, marks, stop=None):
    final = marks is not None
    marks = marks or {}
    seen, count, ring = {}, {}, [0]
    sched = schedule(stop)
    stages = [s[0] for s in sched]

    with ExitStack() as ctx:
        sems = {}

        def sem(name):
            if name not in sems:
                sems[name] = ctx.enter_context(nc.semaphore(name))
            return sems[name]

        def mark(name, *key, by=1):
            count[name] = count.get(name, 0) + by
            seen[(name, *key)] = count[name]
            return by

        def at(name, *key):
            return marks[(name, *key)] if final else 1

        def sb(name, shape, dt):
            return ctx.enter_context(nc.sbuf_tensor(name, shape, dt))

        x = sb("x", [P, B * TB, C], F32)
        ht = sb("ht", [P, B, CC, L], F32)
        qs = sb("qs", [P, HP, L], F16)
        ks = sb("ks", [P, H, L], F16)
        vs = sb("vs", [P, TB, H, 32], F32)
        xn = sb("xn", [P, TB, C], F32)
        onorm = sb("onorm", [P, L], F32)
        area = sb("area", [P, 8192], F32)
        wa = sb("wa", [P, 2, 2048], F32)
        wm = sb("wm", [P, 6144], F32)
        gates = sb("gates", [P, len(GATES), B, C], F32)
        vbias = sb("vbias", [P, 2, C], F32)
        obias = sb("obias", [P, 3, C], F32)
        gbias = sb("gbias", [P, C], F32)
        ct = sb("ct", [P, 3, CC, B, S], F32)
        identf = sb("identf", [P, P], F32)
        identh = sb("identh", [P, P], F16)
        cols = sb("cols", [P, 128], F32)
        silc = sb("silc", [P, 4], F32)
        modc = sb("modc", [P, len(MODS), B], F32)
        stats = sb("stats", [P, TB, 6], F32)
        mv = sb("mv", [P, TB, 2], F32)
        vare = sb("vare", [P, TB], F32)
        rstd = sb("rstd", [P, TB], F32)
        mhalf = sb("mhalf", [P, TB], F32)
        m16 = sb("m16", [P, 2, TB, 2], F16)
        mt = sb("mt", [2, 2, L], F16)
        rec = sb("rec", [P, 32], F32)
        v8 = sb("v8", [P, 2, 8, 8], F32)

        st = area[:, 0:2048].bitcast(F16).rearrange("p (r s n) -> p r s n", r=2, s=2)
        q32 = area[:, 2048:4096].rearrange("p (r n) -> p r n", r=2)
        pr = area[:, 4096:7168].rearrange("p (r n) -> p r n", r=RP)
        turned = area[:, 7168:8192]
        hid = area[:, :].rearrange("p (r k n) -> p r k n", r=2, k=8)
        cx = area[0:S, 4096:4608].rearrange("p (b c) -> p b c", b=B)
        cxn = area[0:S, 4608:5632].rearrange("p (v b c) -> p v b c", v=2, b=B)
        crow = area[:, 5632:5760]
        condb = area[:, 7168:7680].rearrange("p (b c n) -> p b c n", b=B, c=CC)
        xnf = xn[:].rearrange("p a b -> p (a b)")
        US = 8 * S
        top_s = [xnf[:, i * US:(i + 1) * US] for i in range(2)]
        top_w = xnf[:, 2 * US:3 * US]
        vsf = vs[:].rearrange("p a b c -> p (a b c)")
        top_p = [vsf[:, 1024 + i * US:1024 + (i + 1) * US] for i in range(4)]
        ksf = ks[:].rearrange("p a b -> p (a b)").bitcast(F32)
        qsf = qs[:].rearrange("p a b -> p (a b)").bitcast(F32)
        waf = wa[:].rearrange("p a b -> p (a b)")

        psum = ctx.enter_context(nc.psum_tensor("psum", [P, 4, SLOT], F32))
        sl = [psum[:, k, :] for k in range(4)]

        n_split = sum(2 * (1 + (ATT[s[1]]["kind"] in ("self", "win"))) if s[0] == "proj" else 2
                      for s in sched if s[0] in ("proj", "ckv"))
        scratch = nc.dram_tensor("scratch", [n_split, 2, P, L], F16, kind="Internal").ap()
        split_no = {}
        for s in sched:
            if s[0] == "ckv":
                for m in range(CC):
                    split_no[(s[1], "k", "c", m)] = len(split_no)
            if s[0] == "proj":
                for t in ("q", "k") if ATT[s[1]]["kind"] in ("self", "win") else ("q",):
                    for m in range(CC):
                        split_no[(s[1], t, s[2], m)] = len(split_no)
        ln_calls = [s for s in sched if s[0] == "ln"]
        calls = [(s[1], s[2]) for s in sched if s[0] == "attn"]
        step_no, group_no = {}, {}
        for a, b in calls:
            for i in range(len(steps_of(ATT[a]["kind"]))):
                step_no[(a, b, i)] = len(step_no)
            for g in range(H // GH):
                group_no[(a, b, g)] = len(group_no)

        def open_slot(pe, key, k=None, signals=True):
            if k is None:
                k = ring[0]
                ring[0] = (ring[0] + 1) % 4
            n = seen.get(("opened", k), 0)
            if n:
                pe.wait_ge(sem(f"free{k}"), n)
            seen[("opened", k)] = n + 1
            seen[("filled", k)] = seen.get(("filled", k), 0) + signals
            seen[("slot", key)] = (k, seen[("filled", k)], n + 1)
            return k

        def where(key):
            return marks[("slot", key)] if final else (0, 1, 1)

        def filled(eng, key):
            k, n, _ = where(key)
            eng.wait_ge(sem(f"full{k}"), n)
            return sl[k]

        def emptied(eng, key):
            k, _, n = where(key)
            eng.wait_ge(sem(f"free{k}"), n)

        def free(key):
            return sem(f"free{where(key)[0]}")

        def call_before(a, b):
            i = calls.index((a, b))
            return calls[i - 1] if i else None

        def last_reader(a, b, p):
            kind = ATT[a]["kind"]
            if kind == "top":
                return ("p1", a, b, p, 1)
            per = len(steps_of(kind)) // HP
            return ("s", a, b, (p + 1) * per - 1)

        def wviews(a):
            at_, views = 0, []
            for n in ATT[a]["n"]:
                views.append(wa[:, ATT[a]["half"], at_:at_ + CC * n].rearrange("p (c n) -> p c n", c=CC))
                at_ += CC * n
            return views

        def qkv_views(a):
            v = wviews(a)
            if len(v) == 2:
                return v[0][:, :, 0:256], v[0][:, :, 256:512], v[0][:, :, 512:768], v[1]
            return v[0], v[1][:, :, 0:256], v[1][:, :, 256:512], v[2]

        mod_w = {
            "ssq": wm[:, 0:1024].rearrange("p (c n) -> p c n", c=CC),
            "sskv": wm[:, 1024:2048].rearrange("p (c n) -> p c n", c=CC),
            "mod1": wm[:, 2048:5120].rearrange("p (c n) -> p c n", c=CC),
            "ada2": wm[:, 0:4608].rearrange("p (c n) -> p c n", c=CC),
        }
        mod_in = {"ssq": "L0_xcond_Wss_q", "sskv": "L0_xcond_Wss_kv", "mod1": "L1_xcond_W_mod", "ada2": "L2_xcond_w_ada"}

        def mlp_views(m):
            n = MLP[m]["n"][0]
            up = wm[:, 0:CC * n].rearrange("p (c n) -> p c n", c=CC)
            down = wm[:, CC * n:CC * n + 8 * C].rearrange("p (k n) -> p k n", k=8)
            return up, down

        NX = NE * RH + C
        w3 = {
            "nx": ksf[:, 0:CC * NX].rearrange("p (c n) -> p c n", c=CC),
            "w2": ksf[:, CC * NX:CC * NX + 12 * C].rearrange("p (k n) -> p k n", k=12),
            "g2": ksf[:, CC * NX + 12 * C:CC * NX + 14 * C].rearrange("p (c n) -> p c n", c=CC),
            "ev": qsf[:, 0:CC * NX].rearrange("p (c n) -> p c n", c=CC),
            "an": vsf[:, 0:CC * NX].rearrange("p (c n) -> p c n", c=CC),
        }
        w3["ow"] = wm[:, 5632:6144].rearrange("p (c n) -> p c n", c=CC)
        w3q = qsf[:, CC * NX:CC * NX + 512].rearrange("p (c n) -> p c n", c=CC)
        w3k = vsf[:, CC * NX:CC * NX + 512].rearrange("p (c n) -> p c n", c=CC)
        w3v = onorm[:, 0:512].rearrange("p (c n) -> p c n", c=CC)
        wr = onorm[:, 512:530].rearrange("p (c n) -> p c n", c=6)
        VWN = NX + NE
        vw = waf[0:S, 0:B * VWN].rearrange("p (b n) -> p b n", b=B)
        g3 = wm[:, 0:CC * B * S].rearrange("p (c b s) -> p c b s", c=CC, b=B)
        kt3 = wm[:, 512:512 + CC * B * S].rearrange("p (c b s) -> p c b s", c=CC, b=B)
        vt3 = wm[:, 1024:1024 + CC * B * S].rearrange("p (c b s) -> p c b s", c=CC, b=B)
        wqt = wm[:, 1536:2048].rearrange("p (c n) -> p c n", c=CC)
        hb3 = wm[:, 2048:2048 + B * 14].rearrange("p (b n) -> p b n", b=B)
        rb3 = wm[:, 2080:2080 + B * NE].rearrange("p (b n) -> p b n", b=B)
        rbin = wm[:, 2088:2088 + NE]
        b2e = wm[0:NE, 2304:2560]
        p3 = wm[:, 2560:2560 + TB * S].rearrange("p (t s) -> p t s", t=TB)
        wt3 = wm[0:S, 3200:3200 + L]
        pt3 = wm[0:NE, 4224:4224 + L]
        sm3 = wm[:, 5248:5264]
        rs3 = wm[:, 5264:5272]
        lg3 = wm[:, 5280:5280 + TB * NE].rearrange("p (t e) -> p t e", t=TB)
        lm3 = wm[:, 5312:5320]
        ls3 = wm[:, 5320:5328]
        bm3 = wm[:, 5328:5336]
        hid3 = area[:, 0:12 * 512].rearrange("p (k n) -> p k n", k=12)
        gh3 = area[:, 6144:7168].rearrange("p (k n) -> p k n", k=2)
        rt3 = area[:, 7168:8192].rearrange("p (c n) -> p c n", c=CC)

        def mrow_no(a, b, p):
            n = 0
            for c in calls:
                if c == (a, b):
                    break
                if ATT[c[0]]["kind"] != "top":
                    n += HP
            return n + p

        def gz_of(g):
            return xnf[:, 1024:1536] if g == 0 else xnf[:, 1536:2048]

        block = ctx.enter_context(nc.Block())

        @block.tensor
        def _(pe):
            def accumulate(dst, pairs):
                for i, (lhs, rhs) in enumerate(pairs):
                    mm = pe.matmul(dst, lhs, rhs, start=(i == 0), stop=(i == len(pairs) - 1))
                return mm

            def mods(names, key):
                k = open_slot(pe, (key,))
                for n, (w, i, _) in enumerate(MODS):
                    if w in names:
                        mm = accumulate(sl[k][:, 2 * n:2 * n + 2],
                                        [(mod_w[w][:, c, i * P:(i + 1) * P], silc[:].rearrange("p (b c) -> p c b", c=CC)[:, c, :])
                                         for c in range(CC)])
                mm.then_inc(sem(f"full{k}"), 1)

            def gate_rows(layer, w):
                for g, (ly, i) in enumerate(GATES):
                    if ly != layer:
                        continue
                    k = open_slot(pe, ("gate", g))
                    for b in range(B):
                        mm = accumulate(sl[k][:, b * 256:b * 256 + 256],
                                        [(condb[:, b, c, :], mod_w[w][:, c, i * C:(i + 1) * C]) for c in range(CC)])
                    mm.then_inc(sem(f"full{k}"), 1)

            def prep():
                pe.wait_ge(sem("ident"), at("ident", "f"))
                pe.wait_ge(sem("ld_cols"), at("ld_cols", "all"))
                k = open_slot(pe, ("cols",))
                pe.transpose(sl[k][:, 0:NCOL], crow[0:NCOL, :], identf[0:NCOL, 0:NCOL]).then_inc(sem(f"full{k}"), 1)
                pe.wait_ge(sem("ld_ctx"), 16)
                k = open_slot(pe, ("ctraw",))
                for c in range(CC):
                    for b in range(B):
                        mm = pe.transpose(sl[k][:, (c * B + b) * P:(c * B + b) * P + S], cx[:, b, c * P:(c + 1) * P],
                                          identf[0:S, 0:S])
                mm.then_inc(sem(f"full{k}"), 1)
                for v in range(2):
                    pe.wait_ge(sem("cxn"), at("cxn", v))
                    k = open_slot(pe, ("ctn", v))
                    for c in range(CC):
                        for b in range(B):
                            mm = pe.transpose(sl[k][:, (c * B + b) * P:(c * B + b) * P + S],
                                              cxn[:, v, b, c * P:(c + 1) * P], identf[0:S, 0:S])
                    mm.then_inc(sem(f"full{k}"), 1)
                pe.wait_ge(sem("silc"), at("silc", "cols"))
                pe.wait_ge(sem("ld_ss"), 32)
                pe.wait_ge(sem("ld_mod1"), 16)
                mods(("ssq", "sskv", "mod1"), "mods1")
                pe.wait_ge(sem("silc"), at("silc", "rows"))
                gate_rows(1, "mod1")

            def mods2():
                pe.wait_ge(sem("ld_ada2"), 16)
                mods(("ada2",), "mods2")
                pe.wait_ge(sem("condb2"), 1)
                gate_rows(2, "ada2")

            def ckv(a):
                wq, wk, wv, wo = qkv_views(a)
                pe.wait_ge(sem("ld_" + a), at("ld_" + a, "all"))
                v = {"x0": 0, "x1": 1, "t2": 2}[a]
                pe.wait_ge(sem("ctdone"), at("ctdone", v))
                for m in range(CC):
                    k = open_slot(pe, ("k", a, "c", m))
                    accumulate(sl[k][:, 0:B * S],
                               [(wk[:, c, m * P:(m + 1) * P], ct[:, v, c].rearrange("p b s -> p (b s)")) for c in range(CC)]
                               ).then_inc(sem(f"full{k}"), 1)
                k = open_slot(pe, ("v", a, "c"))
                for b in range(B):
                    mm = accumulate(sl[k][0:S, b * C:(b + 1) * C], [(ct[:, v, c, b, :], wv[:, c, :]) for c in range(CC)])
                mm.then_inc(sem(f"full{k}"), 1)

            def ln(i, b):
                for c in range(CC):
                    k = open_slot(pe, ("ln", i, b, c))
                    for t in range(TB):
                        if c == 0:
                            pe.wait_ge(sem("xn"), at("xn", i, b, t))
                        mm = pe.transpose(sl[k][:, t * P:(t + 1) * P], xn[:, t, c * P:(c + 1) * P], identf[:, :])
                    mm.then_inc(sem(f"full{k}"), 1)

            def proj(a, b):
                wq, wk, wv, wo = qkv_views(a)
                both = ATT[a]["kind"] in ("self", "win")
                pe.wait_ge(sem("ld_" + a), at("ld_" + a, "all"))
                emptied(pe, ("ln", ATT[a]["ln"], b, CC - 1))
                for t, w in (("q", wq), ("k", wk)) if both else (("q", wq),):
                    for m in range(CC):
                        k = open_slot(pe, (t, a, b, m))
                        for n in range(2):
                            mm = accumulate(sl[k][:, n * 512:(n + 1) * 512],
                                            [(w[:, c, m * P:(m + 1) * P], ht[:, b, c, n * 512:(n + 1) * 512]) for c in range(CC)])
                        mm.then_inc(sem(f"full{k}"), 1)
                if both:
                    for g in range(2):
                        k = open_slot(pe, ("v", a, b, g))
                        for t in range(4):
                            lo = (g * 4 + t) * P
                            mm = accumulate(sl[k][:, t * C:(t + 1) * C], [(ht[:, b, c, lo:lo + P], wv[:, c, :]) for c in range(CC)])
                        mm.then_inc(sem(f"full{k}"), 1)

            def attn(a, b):
                kind = ATT[a]["kind"]
                units = first_pass_units(kind)
                nk = S if kind in ("cross", "top") else P

                def first_pass(p, u):
                    m = p // 4
                    if u == 0:
                        pe.wait_ge(sem(f"qin{m}"), at(f"qin{m}", a, b))
                        pe.wait_ge(sem(f"kin{m}"), at(f"kin{m}", a, b if kind in ("self", "win") else "c"))
                        pe.wait_ge(sem("mzero"), at("mzero", a, b))
                    k = open_slot(pe, ("p1", a, b, p, u), 3)
                    if kind == "self":
                        j, t = units[u]
                        for n in range(2):
                            mm = pe.matmul(sl[k][:, n * 512:(n + 1) * 512], qs[:, p, t * P:(t + 1) * P],
                                           ks[:, 2 * p + j, n * 512:(n + 1) * 512], start=True, stop=True)
                    else:
                        for q4 in range(4):
                            t = u * 4 + q4
                            lo = t * P if kind == "win" else b * S
                            mm = pe.matmul(sl[k][:, q4 * 256:q4 * 256 + 2 * nk].rearrange("p (j s) -> p j s", j=2),
                                           qs[:, p, t * P:(t + 1) * P], ks[:, 2 * p:2 * p + 2, lo:lo + nk],
                                           start=True, stop=True)
                    mm.then_inc(sem(f"full{k}"), 1)

                def turn(p):
                    k = open_slot(pe, ("t", a, b, p), 3)
                    dst = sl[k].bitcast(F16)
                    for t in range(TB):
                        mm = pe.transpose(dst[0:2, t * P:(t + 1) * P], m16[:, p % 2, t, :], identh[:, :])
                    mm.then_inc(sem(f"full{k}"), 1)

                def side(tasks):
                    for t in tasks:
                        first_pass(t[1], t[2]) if t[0] == "p1" else turn(t[1])

                def scores(i, p, j, kt):
                    k = open_slot(pe, ("s", a, b, i), step_no[(a, b, i)] % 2)
                    h = 2 * p + j
                    if kind == "top":
                        for t in range(TB):
                            if j == 0 and t % 4 == 0:
                                pe.wait_ge(sem("topp"), at("topp", a, b, p, t // 4))
                            src = top_p[(2 * p + t // 4) % 4].rearrange("p (q j s) -> p q j s", q=4, j=2)
                            mm = pe.transpose(sl[k][0:S, t * P:(t + 1) * P], src[:, t % 4, j, :], identf[:, :])
                    elif kind == "win":
                        pe.wait_ge(sem(f"mrow{p % 2}"), at(f"mrow{p % 2}", a, b, p))
                        for w in range(TB):
                            mm = pe.matmul(sl[k][:, w * P:(w + 1) * P], ks[:, h, w * P:(w + 1) * P],
                                           qs[:, p, w * P:(w + 1) * P], start=True, stop=True)
                    else:
                        if kt == 0:
                            pe.wait_ge(sem(f"mrow{p % 2}"), at(f"mrow{p % 2}", a, b, p))
                        lo = kt * P if kind == "self" else b * S
                        for n in range(2):
                            mm = pe.matmul(sl[k][0:nk, n * 512:(n + 1) * 512], ks[:, h, lo:lo + nk],
                                           qs[:, p, n * 512:(n + 1) * 512], start=True, stop=True)
                    mm.then_inc(sem(f"full{k}"), 1)

                def values(i, p, j, kt):
                    h = 2 * p + j
                    g, r = h // GH, 32 * (h % GH)
                    if r == 0 and kt == 0:
                        open_slot(pe, ("o", a, b, g), 2, signals=False)
                    emptied(pe, ("s", a, b, i))
                    e = pr[:, step_no[(a, b, i)] % RP, :]
                    if i == 0:
                        emptied(pe, ("v", a, b, 1) if kind in ("self", "win") else ("v", a, "c"))
                    if kind == "win":
                        for w in range(TB):
                            mm = pe.matmul(sl[2][r:r + 32, w * P:(w + 1) * P], vs[:, w, h, :], e[:, w * P:(w + 1) * P],
                                           start=True, stop=True, tile_position=(0, r))
                    else:
                        vt = kt if kind == "self" else b
                        for n in range(2):
                            mm = pe.matmul(sl[2][r:r + 32, n * 512:(n + 1) * 512], vs[0:nk, vt, h, :],
                                           e[0:nk, n * 512:(n + 1) * 512], start=(kt == 0),
                                           stop=(kind != "self" or kt == TB - 1), tile_position=(0, r))
                    mm.then_inc(sem("pv"), mark("pv", a, b, i))

                start, ahead = side_plan(kind)
                side(start)
                steps = steps_of(kind)
                for i, (p, j, kt) in enumerate(steps):
                    scores(i, p, j, kt)
                    side(ahead[i])
                    if i:
                        values(i - 1, *steps[i - 1])
                values(len(steps) - 1, *steps[-1])

            def post(a, b):
                wo = qkv_views(a)[3]
                for g in range(2):
                    pe.wait_ge(sem(f"pack{g}"), at(f"pack{g}", a, b, H // GH - 2 + g))
                for g in range(2):
                    k = open_slot(pe, ("post", a, b, g))
                    for t in range(4):
                        lo = (g * 4 + t) * P
                        mm = accumulate(sl[k][:, t * C:(t + 1) * C], [(ht[:, b, c, lo:lo + P], wo[:, c, :]) for c in range(CC)])
                    mm.then_inc(sem(f"full{k}"), 1)

            def mlp(m, b):
                up, down = mlp_views(m)
                pe.wait_ge(sem("ld_" + m), at("ld_" + m, "all"))
                emptied(pe, ("ln", MLP[m]["ln"], b, CC - 1))
                njob = 4 if m == "m1" else 8

                def hidden(r):
                    for j in range(njob):
                        k = open_slot(pe, ("up", m, b, r, j))
                        for n in range(2):
                            ch = 2 * j + n if m == "m1" else j + 8 * n
                            mm = accumulate(sl[k][:, n * 512:(n + 1) * 512],
                                            [(up[:, c, ch * P:(ch + 1) * P], ht[:, b, c, r * 512:(r + 1) * 512]) for c in range(CC)])
                        mm.then_inc(sem(f"full{k}"), 1)

                def lower(r):
                    emptied(pe, ("up", m, b, r, njob - 1))
                    k = open_slot(pe, ("post", m, b, r))
                    for t in range(4):
                        mm = accumulate(sl[k][:, t * C:(t + 1) * C],
                                        [(hid[:, r, c, t * P:(t + 1) * P], down[:, c, :]) for c in range(8)])
                    mm.then_inc(sem(f"full{k}"), 1)

                hidden(0)
                hidden(1)
                lower(0)
                lower(1)

            def prep3():
                pe.wait_ge(sem("ld_l3"), at("ld_l3", "all"))
                k = open_slot(pe, ("wqt",))
                for c in range(CC):
                    for m in range(CC):
                        mm = pe.transpose(sl[k][:, (m * CC + c) * P:(m * CC + c + 1) * P], w3q[:, c, m * P:(m + 1) * P], identf[:, :])
                mm.then_inc(sem(f"full{k}"), 1)
                for name, w in (("kt3", w3k), ("vt3", w3v)):
                    k = open_slot(pe, (name,))
                    for m in range(CC):
                        mm = accumulate(sl[k][:, m * 512:m * 512 + B * S],
                                        [(w[:, c, m * P:(m + 1) * P], ct[:, 2, c].rearrange("p b s -> p (b s)")) for c in range(CC)])
                    mm.then_inc(sem(f"full{k}"), 1)
                emptied(pe, ("wqt",))
                emptied(pe, ("kt3",))
                k = open_slot(pe, ("g3",))
                for m in range(CC):
                    mm = accumulate(sl[k][:, m * 512:m * 512 + B * S],
                                    [(wqt[:, c, m * P:(m + 1) * P], kt3[:, c].rearrange("p b s -> p (b s)")) for c in range(CC)])
                mm.then_inc(sem(f"full{k}"), 1)
                emptied(pe, ("vt3",))
                for b in range(B):
                    for g in range(2):
                        k = open_slot(pe, ("vw", b, g))
                        for n in range(2):
                            lo = g * 1024 + n * 512
                            if lo >= NX:
                                continue
                            hi = min(lo + 512, NX)
                            mm = accumulate(sl[k][0:S, n * 512:n * 512 + hi - lo],
                                            [(vt3[:, c, b, :], w3["ev"][:, c, lo:hi]) for c in range(CC)])
                        if g == 1:
                            mm = accumulate(sl[k][0:S, 768:768 + NE], [(vt3[:, c, b, :], wr[:, 2 + c, :]) for c in range(CC)])
                        mm.then_inc(sem(f"full{k}"), 1)
                k = open_slot(pe, ("anchor",))
                cond = cols[:, 0:4].rearrange("p (b c) -> p c b", c=CC)
                for n in range(14):
                    accumulate(sl[k][:, 2 * n:2 * n + 2], [(w3["an"][:, c, n * P:(n + 1) * P], cond[:, c, :]) for c in range(CC)])
                pe.wait_ge(sem("condb3"), 1)
                for b in range(B):
                    mm = accumulate(sl[k][:, 512 + 4 * b:512 + 4 * b + NE], [(condb[:, b, c, :], wr[:, 4 + c, :]) for c in range(CC)])
                mm.then_inc(sem(f"full{k}"), 1)

            def moe(b):
                emptied(pe, ("ln", 7, b, CC - 1))
                emptied(pe, ("g3",))
                k = open_slot(pe, ("sc3", b))
                for t in range(TB):
                    mm = accumulate(sl[k][:, t * P:t * P + S], [(ht[:, b, c, t * P:(t + 1) * P], g3[:, c, b, :]) for c in range(CC)])
                mm.then_inc(sem(f"full{k}"), 1)
                pe.wait_ge(sem("p3"), at("p3", b))
                k = open_slot(pe, ("wt3", b))
                for t in range(TB):
                    mm = pe.transpose(sl[k][0:S, t * P:(t + 1) * P], p3[:, t, :], identf[:, :])
                mm.then_inc(sem(f"full{k}"), 1)
                emptied(pe, ("wt3", b))
                emptied(pe, ("vw", B - 1, 1))
                emptied(pe, ("vw", B - 1, 0))
                emptied(pe, ("vw", 0, 1))
                emptied(pe, ("vw", 0, 0))
                k = open_slot(pe, ("lg3", b))
                for t in range(TB):
                    lo = t * P
                    mm = accumulate(sl[k][:, 4 * t:4 * t + NE],
                                    [(ht[:, b, c, lo:lo + P], wr[:, c, :]) for c in range(CC)] + [(wt3[:, lo:lo + P], vw[:, b, NX:VWN])])
                mm.then_inc(sem(f"full{k}"), 1)
                for r in range(2):
                    lo = r * 512
                    for j in range(7):
                        k = open_slot(pe, ("h3", b, r, j))
                        for n in range(2):
                            ch = 2 * j + n
                            mm = accumulate(sl[k][:, n * 512:(n + 1) * 512],
                                            [(w3["nx"][:, c, ch * P:(ch + 1) * P], ht[:, b, c, lo:lo + 512]) for c in range(CC)]
                                            + [(vw[:, b, ch * P:(ch + 1) * P], wt3[:, lo:lo + 512])])
                        mm.then_inc(sem(f"full{k}"), 1)
                    if r == 0:
                        pe.wait_ge(sem("rp3"), at("rp3", b))
                        k = open_slot(pe, ("pt3", b))
                        for t in range(TB):
                            mm = pe.transpose(sl[k][0:NE, t * P:(t + 1) * P], lg3[:, t, :], identf[:, :])
                        mm.then_inc(sem(f"full{k}"), 1)
                        emptied(pe, ("pt3", b))
                    emptied(pe, ("h3", b, r, 6))
                    for t in range(4):
                        k = open_slot(pe, ("ex3", b, r, t))
                        for e in range(NE):
                            accumulate(sl[k][:, e * C:(e + 1) * C],
                                       [(hid3[:, 4 * e + c, t * P:(t + 1) * P], w3["w2"][:, 4 * e + c, :]) for c in range(4)])
                        pe.matmul(sl[k][:, 768:1024], pt3[:, lo + t * P:lo + (t + 1) * P], b2e, start=True, stop=True
                                  ).then_inc(sem(f"full{k}"), 1)
                    k = open_slot(pe, ("rt3", b, r))
                    for t in range(4):
                        pe.wait_ge(sem("r3"), at("r3", b, r, t))
                        for c in range(CC):
                            mm = pe.transpose(sl[k][:, c * 512 + t * P:c * 512 + (t + 1) * P], xn[:, t, c * P:(c + 1) * P], identf[:, :])
                    mm.then_inc(sem(f"full{k}"), 1)
                    emptied(pe, ("rt3", b, r))
                    for g in range(2):
                        k = open_slot(pe, ("y3", b, r, g))
                        for t in range(2):
                            q = (2 * g + t) * P
                            accumulate(sl[k][:, t * C:(t + 1) * C], [(rt3[:, c, q:q + P], w3["ow"][:, c, :]) for c in range(CC)])
                            mm = accumulate(sl[k][:, 512 + t * C:512 + (t + 1) * C],
                                            [(gh3[:, c, q:q + P], w3["g2"][:, c, :]) for c in range(CC)])
                        mm.then_inc(sem(f"full{k}"), 1)

            run = {"prep": prep, "mods2": mods2, "ckv": ckv, "ln": ln, "proj": proj, "attn": attn, "post": post, "mlp": mlp,
                   "prep3": prep3, "moe": moe}
            for s in sched:
                run[s[0]](*s[1:])

        @block.scalar
        def _(act):
            def silu_cond():
                act.wait_ge(sem("cols"), at("cols", "copied"))
                act.activation(silc[:], cols[:, 0:4], ACT.Silu).then_inc(sem("silc"), mark("silc", "cols"))

            def prep():
                for q in range(4):
                    act.dma_start(x[:, 4 * q:4 * q + 4, :],
                                  ins["x"].rearrange("b (t p) c -> p (b t) c", p=P)[:, 4 * q:4 * q + 4, :]
                                  ).then_inc(sem(f"ld_x{q}"), mark(f"ld_x{q}", by=16))
                silu_cond()

            def mods2():
                pass

            def split_evac(t, a, b, m, n, biascol):
                j = split_no[(a, t, b, m)]
                if j >= 2:
                    act.wait_ge(sem("split"), at("split", j - 2))
                src = filled(act, (t, a, b, m))
                act.activation(q32[:, j % 2, 0:n], src[:, 0:n], ACT.Identity, bias=cols[:, biascol + m:biascol + m + 1]
                               ).then_inc(free((t, a, b, m)), 1)

            def ckv(a):
                for m in range(CC):
                    split_evac("k", a, "c", m, B * S, ATT[a]["kb"])

            def ln(i, b):
                if i == 0:
                    act.wait_ge(sem("modc"), at("modc", 1))
                if i in LN_MOD:
                    w, s0, b0 = LN_MOD[i]
                    if w == "ada2":
                        act.wait_ge(sem("modc"), at("modc", 2))
                for c in range(CC):
                    if i in LN_MOD:
                        scale = modc[:, MOD_AT[(w, s0 + c)], b:b + 1]
                        bias = modc[:, MOD_AT[(w, b0 + c)], b:b + 1]
                    elif i == 7:
                        g0, e0 = COL["L3_xcond_ln_gamma"], COL["L3_xcond_ln_beta"]
                        scale, bias = cols[:, g0 + c:g0 + c + 1], cols[:, e0 + c:e0 + c + 1]
                    else:
                        scale, bias = 1.0, 0.0
                    src = filled(act, ("ln", i, b, c))
                    if i == 4:
                        act.activation(ht[:, b, c, 0:L - SHIFT], src[:, SHIFT:L], ACT.Identity, bias=bias, scale=scale)
                        act.activation(ht[:, b, c, L - SHIFT:L], src[:, 0:SHIFT], ACT.Identity, bias=bias, scale=scale
                                       ).then_inc(free(("ln", i, b, c)), 1)
                    else:
                        act.activation(ht[:, b, c, :], src, ACT.Identity, bias=bias, scale=scale
                                       ).then_inc(free(("ln", i, b, c)), 1)

            def proj(a, b):
                for t in ("q", "k") if ATT[a]["kind"] in ("self", "win") else ("q",):
                    for m in range(CC):
                        split_evac(t, a, b, m, L, ATT[a]["qb" if t == "q" else "kb"])

            def attn(a, b):
                kind = ATT[a]["kind"]
                nk = S if kind in ("cross", "top") else P
                start, ahead = side_plan(kind)

                def top_side(tasks):
                    for _, p, u in tasks:
                        n = 2 * p + u
                        if n >= 2:
                            act.wait_ge(sem("topp"), at("topp", a, b, (n - 2) // 2, (n - 2) % 2))
                        elif (a, b) != calls[0] and b > 0:
                            act.wait_ge(sem("topp"), at("topp", a, b - 1, HP - 1, n))
                        src = filled(act, ("p1", a, b, p, u))
                        act.activation(top_s[n % 2].rearrange("p (q s) -> p q s", q=4),
                                       src.rearrange("p (q s) -> p q s", q=4)[:, :, 0:2 * S], ACT.Identity
                                       ).then_inc(free(("p1", a, b, p, u)), 1)
                        act.wait_ge(sem("topd"), at("topd", a, b, p, u))
                        act.activation(top_p[n % 4], top_p[n % 4], ACT.Exp, scale=SCALE).then_inc(sem("tope"), mark("tope", a, b, p, u))

                if kind == "top":
                    filled(act, ("ln", ATT[a]["ln"], b, CC - 1))
                    top_side(start)
                for i in range(len(steps_of(kind))):
                    n = step_no[(a, b, i)]
                    if n >= RP:
                        act.wait_ge(sem("pv"), n - RP + 1)
                    src = filled(act, ("s", a, b, i))
                    if kind == "top":
                        act.activation(pr[0:nk, n % RP, :], src[0:nk, :], ACT.Identity).then_inc(free(("s", a, b, i)), 1)
                        top_side(ahead[i])
                    else:
                        act.activation(pr[0:nk, n % RP, :], src[0:nk, :], ACT.Exp, scale=SCALE).then_inc(free(("s", a, b, i)), 1)

            def mlp(m, b):
                hb = MLP[m]["hb"]
                for r in range(2):
                    if b:
                        filled(act, ("post", m, b - 1, r))
                    for j in range(4 if m == "m1" else 8):
                        src = filled(act, ("up", m, b, r, j))
                        if m == "m1":
                            for n in range(2):
                                ch = 2 * j + n
                                ins_ = act.activation(hid[:, r, ch, :], src[:, n * 512:(n + 1) * 512], ACT.Gelu_apprx_tanh,
                                                      bias=cols[:, hb + ch:hb + ch + 1])
                            ins_.then_inc(free(("up", m, b, r, j)), 1)
                        else:
                            act.activation(hid[:, r, j, :], src[:, 0:512], ACT.Silu, bias=cols[:, hb + j:hb + j + 1]
                                           ).then_inc(sem("silu"), mark("silu", m, b, r, j))

            def prep3():
                pass

            def moe(b):
                src = filled(act, ("sc3", b))
                act.wait_ge(sem("bm3"), at("bm3", b))
                for t in range(TB):
                    mm = act.activation(p3[:, t, :], src[:, t * P:t * P + S], ACT.Exp, bias=bm3[:, t:t + 1], scale=1.0 / 16,
                                        accum_out=sm3[:, 8 + t:9 + t])
                mm.then_inc(free(("sc3", b)), 1)
                src = filled(act, ("wt3", b))
                act.activation(wt3, src[0:S, :], ACT.Identity).then_inc(free(("wt3", b)), 1)
                act.wait_ge(sem("lgs"), at("lgs", b))
                act.activation(lg3, lg3, ACT.Exp).then_inc(sem("lge"), mark("lge", b))
                for r in range(2):
                    for j in range(7):
                        src = filled(act, ("h3", b, r, j))
                        if j == 0 and (b or r):
                            filled(act, ("y3", (2 * b + r - 1) // 2, (2 * b + r - 1) % 2, 1))
                        if j == 0:
                            act.wait_ge(sem("hb3"), 1)
                        for n in range(2):
                            ch = 2 * j + n
                            dst = hid3[:, ch, :] if ch < 12 else gh3[:, ch - 12, :]
                            mm = act.activation(dst, src[:, n * 512:(n + 1) * 512], ACT.Silu, bias=hb3[:, b, ch:ch + 1])
                        mm.then_inc(free(("h3", b, r, j)), 1)
                    if r == 0:
                        src = filled(act, ("pt3", b))
                        act.activation(pt3, src[0:NE, :], ACT.Identity).then_inc(free(("pt3", b)), 1)
                    src = filled(act, ("rt3", b, r))
                    act.activation(rt3, src.rearrange("p (c n) -> p c n", c=CC), ACT.Identity).then_inc(free(("rt3", b, r)), 1)
                    for g in range(2):
                        act.wait_ge(sem("gz"), at("gz", b, r, g))
                        act.activation(gz_of(g), gz_of(g), ACT.Tanh, scale=0.5).then_inc(sem("tanh"), mark("tanh", b, r, g))

            run = {"prep": prep, "mods2": mods2, "ckv": ckv, "ln": ln, "proj": proj, "attn": attn,
                   "post": lambda a, b: None, "mlp": mlp, "prep3": prep3, "moe": moe}
            for s in sched:
                run[s[0]](*s[1:])

        @block.vector
        def _(dve):
            chain = [0]

            def linked(instr):
                chain[0] += 1
                instr.then_inc(sem("dve_chain"), 1)
                dve.wait_ge(sem("dve_chain"), chain[0])

            def prep():
                dve.memset(mhalf[:], -0.5).then_inc(sem("mhalf"), 1)
                dve.memset(qs[:].rearrange("p a b -> p (a b)").bitcast(U32), 0).then_inc(sem("qzero"), 1)
                dve.wait_ge(sem("ld_ctx"), 16)
                for b in range(B):
                    i = dve.bn_stats(stats[0:S, b, :], cx[:, b, :])
                linked(i)
                for b in range(B):
                    i = dve.bn_aggr(mv[0:S, b, :], stats[0:S, b, :])
                i.then_inc(sem("mv"), mark("mv", "ctx"))
                src = filled(dve, ("cols",))
                linked(dve.tensor_copy(cols[:, 0:NCOL], src[:, 0:NCOL]))
                dve.tensor_copy(cols[:, 127:128], src[:, 0:1]).then_inc(free(("cols",)), 1)
                dve.memset(rec[:, 0:1], 0.0).then_inc(sem("cols"), mark("cols", "copied"))
                src = filled(dve, ("ctraw",))
                dve.tensor_copy(ct[:, 2].rearrange("p c b s -> p (c b) s"),
                                src[:, 0:512].rearrange("p (g s) -> p g s", g=4)[:, :, 0:S]).then_inc(free(("ctraw",)), 1)
                dve.wait_ge(sem("rstd"), at("rstd", "ctx"))
                for v in range(2):
                    for b in range(B):
                        i = dve.tensor_scalar(cxn[:, v, b, :], cx[:, b, :], mv[0:S, b, 0:1], rstd[0:S, 4 * v + b:4 * v + b + 1],
                                              ALU.subtract, ALU.mult)
                    i.then_inc(sem("cxn"), mark("cxn", v))
                dve.wait_ge(sem("silc"), at("silc", "cols"))
                for b in range(B):
                    for c in range(CC):
                        i = dve.tensor_copy(condb[:, b, c, :], silc[:, b * CC + c:b * CC + c + 1].to_broadcast([P, P]))
                i.then_inc(sem("silc"), mark("silc", "rows"))
                src = filled(dve, ("ctn", 1))
                dve.tensor_copy(ct[:, 1].rearrange("p c b s -> p (c b) s"),
                                src[:, 0:512].rearrange("p (g s) -> p g s", g=4)[:, :, 0:S]).then_inc(free(("ctn", 1)), 1)
                mod_columns(1, ("ssq", "sskv", "mod1"), "mods1")
                src = filled(dve, ("ctn", 0))
                for c in range(CC):
                    for b in range(B):
                        i = dve.tensor_scalar(ct[:, 0, c, b, :], src[:, (c * B + b) * P:(c * B + b) * P + S],
                                              modc[:, MOD_AT[("sskv", c)], b:b + 1], modc[:, MOD_AT[("sskv", 2 + c)], b:b + 1],
                                              ALU.mult, ALU.add)
                i.then_inc(free(("ctn", 0)), 1)
                for v in (2, 1, 0):
                    dve.memset(rec[:, v:v + 1], 0.0).then_inc(sem("ctdone"), mark("ctdone", v))
                gate_rows(1)

            def mod_columns(n, names, key):
                lo = min(i for i, mm in enumerate(MODS) if mm[0] in names)
                src = filled(dve, (key,))
                for w in names:
                    blocks = [(i, bl) for i, (ww, bl, _) in enumerate(MODS) if ww == w]
                    run0 = 0
                    for r in range(len(blocks)):
                        if r + 1 == len(blocks) or blocks[r + 1][1] != blocks[r][1] + 1:
                            i0, b0 = blocks[run0]
                            nb = r - run0 + 1
                            c0 = MOD_COL[w] + b0
                            ins_ = dve.tensor_tensor(modc[:, i0:i0 + nb, :], src[:, 2 * i0:2 * (i0 + nb)].rearrange("p (n b) -> p n b", b=B),
                                                     cols[:, c0:c0 + nb].unsqueeze(2).to_broadcast([P, nb, B]), ALU.add)
                            run0 = r + 1
                linked(ins_)
                for i, (w, bl, plus) in enumerate(MODS):
                    if w in names and plus and not (i and MODS[i - 1][0] == w and MODS[i - 1][2] and MODS[i - 1][1] == bl - 1):
                        linked(dve.tensor_scalar_add(modc[:, i:i + 2, :], modc[:, i:i + 2, :], 1.0))
                dve.tensor_copy(rec[:, 4:5], src[:, 2 * lo:2 * lo + 1]).then_inc(free((key,)), 1)
                dve.memset(rec[:, 5:6], 0.0).then_inc(sem("modc"), mark("modc", n))

            def gate_rows(layer):
                for g, (ly, _) in enumerate(GATES):
                    if ly == layer:
                        dve.wait_ge(sem(f"ld_g{layer}"), at(f"ld_g{layer}", "all"))
                        src = filled(dve, ("gate", g))
                        dve.tensor_tensor(gates[:, g], src[:, 0:512].rearrange("p (b c) -> p b c", b=B), gates[:, g], ALU.add
                                          ).then_inc(free(("gate", g)), 1)

            def mods2():
                mod_columns(2, ("ada2",), "mods2")
                dve.wait_ge(sem("ld_g2"), 96)
                i = None
                for b in range(B):
                    for c in range(CC):
                        i = dve.tensor_copy(condb[:, b, c, :], silc[:, b * CC + c:b * CC + c + 1].to_broadcast([P, P]))
                i.then_inc(sem("condb2"), 1)
                gate_rows(2)

            def split(t, a, b, m, n):
                j = split_no[(a, t, b, m)]
                emptied(dve, (t, a, b, m))
                if j >= 2:
                    dve.wait_ge(sem(f"stout{j % 2}"), at(f"stout{j % 2}", j - 2))
                linked(dve.tensor_copy(st[:, j % 2, 0, 0:n], q32[:, j % 2, 0:n]))
                dve.tensor_tensor(st[:, j % 2, 1, 0:n], q32[:, j % 2, 0:n], st[:, j % 2, 0, 0:n], ALU.subtract
                                  ).then_inc(sem("split"), mark("split", j))

            def ckv(a):
                for m in range(CC):
                    split("k", a, "c", m, B * S)
                src = filled(dve, ("v", a, "c"))
                dve.wait_ge(sem("ld_" + a), at("ld_" + a, "all"))
                if a == "x0":
                    dve.wait_ge(sem("vones"), 1)
                dve.tensor_tensor(vs[0:S, 0:B, :, 0:D], src[0:S, 0:B * C].rearrange("p (b h d) -> p b h d", b=B, h=H),
                                  vbias[0:S, ATT[a]["half"], :].rearrange("p (h d) -> p h d", h=H).unsqueeze(1).to_broadcast([S, B, H, D]),
                                  ALU.add).then_inc(free(("v", a, "c")), 1)

            def ln(i, b):
                if i == 0:
                    dve.wait_ge(sem(f"ld_x{2 * b}"), 16)
                    dve.wait_ge(sem(f"ld_x{2 * b + 1}"), 16)
                else:
                    dve.wait_ge(sem("xu"), at("xu", prev_update(i, b), b, 1))
                prev = ln_calls.index(("ln", i, b)) - 1
                for t in range(TB):
                    ins_ = dve.bn_stats(stats[:, t, :], x[:, b * TB + t, :])
                linked(ins_)
                for t in range(TB):
                    ins_ = dve.bn_aggr(mv[:, t, :], stats[:, t, :])
                ins_.then_inc(sem("mv"), mark("mv", i, b))
                if prev >= 0:
                    filled(dve, (*ln_calls[prev], CC - 1))
                dve.wait_ge(sem("rstd"), at("rstd", i, b))
                for t in range(TB):
                    dve.tensor_scalar(xn[:, t, :], x[:, b * TB + t, :], mv[:, t, 0:1], rstd[:, t:t + 1],
                                      ALU.subtract, ALU.mult).then_inc(sem("xn"), mark("xn", i, b, t))

            def prev_update(i, b):
                order = ["x0", "s1", "x1", "m1", "w2", "t2", "m2"]
                return order[i - 1]

            def proj(a, b):
                both = ATT[a]["kind"] in ("self", "win")
                for t in ("q", "k") if both else ("q",):
                    for m in range(CC):
                        split(t, a, b, m, L)
                if both:
                    dve.wait_ge(sem("ld_" + a), at("ld_" + a, "all"))
                    for g in range(2):
                        src = filled(dve, ("v", a, b, g))
                        dve.tensor_tensor(vs[:, 4 * g:4 * g + 4, :, 0:D], src.rearrange("p (t h d) -> p t h d", t=4, h=H),
                                          vbias[:, ATT[a]["half"], :].rearrange("p (h d) -> p h d", h=H).unsqueeze(1).to_broadcast([P, 4, H, D]),
                                          ALU.add).then_inc(free(("v", a, b, g)), 1)

            def attn(a, b):
                kind = ATT[a]["kind"]
                units = first_pass_units(kind)
                nk = S if kind in ("cross", "top") else P
                start, ahead = side_plan(kind)

                def maxima(p, u):
                    src = filled(dve, ("p1", a, b, p, u))
                    if u == 0 and p >= 2:
                        filled(dve, ("t", a, b, p - 2))
                    if u == 0 and p < 2 and call_before(a, b):
                        filled(dve, ("t", *call_before(a, b), HP - 2 + p))
                    if kind == "self":
                        j, t = units[u]
                        dst, v = m16[:, p % 2, t, j:j + 1], src
                    else:
                        dst = m16[:, p % 2, 4 * u:4 * u + 4, :]
                        v = src.rearrange("p (q n) -> p q n", q=4)[:, :, 0:2 * nk].rearrange("p q (j s) -> p q j s", j=2)
                    dve.tensor_reduce(dst, v, AX.X, ALU.max, negate=True).then_inc(free(("p1", a, b, p, u)), 1)

                def turned_out(p):
                    n = mrow_no(a, b, p)
                    if n >= 2:
                        dve.wait_ge(sem(f"mrow{p % 2}"), 32 * (n // 2))
                    src = filled(dve, ("t", a, b, p))
                    dve.tensor_copy(mt[:, p % 2, :], src.bitcast(F16)[0:2, 0:L]).then_inc(free(("t", a, b, p)), 1)

                def keep_top(p, u):
                    n = 2 * p + u
                    sc, w, pp = top_s[n % 2], top_w, top_p[n % 4]
                    emptied(dve, ("p1", a, b, p, u))
                    rows = [slice(r * S, (r + 1) * S) for r in range(8)]
                    for r in range(8):
                        i = dve.max(v8[:, 0, r, :], sc[:, rows[r]])
                    chain[0] += 1
                    i.then_inc(sem("dve_chain"), 1)
                    dve.wait_ge(sem("dve_chain"), chain[0])
                    dve.memset(rec[:, 0:1], 0.0).then_inc(sem("topm"), mark("topm", a, b, p, u))
                    for r in range(8):
                        i = dve.match_replace(w[:, rows[r]], v8[:, 0, r, :], sc[:, rows[r]], TOPK_GONE)
                    linked(i)
                    for r in range(8):
                        i = dve.max(v8[:, 1, r, :], w[:, rows[r]])
                    linked(i)
                    for r in range(8):
                        i = dve.match_replace(w[:, rows[r]], v8[:, 1, r, :], w[:, rows[r]], TOPK_GONE)
                    linked(i)
                    dve.wait_ge(sem("tope"), at("tope", a, b, p, u))
                    dve.scalar_tensor_tensor(out=pp, in0=w, scalar=TOPK_GONE / 2, in1=pp, op0=ALU.is_le, op1=ALU.mult
                                             ).then_inc(sem("topp"), mark("topp", a, b, p, u))

                def side(tasks):
                    for t in tasks:
                        if kind == "top":
                            keep_top(t[1], t[2])
                        else:
                            maxima(t[1], t[2]) if t[0] == "p1" else turned_out(t[1])

                def normalize(g, last):
                    gn = group_no[(a, b, g)]
                    dve.wait_ge(sem("pv"), at("pv", a, b, last))
                    if gn:
                        dve.wait_ge(sem("on"), gn)
                    dve.transpose(turned, sl[2]).then_inc(sem("free2"), 1)
                    emptied(dve, ("o", a, b, g))
                    tv = turned.rearrange("p (q d) -> p q d", d=32)
                    linked(dve.reciprocal(rec[:], tv[:, :, D]))
                    linked(dve.tensor_tensor(tv[:, :, 0:D], tv[:, :, 0:D], rec[:].unsqueeze(2).to_broadcast([P, 32, D]), ALU.mult))
                    if gn:
                        pb = group_key(gn - 1)
                        dve.wait_ge(sem(f"pack{pb[2] % 2}"), at(f"pack{pb[2] % 2}", *pb))
                    if kind == "win":
                        dve.transpose(onorm[:, SHIFT:L], turned[:, 0:L - SHIFT])
                        dve.transpose(onorm[:, 0:SHIFT], turned[:, L - SHIFT:L]).then_inc(sem("on"), mark("on", a, b, g))
                    else:
                        dve.transpose(onorm[:], turned).then_inc(sem("on"), mark("on", a, b, g))

                side(start)
                steps = steps_of(kind)
                for i, (p, j, kt) in enumerate(steps):
                    side(ahead[i])
                    if i and (steps[i - 1][0] % 2 == 1) and steps[i - 1][0] != p:
                        normalize(p // 2 - 1, i - 1)
                normalize(H // GH - 1, len(steps) - 1)

            def group_key(n):
                return next(k for k, v in group_no.items() if v == n)

            def update(s, b, r, gate):
                src = filled(dve, ("post", s, b, r)).rearrange("p (t c) -> p t c", t=4)
                dve.wait_ge(sem("xb"), at("xb", s, b))
                xs = x[:, b * TB + 4 * r:b * TB + 4 * r + 4, :]
                if gate is None:
                    dve.tensor_tensor(xs, src, xs, ALU.add).then_inc(free(("post", s, b, r)), 1)
                    emptied(dve, ("post", s, b, r))
                    dve.memset(rec[:, 0:1], 0.0).then_inc(sem("xu"), mark("xu", s, b, r))
                else:
                    g = gates[:, gate, b, :].unsqueeze(1).to_broadcast([P, 4, C])
                    tmp = xn[:, 4 * r:4 * r + 4, :]
                    dve.tensor_tensor(tmp, src, g, ALU.mult).then_inc(free(("post", s, b, r)), 1)
                    emptied(dve, ("post", s, b, r))
                    dve.tensor_tensor(xs, tmp, xs, ALU.add).then_inc(sem("xu"), mark("xu", s, b, r))

            def post(a, b):
                for g in range(2):
                    update(a, b, g, ATT[a]["gate"])

            def mlp(m, b):
                hb = MLP[m]["hb"]
                for r in range(2):
                    if m == "m2":
                        for j in range(8):
                            dve.wait_ge(sem("silu"), at("silu", m, b, r, j))
                            src = filled(dve, ("up", m, b, r, j))
                            dve.scalar_tensor_tensor(out=hid[:, r, j, :], in0=src[:, 512:1024], scalar=cols[:, hb + 8 + j:hb + 9 + j],
                                                     in1=hid[:, r, j, :], op0=ALU.add, op1=ALU.mult).then_inc(free(("up", m, b, r, j)), 1)
                for r in range(2):
                    update(m, b, r, MLP[m]["gate"])

            def prep3():
                filled(dve, ("post", "m2", B - 1, 1))
                src = filled(dve, ("wqt",))
                dve.tensor_copy(wqt, src[:, 0:512].rearrange("p (c n) -> p c n", c=CC)).then_inc(free(("wqt",)), 1)
                for name, dst in (("kt3", kt3), ("vt3", vt3)):
                    src = filled(dve, (name,))
                    dve.tensor_copy(dst.rearrange("p c b s -> p c (b s)"), src.rearrange("p (c n) -> p c n", c=CC)[:, :, 0:B * S]
                                    ).then_inc(free((name,)), 1)
                src = filled(dve, ("g3",))
                dve.tensor_copy(g3.rearrange("p c b s -> p c (b s)"), src.rearrange("p (c n) -> p c n", c=CC)[:, :, 0:B * S]
                                ).then_inc(free(("g3",)), 1)
                for b in range(B):
                    for c in range(CC):
                        i = dve.tensor_copy(condb[:, b, c, :], cols[:, b * CC + c:b * CC + c + 1].to_broadcast([P, P]))
                i.then_inc(sem("condb3"), 1)
                for b in range(B):
                    for g in range(2):
                        src = filled(dve, ("vw", b, g))
                        n = 1024 if g == 0 else VWN - 1024
                        dve.tensor_copy(vw[:, b, g * 1024:g * 1024 + n], src[0:S, 0:n]).then_inc(free(("vw", b, g)), 1)
                src = filled(dve, ("anchor",))
                c0 = COL["L3_xcond_e_b1"]
                dve.tensor_tensor(hb3.rearrange("p b n -> p n b"), src[:, 0:28].rearrange("p (n b) -> p n b", b=B),
                                  cols[:, c0:c0 + 14].unsqueeze(2).to_broadcast([P, 14, B]), ALU.add).then_inc(sem("hb3"), 1)
                dve.tensor_tensor(rb3, src[:, 512:520].rearrange("p (b n) -> p b n", b=B)[:, :, 0:NE],
                                  rbin.unsqueeze(1).to_broadcast([P, B, NE]), ALU.add).then_inc(free(("anchor",)), 1)

            def moe(b):
                src = filled(dve, ("sc3", b))
                linked(dve.tensor_reduce(sm3[:, 0:8], src.rearrange("p (t n) -> p t n", t=TB)[:, :, 0:S], AX.X, ALU.max, negate=True))
                dve.tensor_scalar(bm3, sm3[:, 0:8], 1.0 / 16, None, ALU.mult).then_inc(sem("bm3"), mark("bm3", b))
                emptied(dve, ("sc3", b))
                linked(dve.reciprocal(rs3, sm3[:, 8:16]))
                dve.tensor_tensor(p3, p3, rs3.unsqueeze(2).to_broadcast([P, TB, S]), ALU.mult).then_inc(sem("p3"), mark("p3", b))
                src = filled(dve, ("lg3", b))
                emptied(dve, ("anchor",))
                dve.tensor_tensor(lg3, src[:, 0:32].rearrange("p (t e) -> p t e", t=TB)[:, :, 0:NE],
                                  rb3[:, b, :].unsqueeze(1).to_broadcast([P, TB, NE]), ALU.add).then_inc(free(("lg3", b)), 1)
                emptied(dve, ("lg3", b))
                linked(dve.tensor_reduce(lm3, lg3, AX.X, ALU.max))
                dve.tensor_tensor(lg3, lg3, lm3.unsqueeze(2).to_broadcast([P, TB, NE]), ALU.subtract).then_inc(sem("lgs"), mark("lgs", b))
                dve.wait_ge(sem("lge"), at("lge", b))
                linked(dve.tensor_reduce(ls3, lg3, AX.X, ALU.add))
                linked(dve.reciprocal(ls3, ls3))
                dve.tensor_tensor(lg3, lg3, ls3.unsqueeze(2).to_broadcast([P, TB, NE]), ALU.mult).then_inc(sem("rp3"), mark("rp3", b))
                dve.wait_ge(sem("rp3"), at("rp3", b))
                for r in range(2):
                    for t in range(4):
                        src = filled(dve, ("ex3", b, r, t))
                        acc = xn[:, t, :]
                        linked(dve.tensor_copy(acc, src[:, 768:1024]))
                        for e in range(NE):
                            i = dve.scalar_tensor_tensor(out=acc, in0=src[:, e * C:(e + 1) * C], scalar=lg3[:, 4 * r + t, e:e + 1], in1=acc,
                                                         op0=ALU.mult, op1=ALU.add)
                            if e < NE - 1:
                                linked(i)
                        i.then_inc(free(("ex3", b, r, t)), 1)
                        emptied(dve, ("ex3", b, r, t))
                        dve.memset(rec[:, 0:1], 0.0).then_inc(sem("r3"), mark("r3", b, r, t))
                    dve.wait_ge(sem("ld_b3"), at("ld_b3", "all"))
                    for g in range(2):
                        src = filled(dve, ("y3", b, r, g))
                        linked(dve.tensor_tensor(gz_of(g).rearrange("p (t c) -> p t c", t=2), src[:, 512:1024].rearrange("p (t c) -> p t c", t=2),
                                                 obias[:, 0, :].unsqueeze(1).to_broadcast([P, 2, C]), ALU.add))
                        dve.memset(rec[:, 0:1], 0.0).then_inc(sem("gz"), mark("gz", b, r, g))
                        y = xnf[:, g * 512:(g + 1) * 512]
                        dve.tensor_tensor(y.rearrange("p (t c) -> p t c", t=2), src[:, 0:512].rearrange("p (t c) -> p t c", t=2),
                                          obias[:, 1, :].unsqueeze(1).to_broadcast([P, 2, C]), ALU.add).then_inc(free(("y3", b, r, g)), 1)
                        emptied(dve, ("y3", b, r, g))
                        dve.wait_ge(sem("tanh"), at("tanh", b, r, g))
                        linked(dve.scalar_tensor_tensor(out=y, in0=gz_of(g), scalar=1.0, in1=y, op0=ALU.add, op1=ALU.mult))
                        xs = x[:, b * TB + 4 * r + 2 * g:b * TB + 4 * r + 2 * g + 2, :].rearrange("p t c -> p (t c)")
                        dve.scalar_tensor_tensor(out=xs, in0=y, scalar=0.5, in1=xs, op0=ALU.mult, op1=ALU.add
                                                 ).then_inc(sem("xu"), mark("xu", "moe", b, 2 * r + g))

            run = {"prep": prep, "mods2": mods2, "ckv": ckv, "ln": ln, "proj": proj, "attn": attn, "post": post, "mlp": mlp,
                   "prep3": prep3, "moe": moe}
            for s in sched:
                run[s[0]](*s[1:])

        @block.gpsimd
        def _(pool):
            def prep():
                pool.memset(identf[:], 0.0).then_inc(sem("ident"), mark("ident", "z"))
                pool.wait_ge(sem("ident"), at("ident", "z"))
                pool.affine_select(out=identf[:], in_=identf[:], compare_op=ALU.not_equal, fill=1.0, base=0,
                                   pattern=[[-1, P]], channel_multiplier=1).then_inc(sem("ident"), mark("ident", "f"))
                pool.wait_ge(sem("ident"), at("ident", "f"))
                pool.tensor_copy(identh[:], identf[:]).then_inc(sem("ident"), mark("ident", "h"))
                pool.wait_ge(sem("ident"), at("ident", "h"))
                pool.wait_ge(sem("mv"), at("mv", "ctx"))
                pool.wait_ge(sem("mhalf"), 1)
                for v, eps in ((0, 1e-5), (1, 1e-6)):
                    pool.tensor_scalar(vare[0:S, 4 * v:4 * v + 2], mv[0:S, 0:2, 1], eps, None, ALU.add).then_inc(sem("vare"), mark("vare", "ctx", v))
                    pool.wait_ge(sem("vare"), at("vare", "ctx", v))
                    i = pool.tensor_tensor(rstd[0:S, 4 * v:4 * v + 2], vare[0:S, 4 * v:4 * v + 2], mhalf[0:S, 0:2], ALU.pow)
                i.then_inc(sem("rstd"), mark("rstd", "ctx"))
                pool.wait_ge(sem("rstd"), at("rstd", "ctx"))
                pool.memset(ks[:].rearrange("p a b -> p (a b)").bitcast(U32), 0).then_inc(sem("kzero"), mark("kzero", 0))
                pool.wait_ge(sem("kzero"), at("kzero", 0))
                pool.memset(vsf, 1.0).then_inc(sem("vones"), 1)
                pool.wait_ge(sem("vones"), 1)
                pool.wait_ge(sem("kzero"), at("kzero", 0))
                kv = ks[:].rearrange("p (a two) n -> p a two n", two=2)
                pool.memset(kv[ROWM:ROWM + 1, :, 0, :], 1.0)
                pool.memset(kv[64 + ROWM:64 + ROWM + 1, :, 1, :], 1.0).then_inc(sem("kzero"), mark("kzero", 1))
                pool.wait_ge(sem("kzero"), at("kzero", 1))

            def ln(i, b):
                pool.wait_ge(sem("mv"), at("mv", i, b))
                pool.tensor_scalar(vare[:], mv[:, :, 1], LN_EPS[i], None, ALU.add).then_inc(sem("vare"), mark("vare", i, b))
                pool.wait_ge(sem("vare"), at("vare", i, b))
                pool.tensor_tensor(rstd[:], vare[:], mhalf[:], ALU.pow).then_inc(sem("rstd"), mark("rstd", i, b))
                pool.wait_ge(sem("rstd"), at("rstd", i, b))
                if i == 7:
                    return
                s = ["x0", "s1", "x1", "m1", "w2", "t2", "m2"][i]
                d = ATT.get(s) or MLP[s]
                row = obias[:, d.get("half", 2), :]
                pool.wait_ge(sem("ld_" + s), at("ld_" + s, "all"))
                if d["gate"] is not None:
                    emptied(pool, ("gate", d["gate"]))
                    pool.tensor_tensor(gbias[:], row, gates[:, d["gate"], b, :], ALU.mult).then_inc(sem("gbias"), mark("gbias", s, b))
                    pool.wait_ge(sem("gbias"), at("gbias", s, b))
                    row = gbias[:]
                pool.wait_ge(sem("xn"), at("xn", i, b, TB - 1))
                xs = x[:, b * TB:(b + 1) * TB, :]
                pool.tensor_tensor(xs, xs, row.unsqueeze(1).to_broadcast([P, TB, C]), ALU.add).then_inc(sem("xb"), mark("xb", s, b))
                pool.wait_ge(sem("xb"), at("xb", s, b))

            def proj(a, b):
                prev = call_before(a, b)
                if prev:
                    filled(pool, last_reader(*prev, HP - 1))
                else:
                    pool.wait_ge(sem("qzero"), 1)
                v = qs[:].rearrange("p a b -> p (a b)").bitcast(U32)
                pool.memset(v[ROWM:ROWM + 1, :], 0)
                pool.memset(v[64 + ROWM:64 + ROWM + 1, :], 0).then_inc(sem("mzero"), mark("mzero", a, b))
                pool.wait_ge(sem("mzero"), at("mzero", a, b))

            def attn_top(a, b):
                start, ahead = side_plan("top")
                for tasks in [start] + ahead:
                    for _, p, u in tasks:
                        n = 2 * p + u
                        emptied(pool, ("p1", a, b, p, u))
                        pool.wait_ge(sem("topm"), at("topm", a, b, p, u))
                        if n >= 4:
                            filled(pool, ("s", a, b, 2 * ((n - 4) // 2) + 1))
                        elif b:
                            filled(pool, ("s", a, b - 1, 2 * ((n + 12) // 2) + 1))
                        else:
                            filled(pool, last_reader(*call_before(a, b), HP - 1))
                            pool.wait_ge(sem("pv"), at("pv", *call_before(a, b), len(steps_of("win")) - 1))
                        pool.tensor_tensor(top_p[n % 4].rearrange("p (r s) -> p r s", r=8), top_s[n % 2].rearrange("p (r s) -> p r s", r=8),
                                           v8[:, 0, :, 0:1].to_broadcast([P, 8, S]), ALU.subtract).then_inc(sem("topd"), mark("topd", a, b, p, u))
                        pool.wait_ge(sem("topd"), at("topd", a, b, p, u))

            for s in sched:
                if s[0] == "prep":
                    prep()
                elif s[0] == "ln":
                    ln(*s[1:])
                elif s[0] == "proj":
                    proj(*s[1:])
                elif s[0] == "attn" and ATT[s[1]]["kind"] == "top":
                    attn_top(*s[1:])

        @block.sync
        def _(sp):
            def rows(ap, n):
                return ap.rearrange("(c p) n -> p c n", p=P)

            def bc(ap):
                return ap.rearrange("(o n) -> o n", o=1).to_broadcast([P, ap.shape[0]])

            def load_att(a):
                d = ATT[a]
                for v, w in zip(wviews(a), d["w"]):
                    sp.dma_start(v, rows(ins[w], 0)).then_inc(sem("ld_" + a), mark("ld_" + a, "w", by=16))
                name, lo = d["vb"]
                sp.dma_start(vbias[:, d["half"], :], bc(ins[name][lo:lo + C])).then_inc(sem("ld_" + a), mark("ld_" + a, "w", by=16))
                sp.dma_start(obias[:, d["half"], :], bc(ins[d["ob"]])).then_inc(sem("ld_" + a), mark("ld_" + a, "all", by=16))

            def load_mlp(m):
                up, down = mlp_views(m)
                d = MLP[m]
                sp.dma_start(up, rows(ins[d["w"][0]], 0)).then_inc(sem("ld_" + m), mark("ld_" + m, "w", by=16))
                sp.dma_start(down, rows(ins[d["w"][1]], 0)).then_inc(sem("ld_" + m), mark("ld_" + m, "w", by=16))
                sp.dma_start(obias[:, 2, :], bc(ins[d["ob"]])).then_inc(sem("ld_" + m), mark("ld_" + m, "all", by=16))

            def load_gates(layer):
                name = {1: "L1_xcond_b_mod", 2: "L2_xcond_b_ada"}[layer]
                for g, (ly, i) in enumerate(GATES):
                    if ly == layer:
                        for b in range(B):
                            sp.dma_start(gates[:, g, b, :], bc(ins[name][i * C:(i + 1) * C])
                                         ).then_inc(sem(f"ld_g{layer}"), mark(f"ld_g{layer}", "all", by=16))

            def prep():
                n = 0
                for name, lo, k in COLUMN_ROWS:
                    src = ins[name]
                    if len(src.shape) == 2:
                        src = src.rearrange("a n -> (a n)")
                    src = src[lo:lo + k * P].rearrange("(k p) -> k p", p=P)
                    sp.dma_start(crow[n:n + k, :], src).then_inc(sem("ld_cols"), mark("ld_cols", "all", by=16))
                    n += k
                sp.dma_start(cx, ins["ctx_1024"].rearrange("b s c -> s b c")).then_inc(sem("ld_ctx"), 16)
                for w in ("ssq", "sskv"):
                    sp.dma_start(mod_w[w], rows(ins[mod_in[w]], 0)).then_inc(sem("ld_ss"), 16)
                sp.dma_start(mod_w["mod1"], rows(ins[mod_in["mod1"]], 0)).then_inc(sem("ld_mod1"), 16)
                load_att("x0")
                load_gates(1)
                load_gates(2)
                if "s1" in [s[1] for s in sched if s[0] == "attn"]:
                    load_att("s1")
                    filled(sp, ("gate", 1))
                    sp.dma_start(mod_w["ada2"], rows(ins[mod_in["ada2"]], 0)).then_inc(sem("ld_ada2"), 16)

            def stack(t, a, b, m, n):
                j = split_no[(a, t, b, m)]
                sp.wait_ge(sem("split"), at("split", j))
                sp.dma_start(scratch[j, :, :, 0:n].rearrange("s p n -> p s n"), st[:, j % 2, :, 0:n]
                             ).then_inc(sem(f"stout{j % 2}"), mark(f"stout{j % 2}", j, by=16))
                sp.wait_ge(sem(f"stout{j % 2}"), at(f"stout{j % 2}", j))
                prev = call_before(a, b if b != "c" else 0)
                if prev:
                    filled(sp, last_reader(*prev, 4 * m + 3))
                elif t == "q":
                    sp.wait_ge(sem("qzero"), 1)
                if t == "k":
                    sp.wait_ge(sem("kzero"), at("kzero", 1))
                name = f"{t}in{m}"
                for r, half in ((0, 0), (D, 1 if t == "q" else 0), (ROWM + 1, 0 if t == "q" else 1)):
                    for par in range(2):
                        src = scratch[j, half, :, 0:n].rearrange("(a two d) n -> two d a n", two=2, d=D)[par]
                        lo = 64 * par + r
                        if t == "q":
                            dst = qs[lo:lo + D, 4 * m:4 * m + 4, 0:n]
                        else:
                            dst = ks[:].rearrange("p (a two) n -> p a two n", two=2)[lo:lo + D, 4 * m:4 * m + 4, par, 0:n]
                        sp.dma_start(dst, src).then_inc(sem(name), mark(name, a, b, by=16))

            def ckv(a):
                for m in range(CC):
                    stack("k", a, "c", m, B * S)

            def proj(a, b):
                for t in ("q", "k") if ATT[a]["kind"] in ("self", "win") else ("q",):
                    for m in range(CC):
                        stack(t, a, b, m, L)

            def attn(a, b):
                kind = ATT[a]["kind"]
                start, ahead = side_plan(kind)

                def side(tasks):
                    for t in tasks:
                        if t[0] == "t":
                            p = t[1]
                            emptied(sp, ("t", a, b, p))
                            for j in range(2):
                                sp.dma_start(qs[64 * j + ROWM:64 * j + ROWM + 1, p, :], mt[j:j + 1, p % 2, :]
                                             ).then_inc(sem(f"mrow{p % 2}"), mark(f"mrow{p % 2}", a, b, p, by=16))

                def pack(g):
                    sp.wait_ge(sem("on"), at("on", a, b, g))
                    for j in range(GH):
                        h = g * GH + j
                        sp.dma_start(ht[D * (h % 8):D * (h % 8) + D, b, h // 8, :], onorm[32 * j:32 * j + D, :]
                                     ).then_inc(sem(f"pack{g % 2}"), mark(f"pack{g % 2}", a, b, g, by=16))

                side(start)
                steps = steps_of(kind)
                for i, (p, j, kt) in enumerate(steps):
                    side(ahead[i])
                    if i and (steps[i - 1][0] % 2 == 1) and steps[i - 1][0] != p:
                        pack(p // 2 - 1)
                pack(H // GH - 1)

            names = [s[1] for s in sched if s[0] == "attn"] + [s[1] for s in sched if s[0] == "mlp"]

            def post(a, b):
                if b < B - 1:
                    return
                nxt = {"x0": "x1", "s1": "w2", "x1": "t2"}.get(a)
                if nxt in names:
                    filled(sp, ("post", a, b, 1))
                    sp.wait_ge(sem("xb"), at("xb", a, b))
                    load_att(nxt)
                if a == "t2" and "prep3" in stages:
                    load_l3()

            def mods2():
                if "m1" in names:
                    filled(sp, ("gate", 4))
                    load_mlp("m1")

            def mlp(m, b):
                if m == "m1" and b == B - 1 and "m2" in names:
                    filled(sp, ("post", m, b, 1))
                    sp.wait_ge(sem("xb"), at("xb", m, b))
                    load_mlp("m2")
                if m == "m2" and b == B - 1 and "prep3" in stages:
                    filled(sp, ("post", m, b, 1))
                    sp.wait_ge(sem("xb"), at("xb", m, b))
                    load_l3b()

            def ld3(dst, src):
                sp.dma_start(dst, src).then_inc(sem("ld_l3"), mark("ld_l3", "all", by=16))

            def load_l3():
                filled(sp, ("post", "t2", B - 1, 1))
                for part, r0 in (("nx", 0), ("ev", C), ("an", 2 * C)):
                    for e in range(NE):
                        ld3(w3[part][:, :, e * RH:(e + 1) * RH], rows(ins["L3_xcond_e_w1"][e, r0:r0 + C, :], 0))
                    ld3(w3[part][:, :, NE * RH:NX], rows(ins["L3_xcond_gate_w1"][r0:r0 + C, :], 0))
                ld3(w3["w2"], ins["L3_xcond_e_w2"].rearrange("e (k p) n -> p (e k) n", p=P))
                ld3(w3["g2"], rows(ins["L3_xcond_gate_w2"], 0))
                ld3(w3q, rows(ins["L3_xcond_Wq"], 0))
                ld3(w3k, rows(ins["L3_xcond_Wk"], 0))
                ld3(w3v, rows(ins["L3_xcond_Wv"], 0))
                ld3(wr, rows(ins["L3_xcond_router_W"], 0))
                for i, name in enumerate(("L3_xcond_gate_b2", "L3_xcond_out_b")):
                    sp.dma_start(obias[:, i, :], bc(ins[name])).then_inc(sem("ld_b3"), mark("ld_b3", "all", by=16))

            def load_l3b():
                ld3(w3["ow"], rows(ins["L3_xcond_out_w"], 0))
                ld3(rbin, bc(ins["L3_xcond_router_b"]))
                ld3(b2e, ins["L3_xcond_e_b2"])

            out_v = out.rearrange("b (t p) c -> p (b t) c", p=P)

            def moe(b):
                for q in range(4):
                    sp.wait_ge(sem("xu"), at("xu", "moe", b, q))
                    lo = b * TB + 2 * q
                    sp.dma_start(out_v[:, lo:lo + 2, :], x[:, lo:lo + 2, :]).then_inc(sem("stored"), mark("stored", "all", by=16))

            run = {"prep": prep, "mods2": mods2, "ckv": ckv, "ln": lambda i, b: None, "proj": proj, "attn": attn, "post": post,
                   "mlp": mlp, "prep3": lambda: None, "moe": moe}
            for s in sched:
                run[s[0]](*s[1:])
            if "moe" not in stages:
                last = sched[-1]
                for b in range(B):
                    for r in range(2):
                        sp.wait_ge(sem("xu"), at("xu", last[1], b, r))
                sp.dma_start(out_v, x[:]).then_inc(sem("stored"), mark("stored", "all", by=16))
            sp.wait_ge(sem("stored"), at("stored", "all"))
    return seen


_INS = ['x', 'ctx_1024', 'cond_1024',
        'L0_xcond_Wq', 'L0_xcond_bq', 'L0_xcond_Wkv', 'L0_xcond_bkv', 'L0_xcond_Wp', 'L0_xcond_bp',
        'L0_xcond_Wss_q', 'L0_xcond_bss_q', 'L0_xcond_Wss_kv', 'L0_xcond_bss_kv',
        'L1_xcond_W_mod', 'L1_xcond_b_mod', 'L1_xcond_W_qkv', 'L1_xcond_b_qkv', 'L1_xcond_W_proj', 'L1_xcond_b_proj',
        'L1_xcond_W_qc', 'L1_xcond_b_qc', 'L1_xcond_W_kvc', 'L1_xcond_b_kvc', 'L1_xcond_W_cproj', 'L1_xcond_b_cproj',
        'L1_xcond_W_mlp1', 'L1_xcond_b_mlp1', 'L1_xcond_W_mlp2', 'L1_xcond_b_mlp2',
        'L2_xcond_w_ada', 'L2_xcond_b_ada', 'L2_xcond_w_qkv', 'L2_xcond_b_qkv', 'L2_xcond_w_so', 'L2_xcond_b_so',
        'L2_xcond_w_q', 'L2_xcond_b_q', 'L2_xcond_w_kv', 'L2_xcond_b_kv', 'L2_xcond_w_co', 'L2_xcond_b_co',
        'L2_xcond_w_m1', 'L2_xcond_b_m1', 'L2_xcond_w_m2', 'L2_xcond_b_m2',
        'L3_xcond_ln_gamma', 'L3_xcond_ln_beta', 'L3_xcond_Wq', 'L3_xcond_Wk', 'L3_xcond_Wv',
        'L3_xcond_router_W', 'L3_xcond_router_b', 'L3_xcond_e_w1', 'L3_xcond_e_b1', 'L3_xcond_e_w2', 'L3_xcond_e_b2',
        'L3_xcond_gate_w1', 'L3_xcond_gate_b1', 'L3_xcond_gate_w2', 'L3_xcond_gate_b2', 'L3_xcond_out_w', 'L3_xcond_out_b']


def kernel(_stop=None, **inputs):
    import numpy as _np
    import concourse.bacc as _bacc
    from concourse.bass_utils import run_bass_kernel_spmd as _run

    marks = None
    for _ in range(2):
        nc = _bacc.Bacc("TRN2", target_bir_lowering=False, num_devices=1)
        arrays, aps = {}, {}
        for name in _INS:
            a = _np.ascontiguousarray(inputs[name])
            arrays[f"in_{name}_dram"] = a
            aps[name] = nc.dram_tensor(f"in_{name}_dram", a.shape, mybir.dt.from_np(a.dtype), kind="ExternalInput").ap()
        out = nc.dram_tensor("out_0_dram", (B, L, C), F32, kind="ExternalOutput").ap()
        marks = build(nc, aps, out, marks, _stop)
    r = _run(nc, [arrays], core_ids=[0])
    return r.results[0]["out_0_dram"]
```

```python
from contextlib import ExitStack

import concourse.bass as bass
from concourse import mybir

P = 128
ALU = mybir.AluOpType
ACT = mybir.ActivationFunctionType
AX = mybir.AxisListType
F32 = mybir.dt.float32
F16 = mybir.dt.float16
U32 = mybir.dt.uint32

B, L, C = 2, 1024, 256
TB = L // P
CC = C // P
H, D = 16, 16
S = 77
HP = H // 2
GH = 4
RP = 7
SCALE = 0.25
TOPK_GONE = -3.0e38
SHIFT = 64
N1, N2, NE = 8, 8, 3
RH = 2 * C
SLOT = 1024
ROWM = 32

COLUMN_ROWS = [
    ("cond_1024", 0, 4),
    ("L0_xcond_bq", 0, 2), ("L0_xcond_bkv", 0, 2), ("L0_xcond_bss_q", 0, 4), ("L0_xcond_bss_kv", 0, 4),
    ("L1_xcond_b_mod", 0, 12), ("L1_xcond_b_qkv", 0, 4), ("L1_xcond_b_qc", 0, 2), ("L1_xcond_b_kvc", 0, 2),
    ("L1_xcond_b_mlp1", 0, 8),
    ("L2_xcond_b_ada", 0, 18), ("L2_xcond_b_qkv", 0, 4), ("L2_xcond_b_q", 0, 2), ("L2_xcond_b_kv", 0, 2),
    ("L2_xcond_b_m1", 0, 16),
    ("L3_xcond_ln_gamma", 0, 2), ("L3_xcond_ln_beta", 0, 2), ("L3_xcond_e_b1", 0, 12), ("L3_xcond_gate_b1", 0, 2),
]
COL = {}
NCOL = 0
for _name, _, _n in COLUMN_ROWS:
    COL[_name] = NCOL
    NCOL += _n

ATT = {
    "x0": dict(kind="cross", half=0, w=["L0_xcond_Wq", "L0_xcond_Wkv", "L0_xcond_Wp"], n=[256, 512, 256],
               vb=("L0_xcond_bkv", 256), ob="L0_xcond_bp", qb=COL["L0_xcond_bq"], kb=COL["L0_xcond_bkv"], ln=0, gate=None),
    "s1": dict(kind="self", half=1, w=["L1_xcond_W_qkv", "L1_xcond_W_proj"], n=[768, 256],
               vb=("L1_xcond_b_qkv", 512), ob="L1_xcond_b_proj", qb=COL["L1_xcond_b_qkv"], kb=COL["L1_xcond_b_qkv"] + 2, ln=1, gate=0),
    "x1": dict(kind="cross", half=0, w=["L1_xcond_W_qc", "L1_xcond_W_kvc", "L1_xcond_W_cproj"], n=[256, 512, 256],
               vb=("L1_xcond_b_kvc", 256), ob="L1_xcond_b_cproj", qb=COL["L1_xcond_b_qc"], kb=COL["L1_xcond_b_kvc"], ln=2, gate=None),
    "w2": dict(kind="win", half=1, w=["L2_xcond_w_qkv", "L2_xcond_w_so"], n=[768, 256],
               vb=("L2_xcond_b_qkv", 512), ob="L2_xcond_b_so", qb=COL["L2_xcond_b_qkv"], kb=COL["L2_xcond_b_qkv"] + 2, ln=4, gate=2),
    "t2": dict(kind="top", half=0, w=["L2_xcond_w_q", "L2_xcond_w_kv", "L2_xcond_w_co"], n=[256, 512, 256],
               vb=("L2_xcond_b_kv", 256), ob="L2_xcond_b_co", qb=COL["L2_xcond_b_q"], kb=COL["L2_xcond_b_kv"], ln=5, gate=3),
}
ATT_ORDER = ["x0", "s1", "x1", "w2", "t2"]
MLP = {
    "m1": dict(ln=3, gate=1, w=["L1_xcond_W_mlp1", "L1_xcond_W_mlp2"], n=[1024, 256], ob="L1_xcond_b_mlp2", hb=COL["L1_xcond_b_mlp1"]),
    "m2": dict(ln=6, gate=4, w=["L2_xcond_w_m1", "L2_xcond_w_m2"], n=[2048, 256], ob="L2_xcond_b_m2", hb=COL["L2_xcond_b_m1"]),
}
LN_EPS = [1e-5, 1e-6, 1e-6, 1e-6, 1e-6, 1e-6, 1e-6, 1e-5]
GATES = [(1, 2), (1, 5), (2, 2), (2, 5), (2, 8)]
MODS = ([("ssq", i, i < 2) for i in range(4)] + [("sskv", i, i < 2) for i in range(4)]
        + [("mod1", i, i in (2, 3, 8, 9)) for i in (0, 1, 2, 3, 6, 7, 8, 9)]
        + [("ada2", i, i in (2, 3, 8, 9, 14, 15)) for i in (0, 1, 2, 3, 6, 7, 8, 9, 12, 13, 14, 15)])
MOD_AT = {(w, i): n for n, (w, i, _) in enumerate(MODS)}
MOD_COL = {"ssq": COL["L0_xcond_bss_q"], "sskv": COL["L0_xcond_bss_kv"], "mod1": COL["L1_xcond_b_mod"], "ada2": COL["L2_xcond_b_ada"]}
LN_MOD = {0: ("ssq", 0, 2), 1: ("mod1", 2, 0), 3: ("mod1", 8, 6), 4: ("ada2", 2, 0), 5: ("ada2", 8, 6), 6: ("ada2", 14, 12)}


def schedule(stop):
    calls = []
    for name in ("x0", "s1", "x1", "m1", "w2", "t2", "m2", "moe"):
        calls += [(name, b) for b in range(B)]
        if name == stop:
            break
    ln = {name: d["ln"] for name, d in (*ATT.items(), *MLP.items())}
    ln["moe"] = 7
    out = [("prep",)]

    def norm(n, stage):
        if n < len(calls):
            out.append((stage, ln[calls[n][0]], calls[n][1]))

    def proj(n):
        if n < len(calls) and calls[n][0] in ATT:
            name, b = calls[n]
            if b == 0 and ATT[name]["kind"] in ("cross", "top"):
                out.append(("ckv", name))
            out.append(("proj", name, b))

    def body(n):
        name, b = calls[n]
        out.append(("attn", name, b) if name in ATT else ("mlp", name, b) if name in MLP else ("moe", b))

    norm(0, "norm")
    norm(0, "turn")
    proj(0)
    norm(1, "norm")
    norm(1, "turn")
    body(0)
    for n in range(len(calls)):
        nxt = calls[n + 1] if n + 1 < len(calls) else None
        proj(n + 1)
        if calls[n][0] in ATT:
            out.append(("post", *calls[n]))
        if calls[n] == ("x0", B - 1) and len(calls) > B:
            out.append(("mods2",))
        norm(n + 2, "norm")
        if nxt == ("moe", 0):
            out.append(("prep3",))
        if nxt and nxt[0] not in MLP:
            norm(n + 2, "turn")
        if nxt:
            body(n + 1)
        if nxt and nxt[0] in MLP:
            norm(n + 2, "turn")
    return out


def split_order(a):
    return [(t, m) for m in range(CC) for t in (("q", "k") if ATT[a]["kind"] in ("self", "win") else ("q",))]


def steps_of(kind):
    n = TB if kind == "self" else 1
    return [(2 * g + r // 2, r % 2, k) for g in range(H // GH) for k in range(n) for r in range(GH)]


def first_pass_units(kind):
    if kind == "self":
        return [(j, t, n) for j in range(2) for t in range(TB) for n in range(2)]
    return list(range(2 if kind == "top" else 4))


def side_plan(kind):
    units, per = first_pass_units(kind), len(steps_of(kind)) // (H // GH)
    ahead = [[] for _ in range(per * (H // GH))]
    start = []
    for p in range(HP):
        tasks = [("p1", p, u) for u in range(len(units))]
        turn = [] if kind == "top" else [("t", p)]
        if p < 2:
            start += tasks + turn
            continue
        base, odd = (p // 2 - 1) * per, p % 2
        if kind == "self":
            for i, t in enumerate(tasks):
                ahead[base + (odd * 32 + i) * 28 // 64].append(t)
            ahead[base + (29 if odd else 16)] += turn
        else:
            ahead[base + odd] += tasks + turn
    return start, ahead


def build(nc, ins, out, marks, stop=None):
    final = marks is not None
    marks = marks or {}
    seen, count, ring, half = {}, {}, [0], [0]
    sched = schedule(stop)
    stages = [s[0] for s in sched]

    with ExitStack() as ctx:
        sems = {}

        def sem(name):
            if name not in sems:
                sems[name] = ctx.enter_context(nc.semaphore(name))
            return sems[name]

        def mark(name, *key, by=1):
            count[name] = count.get(name, 0) + by
            seen[(name, *key)] = count[name]
            return by

        def at(name, *key):
            return marks[(name, *key)] if final else 1

        def sb(name, shape, dt):
            return ctx.enter_context(nc.sbuf_tensor(name, shape, dt))

        x = sb("x", [P, B * TB, C], F32)
        ht = sb("ht", [P, B, CC, L], F32)
        qs = sb("qs", [P, HP, L], F16)
        ks = sb("ks", [P, H, L], F16)
        vs = sb("vs", [P, TB, H, 32], F32)
        xn = sb("xn", [P, TB, C], F32)
        onorm = sb("onorm", [P, L], F32)
        area = sb("area", [P, 8192], F32)
        wa = sb("wa", [P, 2, 2048], F32)
        wm = sb("wm", [P, 6144], F32)
        gates = sb("gates", [P, len(GATES), B, C], F32)
        vbias = sb("vbias", [P, 2, C], F32)
        obias = sb("obias", [P, 3, C], F32)
        gbias = sb("gbias", [P, C], F32)
        ct = sb("ct", [P, 3, CC, B, S], F32)
        identf = sb("identf", [P, P], F32)
        identh = sb("identh", [P, P], F16)
        cols = sb("cols", [P, 128], F32)
        silc = sb("silc", [P, 4], F32)
        modc = sb("modc", [P, len(MODS), B], F32)
        stats = sb("stats", [P, TB, 6], F32)
        mv = sb("mv", [P, TB, 2], F32)
        vare = sb("vare", [P, TB], F32)
        rstd = sb("rstd", [P, TB], F32)
        mhalf = sb("mhalf", [P, TB], F32)
        m16 = sb("m16", [P, 2, 2, TB], F16)
        mhalves = sb("mhalves", [P, 2, 2, 2, TB], F16)
        mt = sb("mt", [2 * TB, 2, P], F16)
        rec = sb("rec", [P, 32], F32)
        w3own = sb("w3own", [P, 530], F32)
        v8 = sb("v8", [P, 2, 8, 8], F32)

        st = area[:, 0:2048].bitcast(F16).rearrange("p (r s n) -> p r s n", r=2, s=2)
        pr = area[:, 0:RP * L].rearrange("p (r n) -> p r n", r=RP)
        turned = area[:, 7168:8192]
        hid = area[:, :].rearrange("p (r k n) -> p r k n", r=2, k=8)
        cx = area[0:S, 4096:4608].rearrange("p (b c) -> p b c", b=B)
        cxn = area[0:S, 4608:5632].rearrange("p (v b c) -> p v b c", v=2, b=B)
        crow = area[:, 5632:5760]
        condb = area[:, 7168:7680].rearrange("p (b c n) -> p b c n", b=B, c=CC)
        xnf = xn[:].rearrange("p a b -> p (a b)")
        US = 8 * S
        top_s = [xnf[:, i * US:(i + 1) * US] for i in range(2)]
        top_w = xnf[:, 2 * US:3 * US]
        vsf = vs[:].rearrange("p a b c -> p (a b c)")
        top_p = [vsf[:, 1024 + i * US:1024 + (i + 1) * US] for i in range(4)]
        ksf = ks[:].rearrange("p a b -> p (a b)").bitcast(F32)
        qsf = qs[:].rearrange("p a b -> p (a b)").bitcast(F32)
        waf = wa[:].rearrange("p a b -> p (a b)")

        psum = ctx.enter_context(nc.psum_tensor("psum", [P, 4, SLOT], F32))
        sl = [psum[:, k, :] for k in range(4)] + [psum[:, 3, 512:1024]]

        n_split = sum(2 * (1 + (ATT[s[1]]["kind"] in ("self", "win"))) if s[0] == "proj" else 2
                      for s in sched if s[0] in ("proj", "ckv"))
        scratch = nc.dram_tensor("scratch", [n_split, 2, P, L], F16, kind="Internal").ap()
        split_no = {}
        for s in sched:
            if s[0] == "ckv":
                for m in range(CC):
                    split_no[(s[1], "k", "c", m)] = len(split_no)
            if s[0] == "proj":
                for t, m in split_order(s[1]):
                    split_no[(s[1], t, s[2], m)] = len(split_no)
        ln_calls = [("ln", *s[1:]) for s in sched if s[0] == "turn"]
        calls = [(s[1], s[2]) for s in sched if s[0] == "attn"]
        step_no, group_no = {}, {}
        for a, b in calls:
            for i in range(len(steps_of(ATT[a]["kind"]))):
                step_no[(a, b, i)] = len(step_no)
            for g in range(H // GH):
                group_no[(a, b, g)] = len(group_no)

        def open_slot(pe, key, k=None, signals=True):
            if k is None:
                k = ring[0]
                ring[0] = (ring[0] + 1) % 4
                if k == 3:
                    if seen.get(("opened", 4), 0):
                        pe.wait_ge(sem("free4"), seen[("opened", 4)])
                    seen["whole"] = seen.get(("opened", 3), 0) + 1
            elif k == "half":
                k = 3 + half[0]
                half[0] = 1 - half[0]
                if k == 4 and "whole" in seen:
                    pe.wait_ge(sem("free3"), seen.pop("whole"))
            n = seen.get(("opened", k), 0)
            if n:
                pe.wait_ge(sem(f"free{k}"), n)
            seen[("opened", k)] = n + 1
            seen[("filled", k)] = seen.get(("filled", k), 0) + signals
            seen[("slot", key)] = (k, seen[("filled", k)], n + 1)
            return k

        def where(key):
            return marks[("slot", key)] if final else (0, 1, 1)

        def filled(eng, key):
            k, n, _ = where(key)
            eng.wait_ge(sem(f"full{k}"), n)
            return sl[k]

        def emptied(eng, key):
            k, _, n = where(key)
            eng.wait_ge(sem(f"free{k}"), n)

        def free(key):
            return sem(f"free{where(key)[0]}")

        def call_before(a, b):
            i = calls.index((a, b))
            return calls[i - 1] if i else None

        def last_reader(a, b, p):
            kind = ATT[a]["kind"]
            if kind == "top":
                return ("p1", a, b, p, 3)
            return ("s", a, b, max(i for i, step in enumerate(steps_of(kind)) if step[0] == p))

        def wviews(a):
            at_, views = 0, []
            for n in ATT[a]["n"]:
                views.append(wa[:, ATT[a]["half"], at_:at_ + CC * n].rearrange("p (c n) -> p c n", c=CC))
                at_ += CC * n
            return views

        def qkv_views(a):
            v = wviews(a)
            if len(v) == 2:
                return v[0][:, :, 0:256], v[0][:, :, 256:512], v[0][:, :, 512:768], v[1]
            return v[0], v[1][:, :, 0:256], v[1][:, :, 256:512], v[2]

        mod_w = {
            "ssq": wm[:, 0:1024].rearrange("p (c n) -> p c n", c=CC),
            "sskv": wm[:, 1024:2048].rearrange("p (c n) -> p c n", c=CC),
            "mod1": wm[:, 2048:5120].rearrange("p (c n) -> p c n", c=CC),
            "ada2": wm[:, 0:4608].rearrange("p (c n) -> p c n", c=CC),
        }
        mod_in = {"ssq": "L0_xcond_Wss_q", "sskv": "L0_xcond_Wss_kv", "mod1": "L1_xcond_W_mod", "ada2": "L2_xcond_w_ada"}

        def mlp_views(m):
            n = MLP[m]["n"][0]
            up = wm[:, 0:CC * n].rearrange("p (c n) -> p c n", c=CC)
            down = wm[:, CC * n:CC * n + 8 * C].rearrange("p (k n) -> p k n", k=8)
            return up, down

        NX = NE * RH + C
        w3 = {
            "nx": ksf[:, 0:CC * NX].rearrange("p (c n) -> p c n", c=CC),
            "w2": ksf[:, CC * NX:CC * NX + 12 * C].rearrange("p (k n) -> p k n", k=12),
            "g2": ksf[:, CC * NX + 12 * C:CC * NX + 14 * C].rearrange("p (c n) -> p c n", c=CC),
            "ev": qsf[:, 0:CC * NX].rearrange("p (c n) -> p c n", c=CC),
            "an": vsf[:, 0:CC * NX].rearrange("p (c n) -> p c n", c=CC),
        }
        w3["ow"] = wm[:, 5632:6144].rearrange("p (c n) -> p c n", c=CC)
        w3q = qsf[:, CC * NX:CC * NX + 512].rearrange("p (c n) -> p c n", c=CC)
        w3k = vsf[:, CC * NX:CC * NX + 512].rearrange("p (c n) -> p c n", c=CC)
        w3v = w3own[:, 0:512].rearrange("p (c n) -> p c n", c=CC)
        wr = w3own[:, 512:530].rearrange("p (c n) -> p c n", c=6)
        VWN = NX + NE
        vw = waf[0:S, 0:B * VWN].rearrange("p (b n) -> p b n", b=B)
        g3 = wm[:, 0:CC * B * S].rearrange("p (c b s) -> p c b s", c=CC, b=B)
        kt3 = wm[:, 512:512 + CC * B * S].rearrange("p (c b s) -> p c b s", c=CC, b=B)
        vt3 = wm[:, 1024:1024 + CC * B * S].rearrange("p (c b s) -> p c b s", c=CC, b=B)
        wqt = wm[:, 1536:2048].rearrange("p (c n) -> p c n", c=CC)
        hb3 = wm[:, 2048:2048 + B * 14].rearrange("p (b n) -> p b n", b=B)
        rb3 = wm[:, 2080:2080 + B * NE].rearrange("p (b n) -> p b n", b=B)
        rbin = wm[:, 2088:2088 + NE]
        b2e = wm[0:NE, 2304:2560]
        p3 = wm[:, 2560:2560 + TB * S].rearrange("p (t s) -> p t s", t=TB)
        wt3 = wm[0:S, 3200:3200 + L]
        pt3 = wm[0:NE, 4224:4224 + L]
        sm3 = wm[:, 5248:5264]
        rs3 = wm[:, 5264:5272]
        lg3 = wm[:, 5280:5280 + TB * NE].rearrange("p (t e) -> p t e", t=TB)
        lm3 = wm[:, 5312:5320]
        ls3 = wm[:, 5320:5328]
        bm3 = wm[:, 5328:5336]
        hid3 = area[:, 0:12 * 512].rearrange("p (k n) -> p k n", k=12)
        gh3 = area[:, 6144:7168].rearrange("p (k n) -> p k n", k=2)
        rt3 = area[:, 7168:8192].rearrange("p (c n) -> p c n", c=CC)

        def mrow_no(a, b, p):
            n = 0
            for c in calls:
                if c == (a, b):
                    break
                if ATT[c[0]]["kind"] != "top":
                    n += HP
            return n + p

        def gz_of(g):
            return xnf[:, 1024:1536] if g == 0 else xnf[:, 1536:2048]

        block = ctx.enter_context(nc.Block())

        @block.tensor
        def _(pe):
            def accumulate(dst, pairs):
                for i, (lhs, rhs) in enumerate(pairs):
                    mm = pe.matmul(dst, lhs, rhs, start=(i == 0), stop=(i == len(pairs) - 1))
                return mm

            def mods(names, key):
                k = open_slot(pe, (key,))
                for n, (w, i, _) in enumerate(MODS):
                    if w in names:
                        mm = accumulate(sl[k][:, 2 * n:2 * n + 2],
                                        [(mod_w[w][:, c, i * P:(i + 1) * P], silc[:].rearrange("p (b c) -> p c b", c=CC)[:, c, :])
                                         for c in range(CC)])
                mm.then_inc(sem(f"full{k}"), 1)

            def gate_rows(layer, w):
                for g, (ly, i) in enumerate(GATES):
                    if ly != layer:
                        continue
                    k = open_slot(pe, ("gate", g))
                    for b in range(B):
                        mm = accumulate(sl[k][:, b * 256:b * 256 + 256],
                                        [(condb[:, b, c, :], mod_w[w][:, c, i * C:(i + 1) * C]) for c in range(CC)])
                    mm.then_inc(sem(f"full{k}"), 1)

            def prep():
                pe.wait_ge(sem("ident"), at("ident", "f"))
                pe.wait_ge(sem("ld_cols"), at("ld_cols", "all"))
                k = open_slot(pe, ("cols",))
                pe.transpose(sl[k][:, 0:NCOL], crow[0:NCOL, :], identf[0:NCOL, 0:NCOL]).then_inc(sem(f"full{k}"), 1)
                pe.wait_ge(sem("ld_ctx"), 16)
                k = open_slot(pe, ("ctraw",))
                for c in range(CC):
                    for b in range(B):
                        mm = pe.transpose(sl[k][:, (c * B + b) * P:(c * B + b) * P + S], cx[:, b, c * P:(c + 1) * P],
                                          identf[0:S, 0:S])
                mm.then_inc(sem(f"full{k}"), 1)
                for v in range(2):
                    pe.wait_ge(sem("cxn"), at("cxn", v))
                    k = open_slot(pe, ("ctn", v))
                    for c in range(CC):
                        for b in range(B):
                            mm = pe.transpose(sl[k][:, (c * B + b) * P:(c * B + b) * P + S],
                                              cxn[:, v, b, c * P:(c + 1) * P], identf[0:S, 0:S])
                    mm.then_inc(sem(f"full{k}"), 1)
                pe.wait_ge(sem("silc"), at("silc", "cols"))
                pe.wait_ge(sem("ld_ss"), 32)
                pe.wait_ge(sem("ld_mod1"), 16)
                mods(("ssq", "sskv", "mod1"), "mods1")
                pe.wait_ge(sem("silc"), at("silc", "rows"))
                gate_rows(1, "mod1")

            def mods2():
                pe.wait_ge(sem("ld_ada2"), 16)
                mods(("ada2",), "mods2")
                pe.wait_ge(sem("condb2"), 1)
                gate_rows(2, "ada2")

            def ckv(a):
                wq, wk, wv, wo = qkv_views(a)
                pe.wait_ge(sem("ld_" + a), at("ld_" + a, "all"))
                v = {"x0": 0, "x1": 1, "t2": 2}[a]
                pe.wait_ge(sem("ctdone"), at("ctdone", v))
                for m in range(CC):
                    k = open_slot(pe, ("k", a, "c", m))
                    accumulate(sl[k][:, 0:B * S],
                               [(wk[:, c, m * P:(m + 1) * P], ct[:, v, c].rearrange("p b s -> p (b s)")) for c in range(CC)]
                               ).then_inc(sem(f"full{k}"), 1)
                k = open_slot(pe, ("v", a, "c"))
                for b in range(B):
                    mm = accumulate(sl[k][0:S, b * C:(b + 1) * C], [(ct[:, v, c, b, :], wv[:, c, :]) for c in range(CC)])
                mm.then_inc(sem(f"full{k}"), 1)

            def ln(i, b):
                for c in range(CC):
                    k = open_slot(pe, ("ln", i, b, c))
                    for t in range(TB):
                        if c == 0:
                            pe.wait_ge(sem("xn"), at("xn", i, b, t))
                        mm = pe.transpose(sl[k][:, t * P:(t + 1) * P], xn[:, t, c * P:(c + 1) * P], identf[:, :])
                    mm.then_inc(sem(f"full{k}"), 1)

            def proj(a, b):
                wq, wk, wv, wo = qkv_views(a)
                both = ATT[a]["kind"] in ("self", "win")
                pe.wait_ge(sem("ld_" + a), at("ld_" + a, "all"))
                emptied(pe, ("ln", ATT[a]["ln"], b, CC - 1))
                for t, m in split_order(a):
                    w = wq if t == "q" else wk
                    k = open_slot(pe, (t, a, b, m))
                    for n in range(2):
                        mm = accumulate(sl[k][:, n * 512:(n + 1) * 512],
                                        [(w[:, c, m * P:(m + 1) * P], ht[:, b, c, n * 512:(n + 1) * 512]) for c in range(CC)])
                    mm.then_inc(sem(f"full{k}"), 1)
                if both:
                    for g in range(2):
                        k = open_slot(pe, ("v", a, b, g))
                        for t in range(4):
                            lo = (g * 4 + t) * P
                            mm = accumulate(sl[k][:, t * C:(t + 1) * C], [(ht[:, b, c, lo:lo + P], wv[:, c, :]) for c in range(CC)])
                        mm.then_inc(sem(f"full{k}"), 1)

            def attn(a, b):
                kind = ATT[a]["kind"]
                units = first_pass_units(kind)
                nk = S if kind in ("cross", "top") else P

                def first_pass(p, u):
                    m = p // 4
                    if u == 0:
                        pe.wait_ge(sem(f"qin{m}"), at(f"qin{m}", a, b))
                        pe.wait_ge(sem(f"kin{m}"), at(f"kin{m}", a, b if kind in ("self", "win") else "c"))
                        pe.wait_ge(sem("mzero"), at("mzero", a, b))
                    k = open_slot(pe, ("p1", a, b, p, u), "half")
                    if kind == "self":
                        j, t, n = units[u]
                        mm = pe.matmul(sl[k][:, 0:512], qs[:, p, t * P:(t + 1) * P],
                                       ks[:, 2 * p + j, n * 512:(n + 1) * 512], start=True, stop=True)
                    else:
                        for q2 in range(2):
                            t = u * 2 + q2
                            lo = t * P if kind == "win" else b * S
                            mm = pe.matmul(sl[k][:, q2 * 256:q2 * 256 + 2 * nk].rearrange("p (j s) -> p j s", j=2),
                                           qs[:, p, t * P:(t + 1) * P], ks[:, 2 * p:2 * p + 2, lo:lo + nk],
                                           start=True, stop=True)
                    mm.then_inc(sem(f"full{k}"), 1)

                def turn(p):
                    if kind == "self":
                        pe.wait_ge(sem("maxed"), at("maxed", a, b, p))
                    else:
                        emptied(pe, ("p1", a, b, p, 2))
                        emptied(pe, ("p1", a, b, p, 3))
                    k = open_slot(pe, ("t", a, b, p), "half")
                    pe.transpose(sl[k].bitcast(F16)[0:2 * TB, 0:P], m16[:, p % 2].rearrange("p j t -> p (j t)"), identh[:, :]
                                 ).then_inc(sem(f"full{k}"), 1)

                def side(tasks):
                    for t in tasks:
                        if t[0] == "t":
                            turn(t[1])
                        elif kind == "top":
                            first_pass(t[1], 2 * t[2])
                            first_pass(t[1], 2 * t[2] + 1)
                        else:
                            first_pass(t[1], t[2])

                def scores(i, p, j, kt):
                    k = open_slot(pe, ("s", a, b, i), step_no[(a, b, i)] % 2)
                    h = 2 * p + j
                    if kind == "top":
                        for t in range(TB):
                            if j == 0 and t % 4 == 0:
                                pe.wait_ge(sem("topp"), at("topp", a, b, p, t // 4))
                            src = top_p[(2 * p + t // 4) % 4].rearrange("p (q j s) -> p q j s", q=4, j=2)
                            mm = pe.transpose(sl[k][0:S, t * P:(t + 1) * P], src[:, t % 4, j, :], identf[:, :])
                    elif kind == "win":
                        pe.wait_ge(sem(f"mrow{p % 2}"), at(f"mrow{p % 2}", a, b, p))
                        for w in range(TB):
                            mm = pe.matmul(sl[k][:, w * P:(w + 1) * P], ks[:, h, w * P:(w + 1) * P],
                                           qs[:, p, w * P:(w + 1) * P], start=True, stop=True)
                    else:
                        if kt == 0:
                            pe.wait_ge(sem(f"mrow{p % 2}"), at(f"mrow{p % 2}", a, b, p))
                        lo = kt * P if kind == "self" else b * S
                        for n in range(2):
                            mm = pe.matmul(sl[k][0:nk, n * 512:(n + 1) * 512], ks[:, h, lo:lo + nk],
                                           qs[:, p, n * 512:(n + 1) * 512], start=True, stop=True)
                    mm.then_inc(sem(f"full{k}"), 1)

                def values(i, half_):
                    p, _, kt = steps[i]
                    g = p // 2
                    if kt == 0 and half_ == 0:
                        open_slot(pe, ("o", a, b, g), 2, signals=False)
                    if half_ == 0:
                        for r in range(GH):
                            emptied(pe, ("s", a, b, i + r))
                    if i == 0 and half_ == 0 and kind in ("self", "win"):
                        for v in range(2):
                            emptied(pe, ("v", a, b, v))
                    elif i == 0 and half_ == 0:
                        emptied(pe, ("v", a, "c"))
                    for n in range(4 * half_, 4 * half_ + 4) if kind == "win" else (half_,):
                        for r in range(GH):
                            h = g * GH + r
                            e = pr[:, step_no[(a, b, i + r)] % RP, :]
                            if kind == "win":
                                mm = pe.matmul(sl[2][32 * r:32 * r + 32, n * P:(n + 1) * P], vs[:, n, h, :], e[:, n * P:(n + 1) * P],
                                               start=True, stop=True, tile_position=(0, 32 * r))
                            else:
                                vt = kt if kind == "self" else b
                                mm = pe.matmul(sl[2][32 * r:32 * r + 32, n * 512:(n + 1) * 512], vs[0:nk, vt, h, :],
                                               e[0:nk, n * 512:(n + 1) * 512], start=(kt == 0),
                                               stop=(kind != "self" or kt == TB - 1), tile_position=(0, 32 * r))
                    if half_ == 1:
                        mm.then_inc(sem("pv"), mark("pv", a, b, i + GH - 1))

                start, ahead = side_plan(kind)
                side(start)
                steps = steps_of(kind)
                for i, (p, j, kt) in enumerate(steps):
                    scores(i, p, j, kt)
                    if i > GH and i % GH in (1, 2):
                        side(ahead[i][:1])
                        values(i - i % GH - GH, i % GH - 1)
                        side(ahead[i][1:])
                    else:
                        side(ahead[i])
                for half_ in range(2):
                    values(len(steps) - GH, half_)

            def post(a, b):
                wo = qkv_views(a)[3]
                for g in range(2):
                    pe.wait_ge(sem(f"pack{g}"), at(f"pack{g}", a, b, H // GH - 2 + g))
                for g in range(2):
                    k = open_slot(pe, ("post", a, b, g))
                    for t in range(4):
                        lo = (g * 4 + t) * P
                        mm = accumulate(sl[k][:, t * C:(t + 1) * C], [(ht[:, b, c, lo:lo + P], wo[:, c, :]) for c in range(CC)])
                    mm.then_inc(sem(f"full{k}"), 1)

            def mlp(m, b):
                up, down = mlp_views(m)
                pe.wait_ge(sem("ld_" + m), at("ld_" + m, "all"))
                emptied(pe, ("ln", MLP[m]["ln"], b, CC - 1))
                njob = 4 if m == "m1" else 8

                def hidden(r):
                    for j in range(njob):
                        k = open_slot(pe, ("up", m, b, r, j))
                        for n in range(2):
                            ch = 2 * j + n if m == "m1" else j + 8 * n
                            mm = accumulate(sl[k][:, n * 512:(n + 1) * 512],
                                            [(up[:, c, ch * P:(ch + 1) * P], ht[:, b, c, r * 512:(r + 1) * 512]) for c in range(CC)])
                        mm.then_inc(sem(f"full{k}"), 1)

                def lower(r):
                    emptied(pe, ("up", m, b, r, njob - 1))
                    k = open_slot(pe, ("post", m, b, r))
                    for t in range(4):
                        mm = accumulate(sl[k][:, t * C:(t + 1) * C],
                                        [(hid[:, r, c, t * P:(t + 1) * P], down[:, c, :]) for c in range(8)])
                    mm.then_inc(sem(f"full{k}"), 1)

                hidden(0)
                hidden(1)
                lower(0)
                lower(1)

            def prep3():
                pe.wait_ge(sem("ld_l3"), at("ld_l3", "all"))
                k = open_slot(pe, ("wqt",))
                for c in range(CC):
                    for m in range(CC):
                        mm = pe.transpose(sl[k][:, (m * CC + c) * P:(m * CC + c + 1) * P], w3q[:, c, m * P:(m + 1) * P], identf[:, :])
                mm.then_inc(sem(f"full{k}"), 1)
                for name, w in (("kt3", w3k), ("vt3", w3v)):
                    k = open_slot(pe, (name,))
                    for m in range(CC):
                        mm = accumulate(sl[k][:, m * 512:m * 512 + B * S],
                                        [(w[:, c, m * P:(m + 1) * P], ct[:, 2, c].rearrange("p b s -> p (b s)")) for c in range(CC)])
                    mm.then_inc(sem(f"full{k}"), 1)
                emptied(pe, ("wqt",))
                emptied(pe, ("kt3",))
                k = open_slot(pe, ("g3",))
                for m in range(CC):
                    mm = accumulate(sl[k][:, m * 512:m * 512 + B * S],
                                    [(wqt[:, c, m * P:(m + 1) * P], kt3[:, c].rearrange("p b s -> p (b s)")) for c in range(CC)])
                mm.then_inc(sem(f"full{k}"), 1)
                emptied(pe, ("vt3",))
                for b in range(B):
                    for g in range(2):
                        k = open_slot(pe, ("vw", b, g))
                        for n in range(2):
                            lo = g * 1024 + n * 512
                            if lo >= NX:
                                continue
                            hi = min(lo + 512, NX)
                            mm = accumulate(sl[k][0:S, n * 512:n * 512 + hi - lo],
                                            [(vt3[:, c, b, :], w3["ev"][:, c, lo:hi]) for c in range(CC)])
                        if g == 1:
                            mm = accumulate(sl[k][0:S, 768:768 + NE], [(vt3[:, c, b, :], wr[:, 2 + c, :]) for c in range(CC)])
                        mm.then_inc(sem(f"full{k}"), 1)
                k = open_slot(pe, ("anchor",))
                cond = cols[:, 0:4].rearrange("p (b c) -> p c b", c=CC)
                for n in range(14):
                    accumulate(sl[k][:, 2 * n:2 * n + 2], [(w3["an"][:, c, n * P:(n + 1) * P], cond[:, c, :]) for c in range(CC)])
                pe.wait_ge(sem("condb3"), 1)
                for b in range(B):
                    mm = accumulate(sl[k][:, 512 + 4 * b:512 + 4 * b + NE], [(condb[:, b, c, :], wr[:, 4 + c, :]) for c in range(CC)])
                mm.then_inc(sem(f"full{k}"), 1)

            def moe(b):
                emptied(pe, ("ln", 7, b, CC - 1))
                emptied(pe, ("g3",))
                k = open_slot(pe, ("sc3", b))
                for t in range(TB):
                    mm = accumulate(sl[k][:, t * P:t * P + S], [(ht[:, b, c, t * P:(t + 1) * P], g3[:, c, b, :]) for c in range(CC)])
                mm.then_inc(sem(f"full{k}"), 1)
                pe.wait_ge(sem("p3"), at("p3", b))
                k = open_slot(pe, ("wt3", b))
                for t in range(TB):
                    mm = pe.transpose(sl[k][0:S, t * P:(t + 1) * P], p3[:, t, :], identf[:, :])
                mm.then_inc(sem(f"full{k}"), 1)
                emptied(pe, ("wt3", b))
                emptied(pe, ("vw", B - 1, 1))
                emptied(pe, ("vw", B - 1, 0))
                emptied(pe, ("vw", 0, 1))
                emptied(pe, ("vw", 0, 0))
                k = open_slot(pe, ("lg3", b))
                for t in range(TB):
                    lo = t * P
                    mm = accumulate(sl[k][:, 4 * t:4 * t + NE],
                                    [(ht[:, b, c, lo:lo + P], wr[:, c, :]) for c in range(CC)] + [(wt3[:, lo:lo + P], vw[:, b, NX:VWN])])
                mm.then_inc(sem(f"full{k}"), 1)
                for r in range(2):
                    lo = r * 512
                    for j in range(7):
                        k = open_slot(pe, ("h3", b, r, j))
                        for n in range(2):
                            ch = 2 * j + n
                            mm = accumulate(sl[k][:, n * 512:(n + 1) * 512],
                                            [(w3["nx"][:, c, ch * P:(ch + 1) * P], ht[:, b, c, lo:lo + 512]) for c in range(CC)]
                                            + [(vw[:, b, ch * P:(ch + 1) * P], wt3[:, lo:lo + 512])])
                        mm.then_inc(sem(f"full{k}"), 1)
                    if r == 0:
                        pe.wait_ge(sem("rp3"), at("rp3", b))
                        k = open_slot(pe, ("pt3", b))
                        for t in range(TB):
                            mm = pe.transpose(sl[k][0:NE, t * P:(t + 1) * P], lg3[:, t, :], identf[:, :])
                        mm.then_inc(sem(f"full{k}"), 1)
                        emptied(pe, ("pt3", b))
                    emptied(pe, ("h3", b, r, 6))
                    for t in range(4):
                        k = open_slot(pe, ("ex3", b, r, t))
                        for e in range(NE):
                            accumulate(sl[k][:, e * C:(e + 1) * C],
                                       [(hid3[:, 4 * e + c, t * P:(t + 1) * P], w3["w2"][:, 4 * e + c, :]) for c in range(4)])
                        pe.matmul(sl[k][:, 768:1024], pt3[:, lo + t * P:lo + (t + 1) * P], b2e, start=True, stop=True
                                  ).then_inc(sem(f"full{k}"), 1)
                    k = open_slot(pe, ("rt3", b, r))
                    for t in range(4):
                        pe.wait_ge(sem("r3"), at("r3", b, r, t))
                        for c in range(CC):
                            mm = pe.transpose(sl[k][:, c * 512 + t * P:c * 512 + (t + 1) * P], xn[:, t, c * P:(c + 1) * P], identf[:, :])
                    mm.then_inc(sem(f"full{k}"), 1)
                    emptied(pe, ("rt3", b, r))
                    for g in range(2):
                        k = open_slot(pe, ("y3", b, r, g))
                        for t in range(2):
                            q = (2 * g + t) * P
                            accumulate(sl[k][:, t * C:(t + 1) * C], [(rt3[:, c, q:q + P], w3["ow"][:, c, :]) for c in range(CC)])
                            mm = accumulate(sl[k][:, 512 + t * C:512 + (t + 1) * C],
                                            [(gh3[:, c, q:q + P], w3["g2"][:, c, :]) for c in range(CC)])
                        mm.then_inc(sem(f"full{k}"), 1)

            run = {"prep": prep, "mods2": mods2, "ckv": ckv, "norm": lambda i, b: None, "turn": ln, "proj": proj, "attn": attn, "post": post,
                   "mlp": mlp, "prep3": prep3, "moe": moe}
            for s in sched:
                run[s[0]](*s[1:])

        @block.scalar
        def _(act):
            def silu_cond():
                act.wait_ge(sem("cols"), at("cols", "copied"))
                act.activation(silc[:], cols[:, 0:4], ACT.Silu).then_inc(sem("silc"), mark("silc", "cols"))

            def prep():
                for q in range(4):
                    act.dma_start(x[:, 4 * q:4 * q + 4, :],
                                  ins["x"].rearrange("b (t p) c -> p (b t) c", p=P)[:, 4 * q:4 * q + 4, :]
                                  ).then_inc(sem(f"ld_x{q}"), mark(f"ld_x{q}", by=16))
                silu_cond()

            def mods2():
                pass

            def split_evac(t, a, b, m, n, biascol):
                j = split_no[(a, t, b, m)]
                if j >= 2:
                    act.wait_ge(sem(f"stout{j % 2}"), at(f"stout{j % 2}", j - 2))
                src = filled(act, (t, a, b, m))
                act.activation(st[:, j % 2, 0, 0:n], src[:, 0:n], ACT.Identity, bias=cols[:, biascol + m:biascol + m + 1]
                               ).then_inc(sem("high"), mark("high", j))

            def ckv(a):
                for m in range(CC):
                    split_evac("k", a, "c", m, B * S, ATT[a]["kb"])

            def ln(i, b):
                if i == 0:
                    act.wait_ge(sem("modc"), at("modc", 1))
                if i in LN_MOD:
                    w, s0, b0 = LN_MOD[i]
                    if w == "ada2":
                        act.wait_ge(sem("modc"), at("modc", 2))
                for c in range(CC):
                    if i in LN_MOD:
                        scale = modc[:, MOD_AT[(w, s0 + c)], b:b + 1]
                        bias = modc[:, MOD_AT[(w, b0 + c)], b:b + 1]
                    elif i == 7:
                        g0, e0 = COL["L3_xcond_ln_gamma"], COL["L3_xcond_ln_beta"]
                        scale, bias = cols[:, g0 + c:g0 + c + 1], cols[:, e0 + c:e0 + c + 1]
                    else:
                        scale, bias = 1.0, 0.0
                    src = filled(act, ("ln", i, b, c))
                    if i == 4:
                        act.activation(ht[:, b, c, 0:L - SHIFT], src[:, SHIFT:L], ACT.Identity, bias=bias, scale=scale)
                        act.activation(ht[:, b, c, L - SHIFT:L], src[:, 0:SHIFT], ACT.Identity, bias=bias, scale=scale
                                       ).then_inc(free(("ln", i, b, c)), 1)
                    else:
                        act.activation(ht[:, b, c, :], src, ACT.Identity, bias=bias, scale=scale
                                       ).then_inc(free(("ln", i, b, c)), 1)

            def proj(a, b):
                for t, m in split_order(a):
                    split_evac(t, a, b, m, L, ATT[a]["qb" if t == "q" else "kb"])

            def attn(a, b):
                kind = ATT[a]["kind"]
                nk = S if kind in ("cross", "top") else P
                start, ahead = side_plan(kind)

                def top_side(tasks):
                    for _, p, u in tasks:
                        n = 2 * p + u
                        if n >= 2:
                            act.wait_ge(sem("topp"), at("topp", a, b, (n - 2) // 2, (n - 2) % 2))
                        elif (a, b) != calls[0] and b > 0:
                            act.wait_ge(sem("topp"), at("topp", a, b - 1, HP - 1, n))
                        for v in range(2):
                            src = filled(act, ("p1", a, b, p, 2 * u + v))
                            act.activation(top_s[n % 2].rearrange("p (q s) -> p q s", q=4)[:, 2 * v:2 * v + 2, :],
                                           src[:, 0:512].rearrange("p (q s) -> p q s", q=2)[:, :, 0:2 * S], ACT.Identity
                                           ).then_inc(free(("p1", a, b, p, 2 * u + v)), 1)
                        act.wait_ge(sem("topd"), at("topd", a, b, p, u))
                        act.activation(top_p[n % 4], top_p[n % 4], ACT.Exp, scale=SCALE).then_inc(sem("tope"), mark("tope", a, b, p, u))

                if kind == "top":
                    turns = [s for s in sched[:sched.index(("attn", a, b))] if s[0] == "turn"]
                    filled(act, ("ln", *turns[-1][1:], CC - 1))
                    top_side(start)
                for i in range(len(steps_of(kind))):
                    n = step_no[(a, b, i)]
                    if n >= RP:
                        act.wait_ge(sem("pv"), (n - RP) // GH + 1)
                    if i == 0:
                        for j in range(split_no[(a, "k" if kind in ("self", "win") else "q", b, CC - 1)] - 1,
                                       split_no[(a, "k" if kind in ("self", "win") else "q", b, CC - 1)] + 1):
                            act.wait_ge(sem(f"stout{j % 2}"), at(f"stout{j % 2}", j))
                    src = filled(act, ("s", a, b, i))
                    if kind == "top":
                        act.activation(pr[0:nk, n % RP, :], src[0:nk, :], ACT.Identity).then_inc(free(("s", a, b, i)), 1)
                        top_side(ahead[i])
                    else:
                        act.activation(pr[0:nk, n % RP, :], src[0:nk, :], ACT.Exp, scale=SCALE).then_inc(free(("s", a, b, i)), 1)

            def mlp(m, b):
                hb = MLP[m]["hb"]
                for r in range(2):
                    if b:
                        filled(act, ("post", m, b - 1, r))
                    for j in range(4 if m == "m1" else 8):
                        src = filled(act, ("up", m, b, r, j))
                        if m == "m1":
                            for n in range(2):
                                ch = 2 * j + n
                                ins_ = act.activation(hid[:, r, ch, :], src[:, n * 512:(n + 1) * 512], ACT.Gelu_apprx_tanh,
                                                      bias=cols[:, hb + ch:hb + ch + 1])
                            ins_.then_inc(free(("up", m, b, r, j)), 1)
                        else:
                            act.activation(hid[:, r, j, :], src[:, 0:512], ACT.Silu, bias=cols[:, hb + j:hb + j + 1]
                                           ).then_inc(sem("silu"), mark("silu", m, b, r, j))

            def prep3():
                pass

            def moe(b):
                src = filled(act, ("sc3", b))
                act.wait_ge(sem("bm3"), at("bm3", b))
                for t in range(TB):
                    mm = act.activation(p3[:, t, :], src[:, t * P:t * P + S], ACT.Exp, bias=bm3[:, t:t + 1], scale=1.0 / 16,
                                        accum_out=sm3[:, 8 + t:9 + t])
                mm.then_inc(free(("sc3", b)), 1)
                src = filled(act, ("wt3", b))
                act.activation(wt3, src[0:S, :], ACT.Identity).then_inc(free(("wt3", b)), 1)
                act.wait_ge(sem("lgs"), at("lgs", b))
                act.activation(lg3, lg3, ACT.Exp).then_inc(sem("lge"), mark("lge", b))
                for r in range(2):
                    for j in range(7):
                        src = filled(act, ("h3", b, r, j))
                        if j == 0 and (b or r):
                            filled(act, ("y3", (2 * b + r - 1) // 2, (2 * b + r - 1) % 2, 1))
                        if j == 0:
                            act.wait_ge(sem("hb3"), 1)
                        for n in range(2):
                            ch = 2 * j + n
                            dst = hid3[:, ch, :] if ch < 12 else gh3[:, ch - 12, :]
                            mm = act.activation(dst, src[:, n * 512:(n + 1) * 512], ACT.Silu, bias=hb3[:, b, ch:ch + 1])
                        mm.then_inc(free(("h3", b, r, j)), 1)
                    if r == 0:
                        src = filled(act, ("pt3", b))
                        act.activation(pt3, src[0:NE, :], ACT.Identity).then_inc(free(("pt3", b)), 1)
                    src = filled(act, ("rt3", b, r))
                    act.activation(rt3, src.rearrange("p (c n) -> p c n", c=CC), ACT.Identity).then_inc(free(("rt3", b, r)), 1)
                    for g in range(2):
                        act.wait_ge(sem("gz"), at("gz", b, r, g))
                        act.activation(gz_of(g), gz_of(g), ACT.Tanh, scale=0.5).then_inc(sem("tanh"), mark("tanh", b, r, g))

            run = {"prep": prep, "mods2": mods2, "ckv": ckv, "norm": lambda i, b: None, "turn": ln, "proj": proj, "attn": attn,
                   "post": lambda a, b: None, "mlp": mlp, "prep3": prep3, "moe": moe}
            for s in sched:
                run[s[0]](*s[1:])

        @block.vector
        def _(dve):
            chain = [0]

            def linked(instr):
                chain[0] += 1
                instr.then_inc(sem("dve_chain"), 1)
                dve.wait_ge(sem("dve_chain"), chain[0])

            def prep():
                dve.memset(mhalf[:], -0.5).then_inc(sem("mhalf"), 1)
                dve.memset(qs[:].rearrange("p a b -> p (a b)").bitcast(U32), 0).then_inc(sem("qzero"), 1)
                dve.wait_ge(sem("ld_ctx"), 16)
                for b in range(B):
                    i = dve.bn_stats(stats[0:S, b, :], cx[:, b, :])
                linked(i)
                for b in range(B):
                    i = dve.bn_aggr(mv[0:S, b, :], stats[0:S, b, :])
                i.then_inc(sem("mv"), mark("mv", "ctx"))
                src = filled(dve, ("cols",))
                linked(dve.tensor_copy(cols[:, 0:NCOL], src[:, 0:NCOL]))
                dve.tensor_copy(cols[:, 127:128], src[:, 0:1]).then_inc(free(("cols",)), 1)
                dve.memset(rec[:, 0:1], 0.0).then_inc(sem("cols"), mark("cols", "copied"))
                src = filled(dve, ("ctraw",))
                dve.tensor_copy(ct[:, 2].rearrange("p c b s -> p (c b) s"),
                                src[:, 0:512].rearrange("p (g s) -> p g s", g=4)[:, :, 0:S]).then_inc(free(("ctraw",)), 1)
                dve.wait_ge(sem("rstd"), at("rstd", "ctx"))
                for v in range(2):
                    for b in range(B):
                        i = dve.tensor_scalar(cxn[:, v, b, :], cx[:, b, :], mv[0:S, b, 0:1], rstd[0:S, 4 * v + b:4 * v + b + 1],
                                              ALU.subtract, ALU.mult)
                    i.then_inc(sem("cxn"), mark("cxn", v))
                dve.wait_ge(sem("silc"), at("silc", "cols"))
                for b in range(B):
                    for c in range(CC):
                        i = dve.tensor_copy(condb[:, b, c, :], silc[:, b * CC + c:b * CC + c + 1].to_broadcast([P, P]))
                i.then_inc(sem("silc"), mark("silc", "rows"))
                src = filled(dve, ("ctn", 1))
                dve.tensor_copy(ct[:, 1].rearrange("p c b s -> p (c b) s"),
                                src[:, 0:512].rearrange("p (g s) -> p g s", g=4)[:, :, 0:S]).then_inc(free(("ctn", 1)), 1)
                mod_columns(1, ("ssq", "sskv", "mod1"), "mods1")
                src = filled(dve, ("ctn", 0))
                for c in range(CC):
                    for b in range(B):
                        i = dve.tensor_scalar(ct[:, 0, c, b, :], src[:, (c * B + b) * P:(c * B + b) * P + S],
                                              modc[:, MOD_AT[("sskv", c)], b:b + 1], modc[:, MOD_AT[("sskv", 2 + c)], b:b + 1],
                                              ALU.mult, ALU.add)
                i.then_inc(free(("ctn", 0)), 1)
                for v in (2, 1, 0):
                    dve.memset(rec[:, v:v + 1], 0.0).then_inc(sem("ctdone"), mark("ctdone", v))
                gate_rows(1)

            def mod_columns(n, names, key):
                lo = min(i for i, mm in enumerate(MODS) if mm[0] in names)
                src = filled(dve, (key,))
                for w in names:
                    blocks = [(i, bl) for i, (ww, bl, _) in enumerate(MODS) if ww == w]
                    run0 = 0
                    for r in range(len(blocks)):
                        if r + 1 == len(blocks) or blocks[r + 1][1] != blocks[r][1] + 1:
                            i0, b0 = blocks[run0]
                            nb = r - run0 + 1
                            c0 = MOD_COL[w] + b0
                            ins_ = dve.tensor_tensor(modc[:, i0:i0 + nb, :], src[:, 2 * i0:2 * (i0 + nb)].rearrange("p (n b) -> p n b", b=B),
                                                     cols[:, c0:c0 + nb].unsqueeze(2).to_broadcast([P, nb, B]), ALU.add)
                            run0 = r + 1
                linked(ins_)
                for i, (w, bl, plus) in enumerate(MODS):
                    if w in names and plus and not (i and MODS[i - 1][0] == w and MODS[i - 1][2] and MODS[i - 1][1] == bl - 1):
                        linked(dve.tensor_scalar_add(modc[:, i:i + 2, :], modc[:, i:i + 2, :], 1.0))
                dve.tensor_copy(rec[:, 4:5], src[:, 2 * lo:2 * lo + 1]).then_inc(free((key,)), 1)
                dve.memset(rec[:, 5:6], 0.0).then_inc(sem("modc"), mark("modc", n))

            def gate_rows(layer):
                for g, (ly, _) in enumerate(GATES):
                    if ly == layer:
                        dve.wait_ge(sem(f"ld_g{layer}"), at(f"ld_g{layer}", "all"))
                        src = filled(dve, ("gate", g))
                        dve.tensor_tensor(gates[:, g], src[:, 0:512].rearrange("p (b c) -> p b c", b=B), gates[:, g], ALU.add
                                          ).then_inc(free(("gate", g)), 1)

            def mods2():
                mod_columns(2, ("ada2",), "mods2")
                dve.wait_ge(sem("ld_g2"), 96)
                i = None
                for b in range(B):
                    for c in range(CC):
                        i = dve.tensor_copy(condb[:, b, c, :], silc[:, b * CC + c:b * CC + c + 1].to_broadcast([P, P]))
                i.then_inc(sem("condb2"), 1)
                gate_rows(2)

            def split(t, a, b, m, n):
                j = split_no[(a, t, b, m)]
                src = filled(dve, (t, a, b, m))
                dve.wait_ge(sem("high"), at("high", j))
                col = ATT[a]["qb" if t == "q" else "kb"] + m
                dve.scalar_tensor_tensor(out=st[:, j % 2, 1, 0:n], in0=src[:, 0:n], scalar=cols[:, col:col + 1], in1=st[:, j % 2, 0, 0:n],
                                         op0=ALU.add, op1=ALU.subtract).then_inc(free((t, a, b, m)), 1)

            def ckv(a):
                for m in range(CC):
                    split("k", a, "c", m, B * S)
                src = filled(dve, ("v", a, "c"))
                dve.wait_ge(sem("ld_" + a), at("ld_" + a, "all"))
                if a == "x0":
                    dve.wait_ge(sem("vones"), 1)
                dve.tensor_tensor(vs[0:S, 0:B, :, 0:D], src[0:S, 0:B * C].rearrange("p (b h d) -> p b h d", b=B, h=H),
                                  vbias[0:S, ATT[a]["half"], :].rearrange("p (h d) -> p h d", h=H).unsqueeze(1).to_broadcast([S, B, H, D]),
                                  ALU.add).then_inc(free(("v", a, "c")), 1)

            def ln(i, b):
                if i == 0:
                    dve.wait_ge(sem(f"ld_x{2 * b}"), 16)
                    dve.wait_ge(sem(f"ld_x{2 * b + 1}"), 16)
                else:
                    dve.wait_ge(sem("xu"), at("xu", prev_update(i, b), b, 1))
                prev = ln_calls.index(("ln", i, b)) - 1
                for t in range(TB):
                    ins_ = dve.bn_stats(stats[:, t, :], x[:, b * TB + t, :])
                linked(ins_)
                for t in range(TB):
                    ins_ = dve.bn_aggr(mv[:, t, :], stats[:, t, :])
                ins_.then_inc(sem("mv"), mark("mv", i, b))
                if prev >= 0:
                    filled(dve, (*ln_calls[prev], CC - 1))
                dve.wait_ge(sem("rstd"), at("rstd", i, b))
                for t in range(TB):
                    dve.tensor_scalar(xn[:, t, :], x[:, b * TB + t, :], mv[:, t, 0:1], rstd[:, t:t + 1],
                                      ALU.subtract, ALU.mult).then_inc(sem("xn"), mark("xn", i, b, t))

            def prev_update(i, b):
                order = ["x0", "s1", "x1", "m1", "w2", "t2", "m2"]
                return order[i - 1]

            def proj(a, b):
                both = ATT[a]["kind"] in ("self", "win")
                for t, m in split_order(a):
                    split(t, a, b, m, L)
                if both:
                    dve.wait_ge(sem("ld_" + a), at("ld_" + a, "all"))
                    for g in range(2):
                        src = filled(dve, ("v", a, b, g))
                        dve.tensor_tensor(vs[:, 4 * g:4 * g + 4, :, 0:D], src.rearrange("p (t h d) -> p t h d", t=4, h=H),
                                          vbias[:, ATT[a]["half"], :].rearrange("p (h d) -> p h d", h=H).unsqueeze(1).to_broadcast([P, 4, H, D]),
                                          ALU.add).then_inc(free(("v", a, b, g)), 1)

            def attn(a, b):
                kind = ATT[a]["kind"]
                units = first_pass_units(kind)
                nk = S if kind in ("cross", "top") else P
                start, ahead = side_plan(kind)

                def maxima(p, u):
                    src = filled(dve, ("p1", a, b, p, u))
                    if u == 0 and p >= 2:
                        filled(dve, ("t", a, b, p - 2))
                    if u == 0 and p < 2 and call_before(a, b):
                        filled(dve, ("t", *call_before(a, b), HP - 2 + p))
                    src = src[:, 0:512]
                    if kind == "self":
                        j, t, n = units[u]
                        dst, v = mhalves[:, p % 2, n, j, t:t + 1], src
                    else:
                        dst = m16[:, p % 2, :, 2 * u:2 * u + 2].rearrange("p j q -> p q j")
                        v = src.rearrange("p (q n) -> p q n", q=2)[:, :, 0:2 * nk].rearrange("p q (j s) -> p q j s", j=2)
                    dve.tensor_reduce(dst, v, AX.X, ALU.max, negate=True).then_inc(free(("p1", a, b, p, u)), 1)
                    if kind == "self" and u == len(units) - 1:
                        emptied(dve, ("p1", a, b, p, u - 1))
                        emptied(dve, ("p1", a, b, p, u))
                        dve.tensor_tensor(m16[:, p % 2], mhalves[:, p % 2, 0], mhalves[:, p % 2, 1], ALU.min
                                          ).then_inc(sem("maxed"), mark("maxed", a, b, p))

                def turned_out(p):
                    n = mrow_no(a, b, p)
                    if n >= 2:
                        dve.wait_ge(sem(f"mrow{p % 2}"), 32 * (n // 2))
                    src = filled(dve, ("t", a, b, p))
                    dve.tensor_copy(mt[:, p % 2, :], src.bitcast(F16)[0:2 * TB, 0:P]).then_inc(free(("t", a, b, p)), 1)

                def keep_top(p, u):
                    n = 2 * p + u
                    sc, w, pp = top_s[n % 2], top_w, top_p[n % 4]
                    emptied(dve, ("p1", a, b, p, 2 * u))
                    emptied(dve, ("p1", a, b, p, 2 * u + 1))
                    rows = [slice(r * S, (r + 1) * S) for r in range(8)]
                    for r in range(8):
                        i = dve.max(v8[:, 0, r, :], sc[:, rows[r]])
                    chain[0] += 1
                    i.then_inc(sem("dve_chain"), 1)
                    dve.wait_ge(sem("dve_chain"), chain[0])
                    dve.memset(rec[:, 0:1], 0.0).then_inc(sem("topm"), mark("topm", a, b, p, u))
                    for r in range(8):
                        i = dve.match_replace(w[:, rows[r]], v8[:, 0, r, :], sc[:, rows[r]], TOPK_GONE)
                    linked(i)
                    for r in range(8):
                        i = dve.max(v8[:, 1, r, :], w[:, rows[r]])
                    linked(i)
                    for r in range(8):
                        i = dve.match_replace(w[:, rows[r]], v8[:, 1, r, :], w[:, rows[r]], TOPK_GONE)
                    linked(i)
                    dve.wait_ge(sem("tope"), at("tope", a, b, p, u))
                    dve.scalar_tensor_tensor(out=pp, in0=w, scalar=TOPK_GONE / 2, in1=pp, op0=ALU.is_le, op1=ALU.mult
                                             ).then_inc(sem("topp"), mark("topp", a, b, p, u))

                def side(tasks):
                    for t in tasks:
                        if kind == "top":
                            keep_top(t[1], t[2])
                        else:
                            maxima(t[1], t[2]) if t[0] == "p1" else turned_out(t[1])

                def normalize(g, last):
                    gn = group_no[(a, b, g)]
                    dve.wait_ge(sem("pv"), at("pv", a, b, last))
                    if gn:
                        dve.wait_ge(sem("on"), gn)
                    dve.transpose(turned, sl[2]).then_inc(sem("free2"), 1)
                    emptied(dve, ("o", a, b, g))
                    tv = turned.rearrange("p (q d) -> p q d", d=32)
                    linked(dve.reciprocal(rec[:], tv[:, :, D]))
                    linked(dve.tensor_tensor(tv[:, :, 0:D], tv[:, :, 0:D], rec[:].unsqueeze(2).to_broadcast([P, 32, D]), ALU.mult))
                    if gn:
                        pb = group_key(gn - 1)
                        dve.wait_ge(sem(f"pack{pb[2] % 2}"), at(f"pack{pb[2] % 2}", *pb))
                    if kind == "win":
                        dve.transpose(onorm[:, SHIFT:L], turned[:, 0:L - SHIFT])
                        dve.transpose(onorm[:, 0:SHIFT], turned[:, L - SHIFT:L]).then_inc(sem("on"), mark("on", a, b, g))
                    else:
                        dve.transpose(onorm[:], turned).then_inc(sem("on"), mark("on", a, b, g))

                side(start)
                steps = steps_of(kind)
                per = len(steps) // (H // GH)
                for i, (p, j, kt) in enumerate(steps):
                    side(ahead[i])
                    if i > GH and i % per == 2:
                        normalize(p // 2 - 1, i - 3)
                normalize(H // GH - 1, len(steps) - 1)

            def group_key(n):
                return next(k for k, v in group_no.items() if v == n)

            added = []

            def update(s, b, r, gate):
                src = filled(dve, ("post", s, b, r)).rearrange("p (t c) -> p t c", t=4)
                dve.wait_ge(sem("xb"), at("xb", s, b))
                xs = x[:, b * TB + 4 * r:b * TB + 4 * r + 4, :]
                if gate is None:
                    dve.tensor_tensor(xs, src, xs, ALU.add).then_inc(free(("post", s, b, r)), 1)
                    emptied(dve, ("post", s, b, r))
                    dve.memset(rec[:, 0:1], 0.0).then_inc(sem("xu"), mark("xu", s, b, r))
                else:
                    g = gates[:, gate, b, :].unsqueeze(1).to_broadcast([P, 4, C])
                    tmp = onorm[:].rearrange("p (t c) -> p t c", t=4)
                    if added:
                        dve.wait_ge(sem("xu"), at("xu", *added[-1]))
                    added.append((s, b, r))
                    dve.tensor_tensor(tmp, src, g, ALU.mult).then_inc(free(("post", s, b, r)), 1)
                    emptied(dve, ("post", s, b, r))
                    dve.tensor_tensor(xs, tmp, xs, ALU.add).then_inc(sem("xu"), mark("xu", s, b, r))

            def post(a, b):
                for g in range(2):
                    update(a, b, g, ATT[a]["gate"])

            def mlp(m, b):
                hb = MLP[m]["hb"]
                for r in range(2):
                    if m == "m2":
                        for j in range(8):
                            dve.wait_ge(sem("silu"), at("silu", m, b, r, j))
                            src = filled(dve, ("up", m, b, r, j))
                            dve.scalar_tensor_tensor(out=hid[:, r, j, :], in0=src[:, 512:1024], scalar=cols[:, hb + 8 + j:hb + 9 + j],
                                                     in1=hid[:, r, j, :], op0=ALU.add, op1=ALU.mult).then_inc(free(("up", m, b, r, j)), 1)
                for r in range(2):
                    update(m, b, r, MLP[m]["gate"])

            def prep3():
                filled(dve, ("post", "m2", B - 1, 1))
                src = filled(dve, ("wqt",))
                dve.tensor_copy(wqt, src[:, 0:512].rearrange("p (c n) -> p c n", c=CC)).then_inc(free(("wqt",)), 1)
                for name, dst in (("kt3", kt3), ("vt3", vt3)):
                    src = filled(dve, (name,))
                    dve.tensor_copy(dst.rearrange("p c b s -> p c (b s)"), src.rearrange("p (c n) -> p c n", c=CC)[:, :, 0:B * S]
                                    ).then_inc(free((name,)), 1)
                src = filled(dve, ("g3",))
                dve.tensor_copy(g3.rearrange("p c b s -> p c (b s)"), src.rearrange("p (c n) -> p c n", c=CC)[:, :, 0:B * S]
                                ).then_inc(free(("g3",)), 1)
                for b in range(B):
                    for c in range(CC):
                        i = dve.tensor_copy(condb[:, b, c, :], cols[:, b * CC + c:b * CC + c + 1].to_broadcast([P, P]))
                i.then_inc(sem("condb3"), 1)
                for b in range(B):
                    for g in range(2):
                        src = filled(dve, ("vw", b, g))
                        n = 1024 if g == 0 else VWN - 1024
                        dve.tensor_copy(vw[:, b, g * 1024:g * 1024 + n], src[0:S, 0:n]).then_inc(free(("vw", b, g)), 1)
                src = filled(dve, ("anchor",))
                c0 = COL["L3_xcond_e_b1"]
                dve.tensor_tensor(hb3.rearrange("p b n -> p n b"), src[:, 0:28].rearrange("p (n b) -> p n b", b=B),
                                  cols[:, c0:c0 + 14].unsqueeze(2).to_broadcast([P, 14, B]), ALU.add).then_inc(sem("hb3"), 1)
                dve.tensor_tensor(rb3, src[:, 512:520].rearrange("p (b n) -> p b n", b=B)[:, :, 0:NE],
                                  rbin.unsqueeze(1).to_broadcast([P, B, NE]), ALU.add).then_inc(free(("anchor",)), 1)

            def moe(b):
                src = filled(dve, ("sc3", b))
                linked(dve.tensor_reduce(sm3[:, 0:8], src.rearrange("p (t n) -> p t n", t=TB)[:, :, 0:S], AX.X, ALU.max, negate=True))
                dve.tensor_scalar(bm3, sm3[:, 0:8], 1.0 / 16, None, ALU.mult).then_inc(sem("bm3"), mark("bm3", b))
                emptied(dve, ("sc3", b))
                linked(dve.reciprocal(rs3, sm3[:, 8:16]))
                dve.tensor_tensor(p3, p3, rs3.unsqueeze(2).to_broadcast([P, TB, S]), ALU.mult).then_inc(sem("p3"), mark("p3", b))
                src = filled(dve, ("lg3", b))
                emptied(dve, ("anchor",))
                dve.tensor_tensor(lg3, src[:, 0:32].rearrange("p (t e) -> p t e", t=TB)[:, :, 0:NE],
                                  rb3[:, b, :].unsqueeze(1).to_broadcast([P, TB, NE]), ALU.add).then_inc(free(("lg3", b)), 1)
                emptied(dve, ("lg3", b))
                linked(dve.tensor_reduce(lm3, lg3, AX.X, ALU.max))
                dve.tensor_tensor(lg3, lg3, lm3.unsqueeze(2).to_broadcast([P, TB, NE]), ALU.subtract).then_inc(sem("lgs"), mark("lgs", b))
                dve.wait_ge(sem("lge"), at("lge", b))
                linked(dve.tensor_reduce(ls3, lg3, AX.X, ALU.add))
                linked(dve.reciprocal(ls3, ls3))
                dve.tensor_tensor(lg3, lg3, ls3.unsqueeze(2).to_broadcast([P, TB, NE]), ALU.mult).then_inc(sem("rp3"), mark("rp3", b))
                dve.wait_ge(sem("rp3"), at("rp3", b))
                for r in range(2):
                    for t in range(4):
                        src = filled(dve, ("ex3", b, r, t))
                        acc = xn[:, t, :]
                        linked(dve.tensor_copy(acc, src[:, 768:1024]))
                        for e in range(NE):
                            i = dve.scalar_tensor_tensor(out=acc, in0=src[:, e * C:(e + 1) * C], scalar=lg3[:, 4 * r + t, e:e + 1], in1=acc,
                                                         op0=ALU.mult, op1=ALU.add)
                            if e < NE - 1:
                                linked(i)
                        i.then_inc(free(("ex3", b, r, t)), 1)
                        emptied(dve, ("ex3", b, r, t))
                        dve.memset(rec[:, 0:1], 0.0).then_inc(sem("r3"), mark("r3", b, r, t))
                    dve.wait_ge(sem("ld_b3"), at("ld_b3", "all"))
                    for g in range(2):
                        src = filled(dve, ("y3", b, r, g))
                        linked(dve.tensor_tensor(gz_of(g).rearrange("p (t c) -> p t c", t=2), src[:, 512:1024].rearrange("p (t c) -> p t c", t=2),
                                                 obias[:, 0, :].unsqueeze(1).to_broadcast([P, 2, C]), ALU.add))
                        dve.memset(rec[:, 0:1], 0.0).then_inc(sem("gz"), mark("gz", b, r, g))
                        y = xnf[:, g * 512:(g + 1) * 512]
                        dve.tensor_tensor(y.rearrange("p (t c) -> p t c", t=2), src[:, 0:512].rearrange("p (t c) -> p t c", t=2),
                                          obias[:, 1, :].unsqueeze(1).to_broadcast([P, 2, C]), ALU.add).then_inc(free(("y3", b, r, g)), 1)
                        emptied(dve, ("y3", b, r, g))
                        dve.wait_ge(sem("tanh"), at("tanh", b, r, g))
                        linked(dve.scalar_tensor_tensor(out=y, in0=gz_of(g), scalar=1.0, in1=y, op0=ALU.add, op1=ALU.mult))
                        xs = x[:, b * TB + 4 * r + 2 * g:b * TB + 4 * r + 2 * g + 2, :].rearrange("p t c -> p (t c)")
                        dve.scalar_tensor_tensor(out=xs, in0=y, scalar=0.5, in1=xs, op0=ALU.mult, op1=ALU.add
                                                 ).then_inc(sem("xu"), mark("xu", "moe", b, 2 * r + g))

            run = {"prep": prep, "mods2": mods2, "ckv": ckv, "norm": ln, "turn": lambda i, b: None, "proj": proj, "attn": attn,
                   "post": post, "mlp": mlp, "prep3": prep3, "moe": moe}
            for s in sched:
                run[s[0]](*s[1:])

        @block.gpsimd
        def _(pool):
            def prep():
                pool.memset(identf[:], 0.0).then_inc(sem("ident"), mark("ident", "z"))
                pool.wait_ge(sem("ident"), at("ident", "z"))
                pool.affine_select(out=identf[:], in_=identf[:], compare_op=ALU.not_equal, fill=1.0, base=0,
                                   pattern=[[-1, P]], channel_multiplier=1).then_inc(sem("ident"), mark("ident", "f"))
                pool.wait_ge(sem("ident"), at("ident", "f"))
                pool.tensor_copy(identh[:], identf[:]).then_inc(sem("ident"), mark("ident", "h"))
                pool.wait_ge(sem("ident"), at("ident", "h"))
                pool.wait_ge(sem("mv"), at("mv", "ctx"))
                pool.wait_ge(sem("mhalf"), 1)
                for v, eps in ((0, 1e-5), (1, 1e-6)):
                    pool.tensor_scalar(vare[0:S, 4 * v:4 * v + 2], mv[0:S, 0:2, 1], eps, None, ALU.add).then_inc(sem("vare"), mark("vare", "ctx", v))
                    pool.wait_ge(sem("vare"), at("vare", "ctx", v))
                    i = pool.tensor_tensor(rstd[0:S, 4 * v:4 * v + 2], vare[0:S, 4 * v:4 * v + 2], mhalf[0:S, 0:2], ALU.pow)
                i.then_inc(sem("rstd"), mark("rstd", "ctx"))
                pool.wait_ge(sem("rstd"), at("rstd", "ctx"))
                pool.memset(ks[:].rearrange("p a b -> p (a b)").bitcast(U32), 0).then_inc(sem("kzero"), mark("kzero", 0))
                pool.wait_ge(sem("kzero"), at("kzero", 0))
                pool.memset(vsf, 1.0).then_inc(sem("vones"), 1)
                pool.wait_ge(sem("vones"), 1)
                pool.wait_ge(sem("kzero"), at("kzero", 0))
                kv = ks[:].rearrange("p (a two) n -> p a two n", two=2)
                pool.memset(kv[ROWM:ROWM + 1, :, 0, :], 1.0)
                pool.memset(kv[64 + ROWM:64 + ROWM + 1, :, 1, :], 1.0).then_inc(sem("kzero"), mark("kzero", 1))
                pool.wait_ge(sem("kzero"), at("kzero", 1))

            def ln(i, b):
                pool.wait_ge(sem("mv"), at("mv", i, b))
                pool.tensor_scalar(vare[:], mv[:, :, 1], LN_EPS[i], None, ALU.add).then_inc(sem("vare"), mark("vare", i, b))
                pool.wait_ge(sem("vare"), at("vare", i, b))
                pool.tensor_tensor(rstd[:], vare[:], mhalf[:], ALU.pow).then_inc(sem("rstd"), mark("rstd", i, b))
                pool.wait_ge(sem("rstd"), at("rstd", i, b))
                if i == 7:
                    return
                s = ["x0", "s1", "x1", "m1", "w2", "t2", "m2"][i]
                d = ATT.get(s) or MLP[s]
                row = obias[:, d.get("half", 2), :]
                pool.wait_ge(sem("ld_" + s), at("ld_" + s, "all"))
                if d["gate"] is not None:
                    emptied(pool, ("gate", d["gate"]))
                    pool.tensor_tensor(gbias[:], row, gates[:, d["gate"], b, :], ALU.mult).then_inc(sem("gbias"), mark("gbias", s, b))
                    pool.wait_ge(sem("gbias"), at("gbias", s, b))
                    row = gbias[:]
                pool.wait_ge(sem("xn"), at("xn", i, b, TB - 1))
                xs = x[:, b * TB:(b + 1) * TB, :]
                pool.tensor_tensor(xs, xs, row.unsqueeze(1).to_broadcast([P, TB, C]), ALU.add).then_inc(sem("xb"), mark("xb", s, b))
                pool.wait_ge(sem("xb"), at("xb", s, b))

            def proj(a, b):
                prev = call_before(a, b)
                if prev:
                    filled(pool, last_reader(*prev, HP - 1))
                else:
                    pool.wait_ge(sem("qzero"), 1)
                v = qs[:].rearrange("p a b -> p (a b)").bitcast(U32)
                pool.memset(v[ROWM:ROWM + 1, :], 0)
                pool.memset(v[64 + ROWM:64 + ROWM + 1, :], 0).then_inc(sem("mzero"), mark("mzero", a, b))
                pool.wait_ge(sem("mzero"), at("mzero", a, b))

            def attn_top(a, b):
                start, ahead = side_plan("top")
                for tasks in [start] + ahead:
                    for _, p, u in tasks:
                        n = 2 * p + u
                        emptied(pool, ("p1", a, b, p, 2 * u))
                        emptied(pool, ("p1", a, b, p, 2 * u + 1))
                        pool.wait_ge(sem("topm"), at("topm", a, b, p, u))
                        if n >= 4:
                            filled(pool, ("s", a, b, 2 * ((n - 4) // 2) + 1))
                        elif b:
                            filled(pool, ("s", a, b - 1, 2 * ((n + 12) // 2) + 1))
                        else:
                            filled(pool, last_reader(*call_before(a, b), HP - 1))
                            pool.wait_ge(sem("pv"), at("pv", *call_before(a, b), len(steps_of("win")) - 1))
                        pool.tensor_tensor(top_p[n % 4].rearrange("p (r s) -> p r s", r=8), top_s[n % 2].rearrange("p (r s) -> p r s", r=8),
                                           v8[:, 0, :, 0:1].to_broadcast([P, 8, S]), ALU.subtract).then_inc(sem("topd"), mark("topd", a, b, p, u))
                        pool.wait_ge(sem("topd"), at("topd", a, b, p, u))

            for s in sched:
                if s[0] == "prep":
                    prep()
                elif s[0] == "norm":
                    ln(*s[1:])
                elif s[0] == "proj":
                    proj(*s[1:])
                elif s[0] == "attn" and ATT[s[1]]["kind"] == "top":
                    attn_top(*s[1:])

        @block.sync
        def _(sp):
            def rows(ap, n):
                return ap.rearrange("(c p) n -> p c n", p=P)

            def bc(ap):
                return ap.rearrange("(o n) -> o n", o=1).to_broadcast([P, ap.shape[0]])

            def load_att(a):
                d = ATT[a]
                for v, w in zip(wviews(a), d["w"]):
                    sp.dma_start(v, rows(ins[w], 0)).then_inc(sem("ld_" + a), mark("ld_" + a, "w", by=16))
                name, lo = d["vb"]
                sp.dma_start(vbias[:, d["half"], :], bc(ins[name][lo:lo + C])).then_inc(sem("ld_" + a), mark("ld_" + a, "w", by=16))
                sp.dma_start(obias[:, d["half"], :], bc(ins[d["ob"]])).then_inc(sem("ld_" + a), mark("ld_" + a, "all", by=16))

            def load_mlp(m):
                up, down = mlp_views(m)
                d = MLP[m]
                sp.dma_start(up, rows(ins[d["w"][0]], 0)).then_inc(sem("ld_" + m), mark("ld_" + m, "w", by=16))
                sp.dma_start(down, rows(ins[d["w"][1]], 0)).then_inc(sem("ld_" + m), mark("ld_" + m, "w", by=16))
                sp.dma_start(obias[:, 2, :], bc(ins[d["ob"]])).then_inc(sem("ld_" + m), mark("ld_" + m, "all", by=16))

            def load_gates(layer):
                name = {1: "L1_xcond_b_mod", 2: "L2_xcond_b_ada"}[layer]
                for g, (ly, i) in enumerate(GATES):
                    if ly == layer:
                        for b in range(B):
                            sp.dma_start(gates[:, g, b, :], bc(ins[name][i * C:(i + 1) * C])
                                         ).then_inc(sem(f"ld_g{layer}"), mark(f"ld_g{layer}", "all", by=16))

            def prep():
                n = 0
                for name, lo, k in COLUMN_ROWS:
                    src = ins[name]
                    if len(src.shape) == 2:
                        src = src.rearrange("a n -> (a n)")
                    src = src[lo:lo + k * P].rearrange("(k p) -> k p", p=P)
                    sp.dma_start(crow[n:n + k, :], src).then_inc(sem("ld_cols"), mark("ld_cols", "all", by=16))
                    n += k
                sp.dma_start(cx, ins["ctx_1024"].rearrange("b s c -> s b c")).then_inc(sem("ld_ctx"), 16)
                for w in ("ssq", "sskv"):
                    sp.dma_start(mod_w[w], rows(ins[mod_in[w]], 0)).then_inc(sem("ld_ss"), 16)
                sp.dma_start(mod_w["mod1"], rows(ins[mod_in["mod1"]], 0)).then_inc(sem("ld_mod1"), 16)
                load_att("x0")
                load_gates(1)
                load_gates(2)
                if "s1" in [s[1] for s in sched if s[0] == "attn"]:
                    load_att("s1")
                    filled(sp, ("gate", 1))
                    sp.dma_start(mod_w["ada2"], rows(ins[mod_in["ada2"]], 0)).then_inc(sem("ld_ada2"), 16)

            def stack(t, a, b, m, n):
                j = split_no[(a, t, b, m)]
                emptied(sp, (t, a, b, m))
                sp.dma_start(scratch[j, :, :, 0:n].rearrange("s p n -> p s n"), st[:, j % 2, :, 0:n]
                             ).then_inc(sem(f"stout{j % 2}"), mark(f"stout{j % 2}", j, by=16))
                sp.wait_ge(sem(f"stout{j % 2}"), at(f"stout{j % 2}", j))
                prev = call_before(a, b if b != "c" else 0)
                if prev:
                    filled(sp, last_reader(*prev, 4 * m + 3))
                elif t == "q":
                    sp.wait_ge(sem("qzero"), 1)
                if t == "k":
                    sp.wait_ge(sem("kzero"), at("kzero", 1))
                name = f"{t}in{m}"
                for r, half in ((0, 0), (D, 1 if t == "q" else 0), (ROWM + 1, 0 if t == "q" else 1)):
                    for par in range(2):
                        src = scratch[j, half, :, 0:n].rearrange("(a two d) n -> two d a n", two=2, d=D)[par]
                        lo = 64 * par + r
                        if t == "q":
                            dst = qs[lo:lo + D, 4 * m:4 * m + 4, 0:n]
                        else:
                            dst = ks[:].rearrange("p (a two) n -> p a two n", two=2)[lo:lo + D, 4 * m:4 * m + 4, par, 0:n]
                        sp.dma_start(dst, src).then_inc(sem(name), mark(name, a, b, by=16))

            def ckv(a):
                for m in range(CC):
                    stack("k", a, "c", m, B * S)

            def proj(a, b):
                for t, m in split_order(a):
                    stack(t, a, b, m, L)

            def attn(a, b):
                kind = ATT[a]["kind"]
                start, ahead = side_plan(kind)

                def side(tasks):
                    for t in tasks:
                        if t[0] == "t":
                            p = t[1]
                            emptied(sp, ("t", a, b, p))
                            for j in range(2):
                                sp.dma_start(qs[64 * j + ROWM:64 * j + ROWM + 1, p, :].rearrange("o (t n) -> o t n", t=TB),
                                             mt[TB * j:TB * (j + 1), p % 2, :]
                                             ).then_inc(sem(f"mrow{p % 2}"), mark(f"mrow{p % 2}", a, b, p, by=16))

                def pack(g):
                    sp.wait_ge(sem("on"), at("on", a, b, g))
                    for j in range(GH):
                        h = g * GH + j
                        sp.dma_start(ht[D * (h % 8):D * (h % 8) + D, b, h // 8, :], onorm[32 * j:32 * j + D, :]
                                     ).then_inc(sem(f"pack{g % 2}"), mark(f"pack{g % 2}", a, b, g, by=16))

                side(start)
                steps = steps_of(kind)
                per = len(steps) // (H // GH)
                for i, (p, j, kt) in enumerate(steps):
                    side(ahead[i])
                    if i > GH and i % per == 2:
                        pack(p // 2 - 1)
                pack(H // GH - 1)

            names = [s[1] for s in sched if s[0] == "attn"] + [s[1] for s in sched if s[0] == "mlp"]

            def post(a, b):
                if b < B - 1:
                    return
                nxt = {"x0": "x1", "s1": "w2", "x1": "t2"}.get(a)
                if nxt in names:
                    filled(sp, ("post", a, b, 1))
                    sp.wait_ge(sem("xb"), at("xb", a, b))
                    load_att(nxt)
                if a == "t2" and "prep3" in stages:
                    load_l3()

            def mods2():
                if "m1" in names:
                    filled(sp, ("gate", 4))
                    load_mlp("m1")

            def mlp(m, b):
                if m == "m1" and b == B - 1 and "m2" in names:
                    filled(sp, ("post", m, b, 1))
                    sp.wait_ge(sem("xb"), at("xb", m, b))
                    load_mlp("m2")
                if m == "m2" and b == B - 1 and "prep3" in stages:
                    filled(sp, ("post", m, b, 1))
                    sp.wait_ge(sem("xb"), at("xb", m, b))
                    load_l3b()

            def ld3(dst, src):
                sp.dma_start(dst, src).then_inc(sem("ld_l3"), mark("ld_l3", "all", by=16))

            def load_l3():
                filled(sp, ("post", "t2", B - 1, 1))
                for part, r0 in (("nx", 0), ("ev", C), ("an", 2 * C)):
                    for e in range(NE):
                        ld3(w3[part][:, :, e * RH:(e + 1) * RH], rows(ins["L3_xcond_e_w1"][e, r0:r0 + C, :], 0))
                    ld3(w3[part][:, :, NE * RH:NX], rows(ins["L3_xcond_gate_w1"][r0:r0 + C, :], 0))
                ld3(w3["w2"], ins["L3_xcond_e_w2"].rearrange("e (k p) n -> p (e k) n", p=P))
                ld3(w3["g2"], rows(ins["L3_xcond_gate_w2"], 0))
                ld3(w3q, rows(ins["L3_xcond_Wq"], 0))
                ld3(w3k, rows(ins["L3_xcond_Wk"], 0))
                ld3(w3v, rows(ins["L3_xcond_Wv"], 0))
                ld3(wr, rows(ins["L3_xcond_router_W"], 0))
                for i, name in enumerate(("L3_xcond_gate_b2", "L3_xcond_out_b")):
                    sp.dma_start(obias[:, i, :], bc(ins[name])).then_inc(sem("ld_b3"), mark("ld_b3", "all", by=16))

            def load_l3b():
                ld3(w3["ow"], rows(ins["L3_xcond_out_w"], 0))
                ld3(rbin, bc(ins["L3_xcond_router_b"]))
                ld3(b2e, ins["L3_xcond_e_b2"])

            out_v = out.rearrange("b (t p) c -> p (b t) c", p=P)

            def moe(b):
                for q in range(4):
                    sp.wait_ge(sem("xu"), at("xu", "moe", b, q))
                    lo = b * TB + 2 * q
                    sp.dma_start(out_v[:, lo:lo + 2, :], x[:, lo:lo + 2, :]).then_inc(sem("stored"), mark("stored", "all", by=16))

            run = {"prep": prep, "mods2": mods2, "ckv": ckv, "norm": lambda i, b: None, "turn": lambda i, b: None,
                   "proj": proj, "attn": attn, "post": post, "mlp": mlp, "prep3": lambda: None, "moe": moe}
            for s in sched:
                run[s[0]](*s[1:])
            if "moe" not in stages:
                last = next(s for s in reversed(sched) if s[0] in ("attn", "mlp"))
                for b in range(B):
                    for r in range(2):
                        sp.wait_ge(sem("xu"), at("xu", last[1], b, r))
                sp.dma_start(out_v, x[:]).then_inc(sem("stored"), mark("stored", "all", by=16))
            sp.wait_ge(sem("stored"), at("stored", "all"))
    return seen


_INS = ['x', 'ctx_1024', 'cond_1024',
        'L0_xcond_Wq', 'L0_xcond_bq', 'L0_xcond_Wkv', 'L0_xcond_bkv', 'L0_xcond_Wp', 'L0_xcond_bp',
        'L0_xcond_Wss_q', 'L0_xcond_bss_q', 'L0_xcond_Wss_kv', 'L0_xcond_bss_kv',
        'L1_xcond_W_mod', 'L1_xcond_b_mod', 'L1_xcond_W_qkv', 'L1_xcond_b_qkv', 'L1_xcond_W_proj', 'L1_xcond_b_proj',
        'L1_xcond_W_qc', 'L1_xcond_b_qc', 'L1_xcond_W_kvc', 'L1_xcond_b_kvc', 'L1_xcond_W_cproj', 'L1_xcond_b_cproj',
        'L1_xcond_W_mlp1', 'L1_xcond_b_mlp1', 'L1_xcond_W_mlp2', 'L1_xcond_b_mlp2',
        'L2_xcond_w_ada', 'L2_xcond_b_ada', 'L2_xcond_w_qkv', 'L2_xcond_b_qkv', 'L2_xcond_w_so', 'L2_xcond_b_so',
        'L2_xcond_w_q', 'L2_xcond_b_q', 'L2_xcond_w_kv', 'L2_xcond_b_kv', 'L2_xcond_w_co', 'L2_xcond_b_co',
        'L2_xcond_w_m1', 'L2_xcond_b_m1', 'L2_xcond_w_m2', 'L2_xcond_b_m2',
        'L3_xcond_ln_gamma', 'L3_xcond_ln_beta', 'L3_xcond_Wq', 'L3_xcond_Wk', 'L3_xcond_Wv',
        'L3_xcond_router_W', 'L3_xcond_router_b', 'L3_xcond_e_w1', 'L3_xcond_e_b1', 'L3_xcond_e_w2', 'L3_xcond_e_b2',
        'L3_xcond_gate_w1', 'L3_xcond_gate_b1', 'L3_xcond_gate_w2', 'L3_xcond_gate_b2', 'L3_xcond_out_w', 'L3_xcond_out_b']


def kernel(_stop=None, **inputs):
    import numpy as _np
    import concourse.bacc as _bacc
    from concourse.bass_utils import run_bass_kernel_spmd as _run

    marks = None
    for _ in range(2):
        nc = _bacc.Bacc("TRN2", target_bir_lowering=False, num_devices=1)
        arrays, aps = {}, {}
        for name in _INS:
            a = _np.ascontiguousarray(inputs[name])
            arrays[f"in_{name}_dram"] = a
            aps[name] = nc.dram_tensor(f"in_{name}_dram", a.shape, mybir.dt.from_np(a.dtype), kind="ExternalInput").ap()
        out = nc.dram_tensor("out_0_dram", (B, L, C), F32, kind="ExternalOutput").ap()
        marks = build(nc, aps, out, marks, _stop)
    r = _run(nc, [arrays], core_ids=[0])
    return r.results[0]["out_0_dram"]
```

```python
from contextlib import ExitStack

import concourse.bass as bass
from concourse import mybir

P = 128
ALU = mybir.AluOpType
ACT = mybir.ActivationFunctionType
AX = mybir.AxisListType
F32 = mybir.dt.float32
F16 = mybir.dt.float16
U32 = mybir.dt.uint32

B, L, C = 2, 1024, 256
TB = L // P
CC = C // P
H, D = 16, 16
S = 77
HP = H // 2
GH = 4
MP = 4
RP = 7
SCALE = 0.25
TOPK_GONE = -3.0e38
SHIFT = 64
N1, N2, NE = 8, 8, 3
RH = 2 * C
SLOT = 1024
ROWM = 32

COLUMN_ROWS = [
    ("cond_1024", 0, 4),
    ("L0_xcond_bq", 0, 2), ("L0_xcond_bkv", 0, 2), ("L0_xcond_bss_q", 0, 4), ("L0_xcond_bss_kv", 0, 4),
    ("L1_xcond_b_mod", 0, 12), ("L1_xcond_b_qkv", 0, 4), ("L1_xcond_b_qc", 0, 2), ("L1_xcond_b_kvc", 0, 2),
    ("L1_xcond_b_mlp1", 0, 8),
    ("L2_xcond_b_ada", 0, 18), ("L2_xcond_b_qkv", 0, 4), ("L2_xcond_b_q", 0, 2), ("L2_xcond_b_kv", 0, 2),
    ("L2_xcond_b_m1", 0, 16),
    ("L3_xcond_ln_gamma", 0, 2), ("L3_xcond_ln_beta", 0, 2), ("L3_xcond_e_b1", 0, 12), ("L3_xcond_gate_b1", 0, 2),
]
COL = {}
NCOL = 0
for _name, _, _n in COLUMN_ROWS:
    COL[_name] = NCOL
    NCOL += _n

ATT = {
    "x0": dict(kind="cross", half=0, w=["L0_xcond_Wq", "L0_xcond_Wkv", "L0_xcond_Wp"], n=[256, 512, 256],
               vb=("L0_xcond_bkv", 256), ob="L0_xcond_bp", qb=COL["L0_xcond_bq"], kb=COL["L0_xcond_bkv"], ln=0, gate=None),
    "s1": dict(kind="self", half=1, w=["L1_xcond_W_qkv", "L1_xcond_W_proj"], n=[768, 256],
               vb=("L1_xcond_b_qkv", 512), ob="L1_xcond_b_proj", qb=COL["L1_xcond_b_qkv"], kb=COL["L1_xcond_b_qkv"] + 2, ln=1, gate=0),
    "x1": dict(kind="cross", half=0, w=["L1_xcond_W_qc", "L1_xcond_W_kvc", "L1_xcond_W_cproj"], n=[256, 512, 256],
               vb=("L1_xcond_b_kvc", 256), ob="L1_xcond_b_cproj", qb=COL["L1_xcond_b_qc"], kb=COL["L1_xcond_b_kvc"], ln=2, gate=None),
    "w2": dict(kind="win", half=1, w=["L2_xcond_w_qkv", "L2_xcond_w_so"], n=[768, 256],
               vb=("L2_xcond_b_qkv", 512), ob="L2_xcond_b_so", qb=COL["L2_xcond_b_qkv"], kb=COL["L2_xcond_b_qkv"] + 2, ln=4, gate=2),
    "t2": dict(kind="top", half=0, w=["L2_xcond_w_q", "L2_xcond_w_kv", "L2_xcond_w_co"], n=[256, 512, 256],
               vb=("L2_xcond_b_kv", 256), ob="L2_xcond_b_co", qb=COL["L2_xcond_b_q"], kb=COL["L2_xcond_b_kv"], ln=5, gate=3),
}
ATT_ORDER = ["x0", "s1", "x1", "w2", "t2"]
MLP = {
    "m1": dict(ln=3, gate=1, w=["L1_xcond_W_mlp1", "L1_xcond_W_mlp2"], n=[1024, 256], ob="L1_xcond_b_mlp2", hb=COL["L1_xcond_b_mlp1"]),
    "m2": dict(ln=6, gate=4, w=["L2_xcond_w_m1", "L2_xcond_w_m2"], n=[2048, 256], ob="L2_xcond_b_m2", hb=COL["L2_xcond_b_m1"]),
}
LN_EPS = [1e-5, 1e-6, 1e-6, 1e-6, 1e-6, 1e-6, 1e-6, 1e-5]
GATES = [(1, 2), (1, 5), (2, 2), (2, 5), (2, 8)]
MODS = ([("ssq", i, i < 2) for i in range(4)] + [("sskv", i, i < 2) for i in range(4)]
        + [("mod1", i, i in (2, 3, 8, 9)) for i in (0, 1, 2, 3, 6, 7, 8, 9)]
        + [("ada2", i, i in (2, 3, 8, 9, 14, 15)) for i in (0, 1, 2, 3, 6, 7, 8, 9, 12, 13, 14, 15)])
MOD_AT = {(w, i): n for n, (w, i, _) in enumerate(MODS)}
MOD_COL = {"ssq": COL["L0_xcond_bss_q"], "sskv": COL["L0_xcond_bss_kv"], "mod1": COL["L1_xcond_b_mod"], "ada2": COL["L2_xcond_b_ada"]}
LN_MOD = {0: ("ssq", 0, 2), 1: ("mod1", 2, 0), 3: ("mod1", 8, 6), 4: ("ada2", 2, 0), 5: ("ada2", 8, 6), 6: ("ada2", 14, 12)}


def schedule(stop):
    calls = []
    for name in ("x0", "s1", "x1", "m1", "w2", "t2", "m2", "moe"):
        calls += [(name, b) for b in range(B)]
        if name == stop:
            break
    ln = {name: d["ln"] for name, d in (*ATT.items(), *MLP.items())}
    ln["moe"] = 7
    out = [("prep",)]

    def norm(n, stage):
        if n < len(calls):
            out.append((stage, ln[calls[n][0]], calls[n][1]))

    def proj(n):
        if n < len(calls) and calls[n][0] in ATT:
            name, b = calls[n]
            if b == 0 and ATT[name]["kind"] in ("cross", "top"):
                out.append(("ckv", name))
            out.append(("proj", name, b))

    def body(n):
        name, b = calls[n]
        if name == "moe":
            parts = [(b_, r) for b_ in range(B) for r in range(2)] if b == 0 else []
            for i, (b_, r) in enumerate(parts):
                out.extend(("hidden3", b_, r, j) for j in range(4 if i else 0, 7))
                if r == 0:
                    out.append(("probs3", b_))
                out.append(("experts3", b_, r))
                for stage, js in (("routed3", (0, 1)), ("gated3", (2, 3))):
                    if i + 1 < len(parts):
                        out.extend(("hidden3", *parts[i + 1], j) for j in js)
                    out.append((stage, b_, r))
            return
        if name in ATT:
            out.append(("attn", name, b))
        else:
            out.append(("up", name, b))
            norm(n + 1, "turn")
            out.append(("down", name, b))

    norm(0, "norm")
    out.append(("mods", 0))
    norm(0, "turn")
    proj(0)
    if len(calls) > B:
        out.append(("mods", 1))
    norm(1, "norm")
    body(0)
    norm(1, "turn")
    for n in range(len(calls)):
        nxt = calls[n + 1] if n + 1 < len(calls) else None
        proj(n + 1)
        if calls[n][0] in ATT:
            out.append(("post", *calls[n]))
        if calls[n] == ("x0", B - 1) and len(calls) > B:
            out.append(("mods", 2))
        norm(n + 2, "norm")
        if nxt == ("moe", 0):
            out.append(("prep3", "keys"))
        first = nxt and nxt[0] == "moe"
        if first:
            norm(n + 2, "turn")
        if nxt == ("moe", 0):
            out.extend([("scores3", b) for b in range(B)] + [("prep3", "values")]
                       + [("evidence", b) for b in range(B)] + [("router", b) for b in range(B)])
        if nxt:
            body(n + 1)
        if nxt and not first and nxt[0] not in MLP:
            norm(n + 2, "turn")
    return out


def split_order(a):
    return [(t, m) for m in range(CC) for t in (("q", "k") if ATT[a]["kind"] in ("self", "win") else ("q",))]


def steps_of(kind):
    n = TB if kind == "self" else 1
    return [(2 * g + r // 2, r % 2, k) for g in range(H // GH) for k in range(n) for r in range(GH)]


def first_pass_units(kind):
    if kind == "self":
        return [(j, t, n) for j in range(2) for t in range(TB) for n in range(2)]
    return list(range(2 if kind == "top" else 4))


def side_plan(kind):
    units, per = first_pass_units(kind), len(steps_of(kind)) // (H // GH)
    ahead = [[] for _ in range(per * (H // GH))]
    start = []
    for p in range(HP):
        tasks = [("p1", p, u) for u in range(len(units))]
        turn = [] if kind == "top" else [("t", p)]
        if p < (2 if kind in ("self", "top") else 4):
            start += ([("wide", p, u) for u in range(2 * TB)] if kind == "self" else tasks) + turn
            continue
        base, odd = (p // 2 - 1) * per, p % 2
        if kind == "self":
            for i, t in enumerate(tasks):
                ahead[base + (odd * len(tasks) + i) * (per - 4) // (2 * len(tasks))].append(t)
            ahead[base + (per - 3 if odd else per // 2)] += turn
        elif kind == "top":
            for i, t in enumerate(tasks):
                ahead[base + 2 * odd + i].append(t)
        else:
            for i, t in enumerate(tasks):
                ahead[base - per + 2 * odd + i // 2].append(t)
            ahead[base - per + 2 * odd + 2][0:0] = turn
    return start, ahead


def build(nc, ins, out, marks, stop=None):
    final = marks is not None
    marks = marks or {}
    seen, count, ring, half = {}, {}, [0], [0]
    sched = schedule(stop)
    stages = [s[0] for s in sched]

    with ExitStack() as ctx:
        sems = {}

        def sem(name):
            if name not in sems:
                sems[name] = ctx.enter_context(nc.semaphore(name))
            return sems[name]

        def mark(name, *key, by=1):
            count[name] = count.get(name, 0) + by
            seen[(name, *key)] = count[name]
            return by

        def at(name, *key):
            return marks[(name, *key)] if final else 1

        def sb(name, shape, dt):
            return ctx.enter_context(nc.sbuf_tensor(name, shape, dt))

        x = sb("x", [P, B * TB, C], F32)
        ht = sb("ht", [P, B, CC, L], F32)
        qs = sb("qs", [P, HP, L], F16)
        ks = sb("ks", [P, H, L], F16)
        vs = sb("vs", [P, TB, H, 32], F32)
        xn = sb("xn", [P, TB, C], F32)
        onorm = sb("onorm", [P, L], F32)
        area = sb("area", [P, 8192], F32)
        wa = sb("wa", [P, 2, 2048], F32)
        wm = sb("wm", [P, 6144], F32)
        gates = sb("gates", [P, len(GATES), B, C], F32)
        vbias = sb("vbias", [P, 2, C], F32)
        obias = sb("obias", [P, 3, C], F32)
        gbias = sb("gbias", [P, C], F32)
        ct = sb("ct", [P, 3, CC, B, S], F32)
        identf = sb("identf", [P, P], F32)
        identh = sb("identh", [P, P], F16)
        cols = sb("cols", [P, 128], F32)
        silc = sb("silc", [P, 4], F32)
        modc = sb("modc", [P, len(MODS), B], F32)
        stats = sb("stats", [P, TB, 6], F32)
        mv = sb("mv", [P, TB, 2], F32)
        vare = sb("vare", [P, TB], F32)
        rstd = sb("rstd", [P, TB], F32)
        mhalf = sb("mhalf", [P, TB], F32)
        m16 = sb("m16", [P, MP, 2, TB], F16)
        mhalves = sb("mhalves", [P, 2, 2, 2, TB], F16)
        mt = sb("mt", [2 * TB, MP, P], F16)
        rec = sb("rec", [P, 32], F32)
        stage = sb("stage", [P, 2, 512], F32)
        wr = sb("wr", [P, 6, NE], F32)
        wrs = sb("wrs", [P, 2, CC, NE], F16)
        router_s = sb("router_s", [P, B, 72], F32)

        hts = ht[:].rearrange("p b c n -> p (b c n)").bitcast(F16).rearrange("p (b s c n) -> p b s c n", b=B, s=2, c=CC)
        tmp32 = area[:, 2048:4096].rearrange("p (c n) -> p c n", c=CC)
        hid32 = onorm[:].rearrange("p (r n) -> p r n", r=2)
        st = area[:, 0:2048].bitcast(F16).rearrange("p (r s n) -> p r s n", r=2, s=2)
        pr = area[:, 0:RP * L].rearrange("p (r n) -> p r n", r=RP)
        turned = area[:, 7168:8192]
        hid = area[:, :].bitcast(F16).rearrange("p (r s k n) -> p r s k n", r=2, s=2, k=8)
        cx = area[0:S, 4096:4608].rearrange("p (b c) -> p b c", b=B)
        cxn = area[0:S, 4608:5632].rearrange("p (v b c) -> p v b c", v=2, b=B)
        crow = area[:, 5632:5760]
        condb = area[:, 7168:7680].rearrange("p (b c n) -> p b c n", b=B, c=CC)
        xnf = xn[:].rearrange("p a b -> p (a b)")
        US = 8 * S
        vsf = vs[:].rearrange("p a b c -> p (a b c)")
        top_p = [vsf[:, 1024 + i * US:1024 + (i + 1) * US] for i in range(4)]
        ks_rest = ks[:].rearrange("p a b -> p (a b)").bitcast(F32).rearrange("p (a n) -> p a n", a=H)[:, :, 128:128 + US // 2]
        top_s = [ks_rest[:, 2 * i:2 * i + 2, :] for i in range(2)]
        top_w = [ks_rest[:, 4 + 2 * i:6 + 2 * i, :] for i in range(2)]
        v8 = ks_rest[:, 8, 0:192].rearrange("p (a r n) -> p a r n", a=3, r=8)
        ksf = ks[:].rearrange("p a b -> p (a b)").bitcast(F32)
        qsf = qs[:].rearrange("p a b -> p (a b)").bitcast(F32)
        waf = wa[:].rearrange("p a b -> p (a b)")

        psum = ctx.enter_context(nc.psum_tensor("psum", [P, 4, SLOT], F32))
        sl = [psum[:, k, :] for k in range(4)] + [psum[:, 3, 512:1024]]

        n_split = sum(2 * (1 + (ATT[s[1]]["kind"] in ("self", "win"))) if s[0] == "proj" else 2
                      for s in sched if s[0] in ("proj", "ckv"))
        scratch = nc.dram_tensor("scratch", [n_split, 2, P, L], F16, kind="Internal").ap()
        split_no = {}
        for s in sched:
            if s[0] == "ckv":
                for m in range(CC):
                    split_no[(s[1], "k", "c", m)] = len(split_no)
            if s[0] == "proj":
                for t, m in split_order(s[1]):
                    split_no[(s[1], t, s[2], m)] = len(split_no)
        relaxed = [s for s, following in zip(sched, sched[1:]) if s[0] == "norm" and following[0] == "attn" and following[1] != "t2"]

        def xn_sem(i, b):
            return "xn_pool" if ("norm", i, b) in relaxed else "xn_dve"

        ln_calls = [("ln", *s[1:]) for s in sched if s[0] == "turn"]
        calls = [(s[1], s[2]) for s in sched if s[0] == "attn"]
        step_no, group_no = {}, {}
        for a, b in calls:
            for i in range(len(steps_of(ATT[a]["kind"]))):
                step_no[(a, b, i)] = len(step_no)
            for g in range(H // GH):
                group_no[(a, b, g)] = len(group_no)

        def open_slot(pe, key, k=None, signals=True):
            if k is None:
                k = ring[0]
                ring[0] = (ring[0] + 1) % 4
                if k == 3:
                    if seen.get(("opened", 4), 0):
                        pe.wait_ge(sem("free4"), seen[("opened", 4)])
                    seen["whole"] = seen.get(("opened", 3), 0) + 1
            elif k == "half":
                k = 3 + half[0]
                half[0] = 1 - half[0]
                if k == 4 and "whole" in seen:
                    pe.wait_ge(sem("free3"), seen.pop("whole"))
            n = seen.get(("opened", k), 0)
            if n:
                pe.wait_ge(sem(f"free{k}"), n)
            seen[("opened", k)] = n + 1
            seen[("filled", k)] = seen.get(("filled", k), 0) + signals
            seen[("slot", key)] = (k, seen[("filled", k)], n + 1)
            return k

        def where(key):
            return marks[("slot", key)] if final else (0, 1, 1)

        def filled(eng, key):
            k, n, _ = where(key)
            eng.wait_ge(sem(f"full{k}"), n)
            return sl[k]

        def emptied(eng, key):
            k, _, n = where(key)
            eng.wait_ge(sem(f"free{k}"), n)

        def free(key):
            return sem(f"free{where(key)[0]}")

        def tmp32_of(i, b, c):
            return onorm[:] if sched[sched.index(("turn", i, b)) - 1][0] == "up" else tmp32[:, c, :]

        hidden_order = [(m, b, r, ch) for m, n in (("m1", 8), ("m2", 8), ("moe", 14)) for b in range(B) for r in range(2) for ch in range(n)]

        def low_two_before(*key):
            return hidden_order[hidden_order.index(key) - 2]

        def update_before(m, b):
            return (m, b - 1, 1) if b else ({"m1": "x1", "m2": "t2"}[m], B - 1, 1)

        def attention_before(m):
            return {"m1": ("x1", B - 1), "m2": ("t2", B - 1)}[m]

        def stack_in(eng, t, a, b, m, n):
            j = split_no[(a, t, b, m)]
            eng.wait_ge(sem(f"stout{j % 2}"), at(f"stout{j % 2}", j))
            prev = call_before(a, b if b != "c" else 0)
            if prev:
                filled(eng, last_reader(*prev, 4 * m + 3))
            elif t == "q":
                eng.wait_ge(sem("qzero"), 1)
            if t == "k":
                eng.wait_ge(sem("kzero"), at("kzero", 1))
            name = f"{t}in{m}"
            for r, half_ in ((0, 0), (D, 1 if t == "q" else 0), (ROWM + 1, 0 if t == "q" else 1)):
                for par in range(2):
                    src = scratch[j, half_, :, 0:n].rearrange("(a two d) n -> two d a n", two=2, d=D)[par]
                    lo = 64 * par + r
                    if t == "q":
                        dst = qs[lo:lo + D, 4 * m:4 * m + 4, 0:n]
                    else:
                        dst = ks[:].rearrange("p (a two) n -> p a two n", two=2)[lo:lo + D, 4 * m:4 * m + 4, par, 0:n]
                    eng.dma_start(dst, src).then_inc(sem(name), mark(name, a, b, by=16))

        def call_before(a, b):
            i = calls.index((a, b))
            return calls[i - 1] if i else None

        def last_reader(a, b, p):
            kind = ATT[a]["kind"]
            if kind == "top":
                return ("p1", a, b, p, 3)
            return ("s", a, b, max(i for i, step in enumerate(steps_of(kind)) if step[0] == p))

        def halves(flat, n):
            return flat.bitcast(F16).rearrange("p (s c n) -> p s c n", s=2, n=n)

        def att_views(a):
            n = 768 if ATT[a]["kind"] in ("self", "win") else 256
            w = wa[:, ATT[a]["half"], :]
            other = w[:, CC * n:2048 - CC * C].rearrange("p (c n) -> p c n", c=CC) if n == 256 else None
            return halves(w[:, 0:CC * n], n), other, w[:, 2048 - CC * C:2048].rearrange("p (c n) -> p c n", c=CC)

        mod_w = {
            "ssq": wm[:, 0:1024].rearrange("p (c n) -> p c n", c=CC),
            "sskv": wm[:, 1024:2048].rearrange("p (c n) -> p c n", c=CC),
            "mod1": wm[:, 2048:5120].rearrange("p (c n) -> p c n", c=CC),
            "ada2": wm[:, 0:4608].rearrange("p (c n) -> p c n", c=CC),
        }
        mod_in = {"ssq": "L0_xcond_Wss_q", "sskv": "L0_xcond_Wss_kv", "mod1": "L1_xcond_W_mod", "ada2": "L2_xcond_w_ada"}

        def mlp_views(m):
            n = MLP[m]["n"][0]
            return halves(wm[:, 0:CC * n], n), halves(wm[:, CC * n:CC * n + 8 * C], C)

        NX = NE * RH + C
        w3 = {
            "nx": halves(ksf[:, 0:CC * NX], NX),
            "w2": halves(ksf[:, CC * NX:CC * NX + 12 * C], C),
            "g2": halves(ksf[:, CC * NX + 12 * C:CC * NX + 14 * C], C),
            "ev": qsf[:, 0:CC * NX].rearrange("p (c n) -> p c n", c=CC),
            "an": vsf[:, 0:CC * NX].rearrange("p (c n) -> p c n", c=CC),
        }
        w3["ow"] = halves(wm[:, 5632:6144], C)
        w3q = qsf[:, CC * NX:CC * NX + 512].rearrange("p (c n) -> p c n", c=CC)
        w3k = vsf[:, CC * NX:CC * NX + 512].rearrange("p (c n) -> p c n", c=CC)
        w3v = stage[:, 0, :].rearrange("p (c n) -> p c n", c=CC)
        VWN = NX + NE
        vw = waf[0:S, 0:B * VWN].bitcast(F16).rearrange("p (s b n) -> p s b n", s=2, b=B)
        g3 = wm[:, 0:CC * B * S].bitcast(F16).rearrange("p (h c b s) -> p h c b s", h=2, c=CC, b=B)
        kt3 = wm[:, 512:512 + CC * B * S].rearrange("p (c b s) -> p c b s", c=CC, b=B)
        vt3 = wm[:, 1024:1024 + CC * B * S].rearrange("p (c b s) -> p c b s", c=CC, b=B)
        wqt = wm[:, 1536:2048].rearrange("p (c n) -> p c n", c=CC)
        hb3 = wm[:, 2048:2048 + B * 14].rearrange("p (b n) -> p b n", b=B)
        rb3 = wm[:, 2080:2080 + B * NE].rearrange("p (b n) -> p b n", b=B)
        rbin = wm[:, 2088:2088 + NE]
        b2e = wm[0:NE, 2304:2560]
        p3 = [v.rearrange("p (t s) -> p t s", t=TB) for v in (wm[:, 2560:2560 + TB * S], area[:, 0:TB * S])]
        wt3 = [v.bitcast(F16).rearrange("p (s n) -> p s n", s=2) for v in (wm[0:S, 3200:3200 + L], wm[0:S, 512:512 + L])]
        pt3 = wm[0:NE, 4224:4224 + L]
        sm3 = [router_s[:, b, 0:16] for b in range(B)]
        rs3 = [router_s[:, b, 16:24] for b in range(B)]
        lg3 = [router_s[:, b, 24:48].rearrange("p (t e) -> p t e", t=TB) for b in range(B)]
        lm3 = [router_s[:, b, 48:56] for b in range(B)]
        ls3 = [router_s[:, b, 56:64] for b in range(B)]
        bm3 = [router_s[:, b, 64:72] for b in range(B)]
        hid3 = halves(area[:, 0:14 * 512], 512)
        rt3 = halves(area[:, 7168:8192], 512)

        def mrow_no(a, b, p):
            n = 0
            for c in calls:
                if c == (a, b):
                    break
                if ATT[c[0]]["kind"] != "top":
                    n += HP
            return n + p

        def gz_of(g):
            return xnf[:, 1024:1536] if g == 0 else xnf[:, 1536:2048]

        def pieces_of(name):
            out_ = []

            def add(src, dst, n):
                chunks = src.shape[0] // P
                v = src.rearrange("(c p) n -> p c n", p=P)
                step = 2 if n <= 256 else 1
                for c in range(0, chunks, step):
                    for lo in range(0, n, 512):
                        hi = min(lo + 512, n)
                        out_.append((v[:, c:c + step, lo:hi], dst[:, 0, c:c + step, lo:hi], dst[:, 1, c:c + step, lo:hi]))

            if name in ATT:
                add(ins[ATT[name]["w"][0]], att_views(name)[0], ATT[name]["n"][0])
            elif name in MLP:
                for w, v, n in zip(MLP[name]["w"], mlp_views(name), MLP[name]["n"]):
                    add(ins[w], v, n)
            elif name == "moe":
                for e in range(NE):
                    add(ins["L3_xcond_e_w1"][e, 0:C, :], w3["nx"][:, :, :, e * RH:(e + 1) * RH], RH)
                add(ins["L3_xcond_gate_w1"][0:C, :], w3["nx"][:, :, :, NE * RH:NX], C)
                add(ins["L3_xcond_e_w2"].rearrange("e k n -> (e k) n"), w3["w2"], C)
                add(ins["L3_xcond_gate_w2"], w3["g2"], C)
            elif name == "ow":
                add(ins["L3_xcond_out_w"], w3["ow"], C)
            return out_

        SPLIT_AT = {("attn", "x0", 0): [("s1", None)], ("attn", "s1", 0): [("x1", ("post", "x0", B - 1, 1)), ("m1", ("gate", 4))],
                    ("attn", "x1", 0): [("w2", ("post", "s1", B - 1, 1))], ("up", "m1", 0): [("t2", ("post", "x1", B - 1, 1))],
                    ("attn", "w2", 0): [("m2", ("post", "m1", B - 1, 1))], ("up", "m2", 0): [("moe", ("post", "t2", B - 1, 1))],
                    ("prep3", "values"): [("ow", ("post", "m2", B - 1, 1))]}

        block = ctx.enter_context(nc.Block())

        @block.tensor
        def _(pe):
            def accumulate(dst, pairs):
                for i, (lhs, rhs) in enumerate(pairs):
                    mm = pe.matmul(dst, lhs, rhs, start=(i == 0), stop=(i == len(pairs) - 1))
                return mm

            def accumulate3(dst, pairs):
                return accumulate(dst, [x_ for (lh, ll), (rh, rl) in pairs for x_ in ((lh, rh), (lh, rl), (ll, rh))])

            def hl(v, *at_):
                return v[(slice(None), 0, *at_)], v[(slice(None), 1, *at_)]

            def mods(names, key):
                k = open_slot(pe, (key,))
                for n, (w, i, _) in enumerate(MODS):
                    if w in names:
                        mm = accumulate(sl[k][:, 2 * n:2 * n + 2],
                                        [(mod_w[w][:, c, i * P:(i + 1) * P], silc[:].rearrange("p (b c) -> p c b", c=CC)[:, c, :])
                                         for c in range(CC)])
                mm.then_inc(sem(f"full{k}"), 1)

            def gate_rows(layer, w):
                for g, (ly, i) in enumerate(GATES):
                    if ly != layer:
                        continue
                    k = open_slot(pe, ("gate", g))
                    for b in range(B):
                        mm = accumulate(sl[k][:, b * 256:b * 256 + 256],
                                        [(condb[:, b, c, :], mod_w[w][:, c, i * C:(i + 1) * C]) for c in range(CC)])
                    mm.then_inc(sem(f"full{k}"), 1)

            def prep():
                pe.wait_ge(sem("ident"), at("ident", "f"))
                pe.wait_ge(sem("ld_cols"), at("ld_cols", "all"))
                k = open_slot(pe, ("cols",))
                pe.transpose(sl[k][:, 0:NCOL], crow[0:NCOL, :], identf[0:NCOL, 0:NCOL]).then_inc(sem(f"full{k}"), 1)
                pe.wait_ge(sem("ld_ctx"), 16)
                k = open_slot(pe, ("ctraw",))
                for c in range(CC):
                    for b in range(B):
                        mm = pe.transpose(sl[k][:, (c * B + b) * P:(c * B + b) * P + S], cx[:, b, c * P:(c + 1) * P],
                                          identf[0:S, 0:S])
                mm.then_inc(sem(f"full{k}"), 1)
                for v in range(2):
                    pe.wait_ge(sem("cxn"), at("cxn", v))
                    k = open_slot(pe, ("ctn", v))
                    for c in range(CC):
                        for b in range(B):
                            mm = pe.transpose(sl[k][:, (c * B + b) * P:(c * B + b) * P + S],
                                              cxn[:, v, b, c * P:(c + 1) * P], identf[0:S, 0:S])
                    mm.then_inc(sem(f"full{k}"), 1)

            def mod_stage(n):
                if n == 0:
                    pe.wait_ge(sem("silc"), at("silc", "cols"))
                    pe.wait_ge(sem("ld_ss"), 32)
                    mods(("ssq", "sskv"), "mods0")
                elif n == 1:
                    pe.wait_ge(sem("ld_mod1"), 16)
                    mods(("mod1",), "mods1")
                    pe.wait_ge(sem("silc"), at("silc", "rows"))
                    gate_rows(1, "mod1")
                else:
                    pe.wait_ge(sem("ld_ada2"), 16)
                    mods(("ada2",), "mods2")
                    pe.wait_ge(sem("condb2"), 1)
                    gate_rows(2, "ada2")

            def ckv(a):
                _, wkv, _ = att_views(a)
                wk, wv = wkv[:, :, 0:256], wkv[:, :, 256:512]
                pe.wait_ge(sem("ld_" + a), at("ld_" + a, "all"))
                v = {"x0": 0, "x1": 1, "t2": 2}[a]
                pe.wait_ge(sem("ctdone"), at("ctdone", v))
                for m in range(CC):
                    k = open_slot(pe, ("k", a, "c", m))
                    accumulate(sl[k][:, 0:B * S],
                               [(wk[:, c, m * P:(m + 1) * P], ct[:, v, c].rearrange("p b s -> p (b s)")) for c in range(CC)]
                               ).then_inc(sem(f"full{k}"), 1)
                k = open_slot(pe, ("v", a, "c"))
                for b in range(B):
                    mm = accumulate(sl[k][0:S, b * C:(b + 1) * C], [(ct[:, v, c, b, :], wv[:, c, :]) for c in range(CC)])
                mm.then_inc(sem(f"full{k}"), 1)

            def ln(i, b):
                for c in range(CC):
                    k = open_slot(pe, ("ln", i, b, c))
                    for t in range(TB):
                        if c == 0:
                            pe.wait_ge(sem(xn_sem(i, b)), at(xn_sem(i, b), i, b, t))
                        mm = pe.transpose(sl[k][:, t * P:(t + 1) * P], xn[:, t, c * P:(c + 1) * P], identf[:, :])
                    mm.then_inc(sem(f"full{k}"), 1)

            def proj(a, b):
                w, _, _ = att_views(a)
                pe.wait_ge(sem("sp_" + a), at("sp_" + a, "all"))
                emptied(pe, ("ln", ATT[a]["ln"], b, CC - 1))
                for t, m in split_order(a):
                    lo = (0 if t == "q" else C) + m * P
                    k = open_slot(pe, (t, a, b, m))
                    for n in range(2):
                        mm = accumulate3(sl[k][:, n * 512:(n + 1) * 512],
                                         [(hl(w, c, slice(lo, lo + P)), hl(hts[:, b], c, slice(n * 512, (n + 1) * 512))) for c in range(CC)])
                    mm.then_inc(sem(f"full{k}"), 1)
                if ATT[a]["kind"] in ("self", "win"):
                    for g in range(2):
                        k = open_slot(pe, ("v", a, b, g))
                        for t in range(4):
                            lo = (g * 4 + t) * P
                            mm = accumulate3(sl[k][:, t * C:(t + 1) * C],
                                             [(hl(hts[:, b], c, slice(lo, lo + P)), hl(w, c, slice(2 * C, 3 * C))) for c in range(CC)])
                        mm.then_inc(sem(f"full{k}"), 1)

            def attn(a, b):
                kind = ATT[a]["kind"]
                units = first_pass_units(kind)
                nk = S if kind in ("cross", "top") else P

                def first_pass(p, u):
                    m = p // 4
                    if u == 0:
                        pe.wait_ge(sem(f"qin{m}"), at(f"qin{m}", a, b))
                        pe.wait_ge(sem(f"kin{m}"), at(f"kin{m}", a, b if kind in ("self", "win") else "c"))
                        pe.wait_ge(sem("mzero"), at("mzero", a, b))
                    k = open_slot(pe, ("p1", a, b, p, u), "half")
                    if kind == "self":
                        j, t, n = units[u]
                        mm = pe.matmul(sl[k][:, 0:512], qs[:, p, t * P:(t + 1) * P],
                                       ks[:, 2 * p + j, n * 512:(n + 1) * 512], start=True, stop=True)
                    else:
                        for q2 in range(2):
                            t = u * 2 + q2
                            lo = t * P if kind == "win" else b * S
                            mm = pe.matmul(sl[k][:, q2 * 256:q2 * 256 + 2 * nk].rearrange("p (j s) -> p j s", j=2),
                                           qs[:, p, t * P:(t + 1) * P], ks[:, 2 * p:2 * p + 2, lo:lo + nk],
                                           start=True, stop=True)
                    mm.then_inc(sem(f"full{k}"), 1)

                def wide_pass(p, u):
                    if u == 0:
                        pe.wait_ge(sem("qin0"), at("qin0", a, b))
                        pe.wait_ge(sem("kin0"), at("kin0", a, b))
                        pe.wait_ge(sem("mzero"), at("mzero", a, b))
                    k = open_slot(pe, ("wide", a, b, p, u))
                    j, t = divmod(u, TB)
                    for n in range(2):
                        mm = pe.matmul(sl[k][:, n * 512:(n + 1) * 512], qs[:, p, t * P:(t + 1) * P],
                                       ks[:, 2 * p + j, n * 512:(n + 1) * 512], start=True, stop=True)
                    mm.then_inc(sem(f"full{k}"), 1)

                def turn(p):
                    if kind == "self" and p < 2:
                        for u in range(2 * TB - 4, 2 * TB):
                            emptied(pe, ("wide", a, b, p, u))
                    elif kind == "self":
                        pe.wait_ge(sem("maxed"), at("maxed", a, b, p))
                    else:
                        emptied(pe, ("p1", a, b, p, 2))
                        emptied(pe, ("p1", a, b, p, 3))
                    k = open_slot(pe, ("t", a, b, p), "half")
                    pe.transpose(sl[k].bitcast(F16)[0:2 * TB, 0:P], m16[:, p % MP].rearrange("p j t -> p (j t)"), identh[:, :]
                                 ).then_inc(sem(f"full{k}"), 1)

                def side(tasks):
                    for t in tasks:
                        if t[0] == "t":
                            turn(t[1])
                        elif t[0] == "wide":
                            wide_pass(t[1], t[2])
                        elif kind == "top":
                            first_pass(t[1], 2 * t[2])
                            first_pass(t[1], 2 * t[2] + 1)
                        else:
                            first_pass(t[1], t[2])

                def scores(i, p, j, kt):
                    k = open_slot(pe, ("s", a, b, i), step_no[(a, b, i)] % 2)
                    h = 2 * p + j
                    if kind == "top":
                        for t in range(TB):
                            if j == 0 and t % 4 == 0:
                                pe.wait_ge(sem("topp"), at("topp", a, b, p, t // 4))
                            src = top_p[(2 * p + t // 4) % 4].rearrange("p (q j s) -> p q j s", q=4, j=2)
                            mm = pe.transpose(sl[k][0:S, t * P:(t + 1) * P], src[:, t % 4, j, :], identf[:, :])
                    elif kind == "win":
                        pe.wait_ge(sem(f"mrow{p % MP}"), at(f"mrow{p % MP}", a, b, p))
                        for w in range(TB):
                            mm = pe.matmul(sl[k][:, w * P:(w + 1) * P], ks[:, h, w * P:(w + 1) * P],
                                           qs[:, p, w * P:(w + 1) * P], start=True, stop=True)
                    else:
                        if kt == 0:
                            pe.wait_ge(sem(f"mrow{p % MP}"), at(f"mrow{p % MP}", a, b, p))
                        lo = kt * P if kind == "self" else b * S
                        for n in range(2):
                            mm = pe.matmul(sl[k][0:nk, n * 512:(n + 1) * 512], ks[:, h, lo:lo + nk],
                                           qs[:, p, n * 512:(n + 1) * 512], start=True, stop=True)
                    mm.then_inc(sem(f"full{k}"), 1)

                def values(i, half_):
                    p, _, kt = steps[i]
                    g = p // 2
                    if kt == 0 and half_ == 0:
                        open_slot(pe, ("o", a, b, g), 2, signals=False)
                    if half_ == 0:
                        for r in range(GH):
                            emptied(pe, ("s", a, b, i + r))
                    if i == 0 and half_ == 0 and kind in ("self", "win"):
                        for v in range(2):
                            emptied(pe, ("v", a, b, v))
                    elif i == 0 and half_ == 0:
                        emptied(pe, ("v", a, "c"))
                    for n in range(4 * half_, 4 * half_ + 4) if kind == "win" else (half_,):
                        for r in range(GH):
                            h = g * GH + r
                            e = pr[:, step_no[(a, b, i + r)] % RP, :]
                            if kind == "win":
                                mm = pe.matmul(sl[2][32 * r:32 * r + 32, n * P:(n + 1) * P], vs[:, n, h, :], e[:, n * P:(n + 1) * P],
                                               start=True, stop=True, tile_position=(0, 32 * r))
                            else:
                                vt = kt if kind == "self" else b
                                mm = pe.matmul(sl[2][32 * r:32 * r + 32, n * 512:(n + 1) * 512], vs[0:nk, vt, h, :],
                                               e[0:nk, n * 512:(n + 1) * 512], start=(kt == 0),
                                               stop=(kind != "self" or kt == TB - 1), tile_position=(0, 32 * r))
                    if half_ == 1:
                        mm.then_inc(sem("pv"), mark("pv", a, b, i + GH - 1))

                start, ahead = side_plan(kind)
                side(start)
                steps = steps_of(kind)
                for i, (p, j, kt) in enumerate(steps):
                    scores(i, p, j, kt)
                    when = (0, 2)
                    if i >= GH and i % GH in when:
                        half_ = when.index(i % GH)
                        before = 2 if i % GH == 0 else 1
                        side(ahead[i][:before])
                        values(i - i % GH - GH, half_)
                        side(ahead[i][before:])
                    else:
                        side(ahead[i])
                for half_ in range(2):
                    values(len(steps) - GH, half_)

            def post(a, b):
                wo = att_views(a)[2]
                pe.wait_ge(sem("ld_" + a), at("ld_" + a, "all"))
                for g in range(2):
                    pe.wait_ge(sem(f"pack{g}"), at(f"pack{g}", a, b, H // GH - 2 + g))
                for g in range(2):
                    k = open_slot(pe, ("post", a, b, g))
                    for t in range(4):
                        lo = (g * 4 + t) * P
                        mm = accumulate(sl[k][:, t * C:(t + 1) * C], [(ht[:, b, c, lo:lo + P], wo[:, c, :]) for c in range(CC)])
                    mm.then_inc(sem(f"full{k}"), 1)

            def mlp(m, b, lowering):
                up, down = mlp_views(m)
                pe.wait_ge(sem("sp_" + m), at("sp_" + m, "all"))
                emptied(pe, ("ln", MLP[m]["ln"], b, CC - 1))
                njob = 4 if m == "m1" else 8

                def hidden(r):
                    for j in range(njob):
                        k = open_slot(pe, ("up", m, b, r, j))
                        for n in range(2):
                            ch = 2 * j + n if m == "m1" else j + 8 * n
                            mm = accumulate3(sl[k][:, n * 512:(n + 1) * 512],
                                             [(hl(up, c, slice(ch * P, (ch + 1) * P)), hl(hts[:, b], c, slice(r * 512, (r + 1) * 512)))
                                              for c in range(CC)])
                        mm.then_inc(sem(f"full{k}"), 1)

                def lower(r):
                    pe.wait_ge(sem("low"), at("low", m, b, r, 7))
                    k = open_slot(pe, ("post", m, b, r))
                    for t in range(4):
                        mm = accumulate3(sl[k][:, t * C:(t + 1) * C],
                                         [(hl(hid[:, r], c, slice(t * P, (t + 1) * P)), hl(down, c)) for c in range(8)])
                    mm.then_inc(sem(f"full{k}"), 1)

                for r in range(2):
                    (lower if lowering else hidden)(r)

            def prep3(part):
                if part == "values":
                    values3()
                    return
                pe.wait_ge(sem("ld_l3"), at("ld_l3", "all"))
                k = open_slot(pe, ("wqt",))
                for c in range(CC):
                    for m in range(CC):
                        mm = pe.transpose(sl[k][:, (m * CC + c) * P:(m * CC + c + 1) * P], w3q[:, c, m * P:(m + 1) * P], identf[:, :])
                mm.then_inc(sem(f"full{k}"), 1)
                for name, w in (("kt3", w3k), ("vt3", w3v)):
                    k = open_slot(pe, (name,))
                    for m in range(CC):
                        mm = accumulate(sl[k][:, m * 512:m * 512 + B * S],
                                        [(w[:, c, m * P:(m + 1) * P], ct[:, 2, c].rearrange("p b s -> p (b s)")) for c in range(CC)])
                    mm.then_inc(sem(f"full{k}"), 1)
                emptied(pe, ("wqt",))
                emptied(pe, ("kt3",))
                k = open_slot(pe, ("g3",))
                for m in range(CC):
                    mm = accumulate(sl[k][:, m * 512:m * 512 + B * S],
                                    [(wqt[:, c, m * P:(m + 1) * P], kt3[:, c].rearrange("p b s -> p (b s)")) for c in range(CC)])
                mm.then_inc(sem(f"full{k}"), 1)

            def values3():
                emptied(pe, ("vt3",))
                for b in range(B):
                    for g in range(2):
                        k = open_slot(pe, ("vw", b, g))
                        for n in range(2):
                            lo = g * 1024 + n * 512
                            if lo >= NX:
                                continue
                            hi = min(lo + 512, NX)
                            mm = accumulate(sl[k][0:S, n * 512:n * 512 + hi - lo],
                                            [(vt3[:, c, b, :], w3["ev"][:, c, lo:hi]) for c in range(CC)])
                        if g == 1:
                            mm = accumulate(sl[k][0:S, 768:768 + NE], [(vt3[:, c, b, :], wr[:, 2 + c, :]) for c in range(CC)])
                        mm.then_inc(sem(f"full{k}"), 1)
                k = open_slot(pe, ("anchor",))
                cond = cols[:, 0:4].rearrange("p (b c) -> p c b", c=CC)
                for n in range(14):
                    accumulate(sl[k][:, 2 * n:2 * n + 2], [(w3["an"][:, c, n * P:(n + 1) * P], cond[:, c, :]) for c in range(CC)])
                pe.wait_ge(sem("condb3"), 1)
                for b in range(B):
                    mm = accumulate(sl[k][:, 512 + 4 * b:512 + 4 * b + NE], [(condb[:, b, c, :], wr[:, 4 + c, :]) for c in range(CC)])
                mm.then_inc(sem(f"full{k}"), 1)

            def scores3(b):
                emptied(pe, ("ln", 7, b, CC - 1))
                emptied(pe, ("g3",))
                k = open_slot(pe, ("sc3", b))
                for t in range(TB):
                    mm = accumulate3(sl[k][:, t * P:t * P + S], [(hl(hts[:, b], c, slice(t * P, (t + 1) * P)), hl(g3, c, b)) for c in range(CC)])
                mm.then_inc(sem(f"full{k}"), 1)

            def evidence(b):
                pe.wait_ge(sem("p3"), at("p3", b))
                k = open_slot(pe, ("wt3", b))
                for t in range(TB):
                    mm = pe.transpose(sl[k][0:S, t * P:(t + 1) * P], p3[b][:, t, :], identf[:, :])
                mm.then_inc(sem(f"full{k}"), 1)

            def router(b):
                emptied(pe, ("wt3", b))
                pe.wait_ge(sem("wrs"), 1)
                emptied(pe, ("vw", B - 1, 1))
                emptied(pe, ("vw", B - 1, 0))
                emptied(pe, ("vw", 0, 1))
                emptied(pe, ("vw", 0, 0))
                k = open_slot(pe, ("lg3", b))
                for t in range(TB):
                    lo = t * P
                    mm = accumulate3(sl[k][:, 4 * t:4 * t + NE],
                                     [(hl(hts[:, b], c, slice(lo, lo + P)), hl(wrs, c)) for c in range(CC)]
                                     + [(hl(wt3[b], slice(lo, lo + P)), hl(vw, b, slice(NX, VWN)))])
                mm.then_inc(sem(f"full{k}"), 1)

            def hidden3(b, r, j):
                lo = r * 512
                if (b, r, j) == (0, 0, 0):
                    pe.wait_ge(sem("sp_moe"), at("sp_moe", "all"))
                k = open_slot(pe, ("h3", b, r, j))
                for n in range(2):
                    ch = 2 * j + n
                    mm = accumulate3(sl[k][:, n * 512:(n + 1) * 512],
                                     [(hl(w3["nx"], c, slice(ch * P, (ch + 1) * P)), hl(hts[:, b], c, slice(lo, lo + 512)))
                                      for c in range(CC)]
                                     + [(hl(vw, b, slice(ch * P, (ch + 1) * P)), hl(wt3[b], slice(lo, lo + 512)))])
                mm.then_inc(sem(f"full{k}"), 1)

            def probs3(b):
                pe.wait_ge(sem("rp3"), at("rp3", b))
                k = open_slot(pe, ("pt3", b))
                for t in range(TB):
                    mm = pe.transpose(sl[k][0:NE, t * P:(t + 1) * P], lg3[b][:, t, :], identf[:, :])
                mm.then_inc(sem(f"full{k}"), 1)

            def experts3(b, r):
                emptied(pe, ("pt3", b))
                pe.wait_ge(sem("low"), at("low", "moe", b, r, 13))
                for t in range(4):
                    k = open_slot(pe, ("ex3", b, r, t))
                    for e in range(NE):
                        accumulate3(sl[k][:, e * C:(e + 1) * C],
                                    [(hl(hid3, 4 * e + c, slice(t * P, (t + 1) * P)), hl(w3["w2"], 4 * e + c)) for c in range(4)])
                    lo = r * 512 + t * P
                    pe.matmul(sl[k][:, 768:1024], pt3[:, lo:lo + P], b2e, start=True, stop=True).then_inc(sem(f"full{k}"), 1)

            def routed3(b, r):
                k = open_slot(pe, ("rt3", b, r))
                for t in range(4):
                    emptied(pe, ("ex3", b, r, t))
                    for c in range(CC):
                        mm = pe.transpose(sl[k][:, c * 512 + t * P:c * 512 + (t + 1) * P], xn[:, t, c * P:(c + 1) * P], identf[:, :])
                mm.then_inc(sem(f"full{k}"), 1)

            def gated3(b, r):
                emptied(pe, ("rt3", b, r))
                pe.wait_ge(sem("sp_ow"), at("sp_ow", "all"))
                for g in range(2):
                    k = open_slot(pe, ("y3", b, r, g))
                    for t in range(2):
                        q = (2 * g + t) * P
                        accumulate3(sl[k][:, t * C:(t + 1) * C], [(hl(rt3, c, slice(q, q + P)), hl(w3["ow"], c)) for c in range(CC)])
                        mm = accumulate3(sl[k][:, 512 + t * C:512 + (t + 1) * C],
                                         [(hl(hid3, 12 + c, slice(q, q + P)), hl(w3["g2"], c)) for c in range(CC)])
                    mm.then_inc(sem(f"full{k}"), 1)

            run = {"prep": prep, "mods": mod_stage, "ckv": ckv, "norm": lambda i, b: None, "turn": ln, "proj": proj, "attn": attn, "post": post,
                   "up": lambda m, b: mlp(m, b, False),
                   "down": lambda m, b: mlp(m, b, True), "prep3": prep3, "scores3": scores3, "evidence": evidence, "router": router,
                   "hidden3": hidden3, "probs3": probs3, "experts3": experts3, "routed3": routed3, "gated3": gated3}
            for s in sched:
                run[s[0]](*s[1:])

        @block.scalar
        def _(act):
            def silu_cond():
                act.wait_ge(sem("cols"), at("cols", "copied"))
                act.activation(silc[:], cols[:, 0:4], ACT.Silu).then_inc(sem("silc"), mark("silc", "cols"))

            def prep():
                for q in range(4):
                    act.dma_start(x[:, 4 * q:4 * q + 4, :],
                                  ins["x"].rearrange("b (t p) c -> p (b t) c", p=P)[:, 4 * q:4 * q + 4, :]
                                  ).then_inc(sem(f"ld_x{q}"), mark(f"ld_x{q}", by=16))
                silu_cond()

            def mod_stage(n):
                pass

            def split_evac(t, a, b, m, n, biascol):
                j = split_no[(a, t, b, m)]
                if j >= 2:
                    act.wait_ge(sem(f"stout{j % 2}"), at(f"stout{j % 2}", j - 2))
                src = filled(act, (t, a, b, m))
                act.activation(st[:, j % 2, 0, 0:n], src[:, 0:n], ACT.Identity, bias=cols[:, biascol + m:biascol + m + 1]
                               ).then_inc(sem("high"), mark("high", j))

            def ckv(a):
                for m in range(CC):
                    split_evac("k", a, "c", m, B * S, ATT[a]["kb"])

            def ln(i, b):
                if i in LN_MOD:
                    w, s0, b0 = LN_MOD[i]
                    act.wait_ge(sem("modc"), at("modc", {"ssq": 0, "mod1": 1, "ada2": 2}[w]))
                for c in range(CC):
                    if i in LN_MOD:
                        scale = modc[:, MOD_AT[(w, s0 + c)], b:b + 1]
                        bias = modc[:, MOD_AT[(w, b0 + c)], b:b + 1]
                    elif i == 7:
                        g0, e0 = COL["L3_xcond_ln_gamma"], COL["L3_xcond_ln_beta"]
                        scale, bias = cols[:, g0 + c:g0 + c + 1], cols[:, e0 + c:e0 + c + 1]
                    else:
                        scale, bias = 1.0, 0.0
                    src = filled(act, ("ln", i, b, c))
                    n = ln_calls.index(("ln", i, b))
                    tmp = tmp32_of(i, b, c)
                    if n:
                        emptied(act, (*ln_calls[n - 1], c))
                    body_before = sched[sched.index(("turn", i, b)) - 1]
                    if body_before[0] == "up" and c == 0:
                        act.wait_ge(sem("low"), at("low", *body_before[1:], 1, 7))
                    elif body_before[0] == "up":
                        emptied(act, ("ln", i, b, c - 1))
                    cuts = ((0, SHIFT, L - SHIFT), (L - SHIFT, 0, SHIFT)) if i == 4 else ((0, 0, L),)
                    for dst in (hts[:, b, 0, c, :], tmp):
                        for to, lo, n in cuts:
                            mm = act.activation(dst[:, to:to + n], src[:, lo:lo + n], ACT.Identity, bias=bias, scale=scale)
                    mm.then_inc(sem("lnhigh"), mark("lnhigh", i, b, c))

            def proj(a, b):
                for t, m in split_order(a):
                    split_evac(t, a, b, m, L, ATT[a]["qb" if t == "q" else "kb"])
                if b == 0 and ATT[a]["kind"] in ("cross", "top"):
                    stack_in(act, "k", a, "c", 1, B * S)
                for t, m in split_order(a):
                    if m:
                        stack_in(act, t, a, b, m, L)

            def attn(a, b):
                kind = ATT[a]["kind"]
                nk = S if kind in ("cross", "top") else P
                start, ahead = side_plan(kind)

                def top_side(tasks):
                    for _, p, u in tasks:
                        n = 2 * p + u
                        if n >= 2 or b:
                            before = (a, b, (n - 2) // 2, n % 2) if n >= 2 else (a, b - 1, HP - 1, n)
                            act.wait_ge(sem("topw"), at("topw", *before))
                            act.wait_ge(sem("topd"), at("topd", *before))
                        for v in range(2):
                            src = filled(act, ("p1", a, b, p, 2 * u + v))
                            act.activation(top_s[n % 2][:, v, :].rearrange("p (q s) -> p q s", q=2),
                                           src[:, 0:512].rearrange("p (q s) -> p q s", q=2)[:, :, 0:2 * S], ACT.Identity
                                           ).then_inc(free(("p1", a, b, p, 2 * u + v)), 1)
                        if n:
                            top_exp(n - 1)

                def top_exp(n):
                    act.wait_ge(sem("topd"), at("topd", a, b, n // 2, n % 2))
                    act.activation(top_p[n % 4], top_p[n % 4], ACT.Exp, scale=SCALE).then_inc(sem("tope"), mark("tope", a, b, n // 2, n % 2))

                if kind == "top":
                    top_side(start)
                for i in range(len(steps_of(kind))):
                    n = step_no[(a, b, i)]
                    if n >= RP:
                        act.wait_ge(sem("pv"), (n - RP) // GH + 1)
                    if i == 0:
                        for j in range(split_no[(a, "k" if kind in ("self", "win") else "q", b, CC - 1)] - 1,
                                       split_no[(a, "k" if kind in ("self", "win") else "q", b, CC - 1)] + 1):
                            act.wait_ge(sem(f"stout{j % 2}"), at(f"stout{j % 2}", j))
                    src = filled(act, ("s", a, b, i))
                    if kind == "top":
                        act.activation(pr[0:nk, n % RP, :], src[0:nk, :], ACT.Identity).then_inc(free(("s", a, b, i)), 1)
                        top_side(ahead[i])
                        if ahead[i - 1] and not ahead[i]:
                            top_exp(2 * HP - 1)
                    else:
                        act.activation(pr[0:nk, n % RP, :], src[0:nk, :], ACT.Exp, scale=SCALE).then_inc(free(("s", a, b, i)), 1)

            def mlp(m, b, lowering):
                if lowering:
                    return
                hb = MLP[m]["hb"]
                for r in range(2):
                    if b:
                        filled(act, ("post", m, b - 1, r))
                    elif r == 0:
                        act.wait_ge(sem("on"), at("on", *attention_before(m), H // GH - 1))
                    for j in range(4 if m == "m1" else 8):
                        src = filled(act, ("up", m, b, r, j))
                        for n in range(2 if m == "m1" else 1):
                            ch = 2 * j + n if m == "m1" else j
                            if (b, r, ch) >= (0, 0, 2):
                                act.wait_ge(sem("low"), at("low", *low_two_before(m, b, r, ch)))
                            if ch < 2 and r == 0:
                                act.wait_ge(sem("xu"), at("xu", *update_before(m, b)))
                            if m == "m1":
                                f = dict(func=ACT.Gelu_apprx_tanh, bias=cols[:, hb + ch:hb + ch + 1])
                                s_ = src[:, n * 512:(n + 1) * 512]
                                act.activation(hid32[:, ch % 2, :], s_, **f).then_inc(sem("silu"), mark("silu", m, b, r, ch))
                                high = act.activation(hid[:, r, 0, ch, :], s_, **f)
                                if n == 0:
                                    high.then_inc(sem("uhigh"), mark("uhigh", m, b, r, ch))
                                else:
                                    high.then_inc(free(("up", m, b, r, j)), 1)
                            else:
                                act.activation(hid32[:, ch % 2, :], src[:, 0:512], ACT.Silu, bias=cols[:, hb + j:hb + j + 1]
                                               ).then_inc(sem("silu"), mark("silu", m, b, r, ch))

            def prep3(part):
                pass

            def scores3(b):
                src = filled(act, ("sc3", b))
                act.wait_ge(sem("bm3"), at("bm3", b))
                for t in range(TB):
                    mm = act.activation(p3[b][:, t, :], src[:, t * P:t * P + S], ACT.Exp, bias=bm3[b][:, t:t + 1], scale=1.0 / 16,
                                        accum_out=sm3[b][:, 8 + t:9 + t])
                mm.then_inc(free(("sc3", b)), 1)

            def evidence(b):
                src = filled(act, ("wt3", b))
                act.activation(wt3[b][:, 0, :], src[0:S, :], ACT.Identity).then_inc(sem("wthigh"), mark("wthigh", b))

            def router(b):
                act.wait_ge(sem("lgs"), at("lgs", b))
                act.activation(lg3[b], lg3[b], ACT.Exp).then_inc(sem("lge"), mark("lge", b))

            def hidden3(b, r, j):
                src = filled(act, ("h3", b, r, j))
                before = divmod(2 * b + r - 1, 2)
                if j == 0 and (b or r):
                    filled(act, ("ex3", *before, 3))
                if j == 6 and (b or r):
                    filled(act, ("y3", *before, 1))
                if (b, r, j) == (0, 0, 0):
                    act.wait_ge(sem("hb3"), 1)
                    act.wait_ge(sem("xu"), at("xu", "m2", B - 1, 1))
                    act.wait_ge(sem("p3"), at("p3", B - 1))
                    filled(act, ("wt3", B - 1))
                for n in range(2):
                    ch = 2 * j + n
                    if (b, r, ch) >= (0, 0, 2):
                        act.wait_ge(sem("low"), at("low", *low_two_before("moe", b, r, ch)))
                    f = dict(func=ACT.Silu, bias=hb3[:, b, ch:ch + 1])
                    act.activation(hid32[:, ch % 2, :], src[:, n * 512:(n + 1) * 512], **f).then_inc(sem("silu"), mark("silu", "moe", b, r, ch))
                    high = act.activation(hid3[:, 0, ch, :], src[:, n * 512:(n + 1) * 512], **f)
                    if n == 0:
                        high.then_inc(sem("uhigh"), mark("uhigh", "moe", b, r, ch))
                    else:
                        high.then_inc(free(("h3", b, r, j)), 1)

            def probs3(b):
                src = filled(act, ("pt3", b))
                act.activation(pt3, src[0:NE, :], ACT.Identity).then_inc(free(("pt3", b)), 1)

            def experts3(b, r):
                pass

            def routed3(b, r):
                src = filled(act, ("rt3", b, r))
                act.activation(rt3[:, 0], src.rearrange("p (c n) -> p c n", c=CC), ACT.Identity).then_inc(sem("rthigh"), mark("rthigh", b, r))

            def gated3(b, r):
                for g in range(2):
                    act.wait_ge(sem("gz"), at("gz", b, r, g))
                    act.activation(gz_of(g), gz_of(g), ACT.Tanh, scale=0.5).then_inc(sem("tanh"), mark("tanh", b, r, g))

            run = {"prep": prep, "mods": mod_stage, "ckv": ckv, "norm": lambda i, b: None, "turn": ln, "proj": proj, "attn": attn,
                   "post": lambda a, b: None, "up": lambda m, b: mlp(m, b, False),
                   "down": lambda m, b: mlp(m, b, True), "prep3": prep3, "scores3": scores3, "evidence": evidence, "router": router,
                   "hidden3": hidden3, "probs3": probs3, "experts3": experts3, "routed3": routed3, "gated3": gated3}
            for s in sched:
                run[s[0]](*s[1:])

        @block.vector
        def _(dve):
            chain = [0]

            def linked(instr):
                chain[0] += 1
                instr.then_inc(sem("dve_chain"), 1)
                dve.wait_ge(sem("dve_chain"), chain[0])

            def prep():
                dve.memset(mhalf[:], -0.5).then_inc(sem("mhalf"), 1)
                dve.memset(qs[:].rearrange("p a b -> p (a b)").bitcast(U32), 0).then_inc(sem("qzero"), 1)
                dve.memset(ks[:].rearrange("p a b -> p (a b)").bitcast(U32), 0).then_inc(sem("kzero"), mark("kzero", 0))
                dve.wait_ge(sem("ld_ctx"), 16)
                for b in range(B):
                    i = dve.bn_stats(stats[0:S, b, :], cx[:, b, :])
                linked(i)
                for b in range(B):
                    i = dve.bn_aggr(mv[0:S, b, :], stats[0:S, b, :])
                i.then_inc(sem("mv"), mark("mv", "ctx"))
                src = filled(dve, ("cols",))
                linked(dve.tensor_copy(cols[:, 0:NCOL], src[:, 0:NCOL]))
                dve.tensor_copy(cols[:, 127:128], src[:, 0:1]).then_inc(free(("cols",)), 1)
                dve.memset(rec[:, 0:1], 0.0).then_inc(sem("cols"), mark("cols", "copied"))
                src = filled(dve, ("ctraw",))
                dve.tensor_copy(ct[:, 2].rearrange("p c b s -> p (c b) s"),
                                src[:, 0:512].rearrange("p (g s) -> p g s", g=4)[:, :, 0:S]).then_inc(free(("ctraw",)), 1)
                dve.wait_ge(sem("rstd"), at("rstd", "ctx"))
                for v in range(2):
                    for b in range(B):
                        i = dve.tensor_scalar(cxn[:, v, b, :], cx[:, b, :], mv[0:S, b, 0:1], rstd[0:S, 4 * v + b:4 * v + b + 1],
                                              ALU.subtract, ALU.mult)
                    i.then_inc(sem("cxn"), mark("cxn", v))
                dve.wait_ge(sem("silc"), at("silc", "cols"))
                for b in range(B):
                    for c in range(CC):
                        i = dve.tensor_copy(condb[:, b, c, :], silc[:, b * CC + c:b * CC + c + 1].to_broadcast([P, P]))
                i.then_inc(sem("silc"), mark("silc", "rows"))
                src = filled(dve, ("ctn", 1))
                dve.tensor_copy(ct[:, 1].rearrange("p c b s -> p (c b) s"),
                                src[:, 0:512].rearrange("p (g s) -> p g s", g=4)[:, :, 0:S]).then_inc(free(("ctn", 1)), 1)

            def mod_stage(n):
                if n == 1:
                    mod_columns(1, ("mod1",), "mods1")
                    gate_rows(1)
                    return
                if n == 2:
                    mods2()
                    return
                mod_columns(0, ("ssq", "sskv"), "mods0")
                src = filled(dve, ("ctn", 0))
                for c in range(CC):
                    for b in range(B):
                        i = dve.tensor_scalar(ct[:, 0, c, b, :], src[:, (c * B + b) * P:(c * B + b) * P + S],
                                              modc[:, MOD_AT[("sskv", c)], b:b + 1], modc[:, MOD_AT[("sskv", 2 + c)], b:b + 1],
                                              ALU.mult, ALU.add)
                i.then_inc(free(("ctn", 0)), 1)
                for v in (2, 1, 0):
                    dve.memset(rec[:, v:v + 1], 0.0).then_inc(sem("ctdone"), mark("ctdone", v))

            def mod_columns(n, names, key):
                lo = min(i for i, mm in enumerate(MODS) if mm[0] in names)
                src = filled(dve, (key,))
                for w in names:
                    blocks = [(i, bl) for i, (ww, bl, _) in enumerate(MODS) if ww == w]
                    run0 = 0
                    for r in range(len(blocks)):
                        if r + 1 == len(blocks) or blocks[r + 1][1] != blocks[r][1] + 1:
                            i0, b0 = blocks[run0]
                            nb = r - run0 + 1
                            c0 = MOD_COL[w] + b0
                            ins_ = dve.tensor_tensor(modc[:, i0:i0 + nb, :], src[:, 2 * i0:2 * (i0 + nb)].rearrange("p (n b) -> p n b", b=B),
                                                     cols[:, c0:c0 + nb].unsqueeze(2).to_broadcast([P, nb, B]), ALU.add)
                            run0 = r + 1
                linked(ins_)
                for i, (w, bl, plus) in enumerate(MODS):
                    if w in names and plus and not (i and MODS[i - 1][0] == w and MODS[i - 1][2] and MODS[i - 1][1] == bl - 1):
                        linked(dve.tensor_scalar_add(modc[:, i:i + 2, :], modc[:, i:i + 2, :], 1.0))
                dve.tensor_copy(rec[:, 4:5], src[:, 2 * lo:2 * lo + 1]).then_inc(free((key,)), 1)
                dve.memset(rec[:, 5:6], 0.0).then_inc(sem("modc"), mark("modc", n))

            def gate_rows(layer):
                for g, (ly, _) in enumerate(GATES):
                    if ly == layer:
                        dve.wait_ge(sem(f"ld_g{layer}"), at(f"ld_g{layer}", "all"))
                        src = filled(dve, ("gate", g))
                        dve.tensor_tensor(gates[:, g], src[:, 0:512].rearrange("p (b c) -> p b c", b=B), gates[:, g], ALU.add
                                          ).then_inc(free(("gate", g)), 1)

            def mods2():
                mod_columns(2, ("ada2",), "mods2")
                dve.wait_ge(sem("ld_g2"), 96)
                i = None
                for b in range(B):
                    for c in range(CC):
                        i = dve.tensor_copy(condb[:, b, c, :], silc[:, b * CC + c:b * CC + c + 1].to_broadcast([P, P]))
                i.then_inc(sem("condb2"), 1)
                gate_rows(2)

            def split(t, a, b, m, n):
                j = split_no[(a, t, b, m)]
                src = filled(dve, (t, a, b, m))
                dve.wait_ge(sem("high"), at("high", j))
                col = ATT[a]["qb" if t == "q" else "kb"] + m
                dve.scalar_tensor_tensor(out=st[:, j % 2, 1, 0:n], in0=src[:, 0:n], scalar=cols[:, col:col + 1], in1=st[:, j % 2, 0, 0:n],
                                         op0=ALU.add, op1=ALU.subtract).then_inc(free((t, a, b, m)), 1)

            def ckv(a):
                for m in range(CC):
                    split("k", a, "c", m, B * S)
                src = filled(dve, ("v", a, "c"))
                dve.wait_ge(sem("ld_" + a), at("ld_" + a, "all"))
                if a == "x0":
                    dve.wait_ge(sem("vones"), 1)
                dve.tensor_tensor(vs[0:S, 0:B, :, 0:D], src[0:S, 0:B * C].rearrange("p (b h d) -> p b h d", b=B, h=H),
                                  vbias[0:S, ATT[a]["half"], :].rearrange("p (h d) -> p h d", h=H).unsqueeze(1).to_broadcast([S, B, H, D]),
                                  ALU.add).then_inc(free(("v", a, "c")), 1)

            def ln(i, b):
                if i == 0:
                    dve.wait_ge(sem(f"ld_x{2 * b}"), 16)
                    dve.wait_ge(sem(f"ld_x{2 * b + 1}"), 16)
                else:
                    dve.wait_ge(sem("xu"), at("xu", prev_update(i, b), b, 1))
                prev = ln_calls.index(("ln", i, b)) - 1
                for t in range(TB):
                    ins_ = dve.bn_stats(stats[:, t, :], x[:, b * TB + t, :])
                linked(ins_)
                if prev >= 0:
                    dve.wait_ge(sem(xn_sem(*ln_calls[prev][1:])), at(xn_sem(*ln_calls[prev][1:]), *ln_calls[prev][1:], TB - 1))
                for t in range(TB):
                    ins_ = dve.bn_aggr(mv[:, t, :], stats[:, t, :])
                ins_.then_inc(sem("mv"), mark("mv", i, b))
                if ("norm", i, b) not in relaxed:
                    if prev >= 0:
                        filled(dve, (*ln_calls[prev], CC - 1))
                    dve.wait_ge(sem("rstd"), at("rstd", i, b))
                    for t in range(TB):
                        dve.tensor_scalar(xn[:, t, :], x[:, b * TB + t, :], mv[:, t, 0:1], rstd[:, t:t + 1],
                                          ALU.subtract, ALU.mult).then_inc(sem(xn_sem(i, b)), mark(xn_sem(i, b), i, b, t))

            def turn(i, b):
                for c in range(CC):
                    dve.wait_ge(sem("lnhigh"), at("lnhigh", i, b, c))
                    dve.tensor_tensor(hts[:, b, 1, c, :], tmp32_of(i, b, c), hts[:, b, 0, c, :], ALU.subtract).then_inc(free(("ln", i, b, c)), 1)

            def prev_update(i, b):
                order = ["x0", "s1", "x1", "m1", "w2", "t2", "m2"]
                return order[i - 1]

            def proj(a, b):
                both = ATT[a]["kind"] in ("self", "win")
                for t, m in split_order(a):
                    split(t, a, b, m, L)
                if both:
                    dve.wait_ge(sem("ld_" + a), at("ld_" + a, "all"))
                    for g in range(2):
                        src = filled(dve, ("v", a, b, g))
                        dve.tensor_tensor(vs[:, 4 * g:4 * g + 4, :, 0:D], src.rearrange("p (t h d) -> p t h d", t=4, h=H),
                                          vbias[:, ATT[a]["half"], :].rearrange("p (h d) -> p h d", h=H).unsqueeze(1).to_broadcast([P, 4, H, D]),
                                          ALU.add).then_inc(free(("v", a, b, g)), 1)

            def attn(a, b):
                kind = ATT[a]["kind"]
                units = first_pass_units(kind)
                nk = S if kind in ("cross", "top") else P
                start, ahead = side_plan(kind)

                def maxima(p, u):
                    src = filled(dve, ("p1", a, b, p, u))
                    if u == 0 and p >= MP:
                        filled(dve, ("t", a, b, p - MP))
                    if u == 0 and p < MP and call_before(a, b):
                        filled(dve, ("t", *call_before(a, b), HP - MP + p))
                    src = src[:, 0:512]
                    if kind == "self":
                        j, t, n = units[u]
                        dst, v = mhalves[:, p % 2, n, j, t:t + 1], src
                    else:
                        dst = m16[:, p % MP, :, 2 * u:2 * u + 2].rearrange("p j q -> p q j")
                        v = src.rearrange("p (q n) -> p q n", q=2)[:, :, 0:2 * nk].rearrange("p q (j s) -> p q j s", j=2)
                    dve.tensor_reduce(dst, v, AX.X, ALU.max, negate=True).then_inc(free(("p1", a, b, p, u)), 1)
                    if kind == "self" and u == len(units) - 1:
                        emptied(dve, ("p1", a, b, p, u - 1))
                        emptied(dve, ("p1", a, b, p, u))
                        dve.tensor_tensor(m16[:, p % MP], mhalves[:, p % 2, 0], mhalves[:, p % 2, 1], ALU.min
                                          ).then_inc(sem("maxed"), mark("maxed", a, b, p))

                def wide_maxima(p, u):
                    src = filled(dve, ("wide", a, b, p, u))
                    if u == 0:
                        filled(dve, ("t", *call_before(a, b), HP - MP + p))
                    j, t = divmod(u, TB)
                    dve.tensor_reduce(m16[:, p % MP, j, t:t + 1], src, AX.X, ALU.max, negate=True).then_inc(free(("wide", a, b, p, u)), 1)

                def turned_out(p):
                    n = mrow_no(a, b, p)
                    if n >= MP:
                        dve.wait_ge(sem(f"mrow{p % MP}"), 32 * (n // MP))
                    src = filled(dve, ("t", a, b, p))
                    dve.tensor_copy(mt[:, p % MP, :], src.bitcast(F16)[0:2 * TB, 0:P]).then_inc(free(("t", a, b, p)), 1)

                def keep_top(p, u):
                    n = 2 * p + u
                    sc, w = top_s[n % 2], top_w[n % 2]
                    emptied(dve, ("p1", a, b, p, 2 * u))
                    emptied(dve, ("p1", a, b, p, 2 * u + 1))
                    rows = [(slice(None), r // 4, slice(r % 4 * S, (r % 4 + 1) * S)) for r in range(8)]
                    if n >= 2 or b:
                        before = (a, b, (n - 2) // 2, n % 2) if n >= 2 else (a, b - 1, HP - 1, n)
                        dve.wait_ge(sem("topd"), at("topd", *before))
                    for r in range(8):
                        i = dve.max(v8[:, n % 2, r, :], sc[rows[r]])
                    i.then_inc(sem("topm"), mark("topm", a, b, p, u))
                    dve.wait_ge(sem("topm"), at("topm", a, b, p, u))
                    if n >= 2:
                        dve.wait_ge(sem("topp"), at("topp", a, b, (n - 2) // 2, n % 2))
                    elif b:
                        dve.wait_ge(sem("topp"), at("topp", a, b - 1, HP - 1, n % 2))
                    for r in range(8):
                        i = dve.match_replace(w[rows[r]], v8[:, n % 2, r, :], sc[rows[r]], TOPK_GONE)
                    linked(i)
                    for r in range(8):
                        i = dve.max(v8[:, 2, r, :], w[rows[r]])
                    linked(i)
                    for r in range(8):
                        i = dve.match_replace(w[rows[r]], v8[:, 2, r, :], w[rows[r]], TOPK_GONE)
                    i.then_inc(sem("topw"), mark("topw", a, b, p, u))

                def side(tasks):
                    for t in tasks:
                        if kind == "top":
                            keep_top(t[1], t[2])
                        elif t[0] == "wide":
                            wide_maxima(t[1], t[2])
                        else:
                            maxima(t[1], t[2]) if t[0] == "p1" else turned_out(t[1])

                def normalize(g, last, part):
                    if part:
                        return turn_back(g)
                    gn = group_no[(a, b, g)]
                    dve.wait_ge(sem("pv"), at("pv", a, b, last))
                    if gn:
                        dve.wait_ge(sem("on"), gn)
                    dve.transpose(turned, sl[2]).then_inc(sem("free2"), 1)
                    emptied(dve, ("o", a, b, g))
                    tv = turned.rearrange("p (q d) -> p q d", d=32)
                    linked(dve.reciprocal(rec[:], tv[:, :, D]))
                    linked(dve.tensor_tensor(tv[:, :, 0:D], tv[:, :, 0:D], rec[:].unsqueeze(2).to_broadcast([P, 32, D]), ALU.mult))

                def turn_back(g):
                    gn = group_no[(a, b, g)]
                    if gn:
                        pb = group_key(gn - 1)
                        dve.wait_ge(sem(f"pack{pb[2] % 2}"), at(f"pack{pb[2] % 2}", *pb))
                    if kind == "win":
                        dve.transpose(onorm[:, SHIFT:L], turned[:, 0:L - SHIFT])
                        dve.transpose(onorm[:, 0:SHIFT], turned[:, L - SHIFT:L]).then_inc(sem("on"), mark("on", a, b, g))
                    else:
                        dve.transpose(onorm[:], turned).then_inc(sem("on"), mark("on", a, b, g))

                side(start)
                if norms_ahead:
                    ln(*norms_ahead.pop())
                steps = steps_of(kind)
                per = len(steps) // (H // GH)
                for i, (p, j, kt) in enumerate(steps):
                    side(ahead[i])
                    if i > GH and i % per in (2, 3):
                        normalize(p // 2 - 1, i - i % per - 1, i % per - 2)
                for part in range(2):
                    normalize(H // GH - 1, len(steps) - 1, part)

            def group_key(n):
                return next(k for k, v in group_no.items() if v == n)

            added = []
            norms_ahead = []

            def update(s, b, r, gate):
                src = filled(dve, ("post", s, b, r)).rearrange("p (t c) -> p t c", t=4)
                dve.wait_ge(sem("xb"), at("xb", s, b))
                xs = x[:, b * TB + 4 * r:b * TB + 4 * r + 4, :]
                if gate is None:
                    dve.tensor_tensor(xs, src, xs, ALU.add).then_inc(free(("post", s, b, r)), 1)
                    emptied(dve, ("post", s, b, r))
                    dve.memset(rec[:, 0:1], 0.0).then_inc(sem("xu"), mark("xu", s, b, r))
                else:
                    g = gates[:, gate, b, :].unsqueeze(1).to_broadcast([P, 4, C])
                    tmp = onorm[:].rearrange("p (t c) -> p t c", t=4)
                    if added:
                        dve.wait_ge(sem("xu"), at("xu", *added[-1]))
                    added.append((s, b, r))
                    dve.tensor_tensor(tmp, src, g, ALU.mult).then_inc(free(("post", s, b, r)), 1)
                    emptied(dve, ("post", s, b, r))
                    dve.tensor_tensor(xs, tmp, xs, ALU.add).then_inc(sem("xu"), mark("xu", s, b, r))

            def post(a, b):
                for g in range(2):
                    update(a, b, g, ATT[a]["gate"])

            def mlp(m, b, lowering):
                hb = MLP[m]["hb"]
                for r in () if lowering else range(2):
                    for ch in range(8):
                        dve.wait_ge(sem("silu"), at("silu", m, b, r, ch))
                        y = hid32[:, ch % 2, :]
                        if m == "m2":
                            src = filled(dve, ("up", m, b, r, ch))
                            dve.scalar_tensor_tensor(out=y, in0=src[:, 512:1024], scalar=cols[:, hb + 8 + ch:hb + 9 + ch],
                                                     in1=y, op0=ALU.add, op1=ALU.mult).then_inc(free(("up", m, b, r, ch)), 1)
                            emptied(dve, ("up", m, b, r, ch))
                            linked(dve.tensor_copy(hid[:, r, 0, ch, :], y))
                        elif ch % 2:
                            emptied(dve, ("up", m, b, r, ch // 2))
                        else:
                            dve.wait_ge(sem("uhigh"), at("uhigh", m, b, r, ch))
                        dve.tensor_tensor(hid[:, r, 1, ch, :], y, hid[:, r, 0, ch, :], ALU.subtract).then_inc(sem("low"), mark("low", m, b, r, ch))
                if not lowering:
                    return
                dve.wait_ge(sem("low"), at("low", m, b, 1, 7))
                beside = sched[sched.index(("down", m, b)) - 1]
                if beside[0] == "turn":
                    emptied(dve, ("ln", *beside[1:], CC - 1))
                for r in range(2):
                    update(m, b, r, MLP[m]["gate"])

            def prep3(part):
                if part == "values":
                    values3()
                    return
                filled(dve, ("post", "m2", B - 1, 1))
                src = filled(dve, ("wqt",))
                dve.tensor_copy(wqt, src[:, 0:512].rearrange("p (c n) -> p c n", c=CC)).then_inc(free(("wqt",)), 1)
                for name, dst in (("kt3", kt3), ("vt3", vt3)):
                    src = filled(dve, (name,))
                    dve.tensor_copy(dst.rearrange("p c b s -> p c (b s)"), src.rearrange("p (c n) -> p c n", c=CC)[:, :, 0:B * S]
                                    ).then_inc(free((name,)), 1)
                src = filled(dve, ("g3",))
                gv = [g3[:, h].rearrange("p c b s -> p c (b s)") for h in range(2)]
                src = src.rearrange("p (c n) -> p c n", c=CC)[:, :, 0:B * S]
                linked(dve.tensor_copy(gv[0], src))
                dve.tensor_tensor(gv[1], src, gv[0], ALU.subtract).then_inc(free(("g3",)), 1)
                dve.wait_ge(sem("ld_l3"), at("ld_l3", "all"))
                linked(dve.tensor_copy(wrs[:, 0], wr[:, 0:CC, :]))
                dve.tensor_tensor(wrs[:, 1], wr[:, 0:CC, :], wrs[:, 0], ALU.subtract).then_inc(sem("wrs"), 1)
                for b in range(B):
                    for c in range(CC):
                        i = dve.tensor_copy(condb[:, b, c, :], cols[:, b * CC + c:b * CC + c + 1].to_broadcast([P, P]))
                i.then_inc(sem("condb3"), 1)

            def values3():
                for b in range(B):
                    for g in range(2):
                        src = filled(dve, ("vw", b, g))
                        n = 1024 if g == 0 else VWN - 1024
                        at_ = slice(g * 1024, g * 1024 + n)
                        linked(dve.tensor_copy(vw[:, 0, b, at_], src[0:S, 0:n]))
                        dve.tensor_tensor(vw[:, 1, b, at_], src[0:S, 0:n], vw[:, 0, b, at_], ALU.subtract).then_inc(free(("vw", b, g)), 1)
                src = filled(dve, ("anchor",))
                c0 = COL["L3_xcond_e_b1"]
                dve.tensor_tensor(hb3.rearrange("p b n -> p n b"), src[:, 0:28].rearrange("p (n b) -> p n b", b=B),
                                  cols[:, c0:c0 + 14].unsqueeze(2).to_broadcast([P, 14, B]), ALU.add).then_inc(sem("hb3"), 1)
                dve.tensor_tensor(rb3, src[:, 512:520].rearrange("p (b n) -> p b n", b=B)[:, :, 0:NE],
                                  rbin.unsqueeze(1).to_broadcast([P, B, NE]), ALU.add).then_inc(free(("anchor",)), 1)

            def scores3(b):
                src = filled(dve, ("sc3", b))
                linked(dve.tensor_reduce(sm3[b][:, 0:8], src.rearrange("p (t n) -> p t n", t=TB)[:, :, 0:S], AX.X, ALU.max, negate=True))
                dve.tensor_scalar(bm3[b], sm3[b][:, 0:8], 1.0 / 16, None, ALU.mult).then_inc(sem("bm3"), mark("bm3", b))
                emptied(dve, ("sc3", b))
                linked(dve.reciprocal(rs3[b], sm3[b][:, 8:16]))
                dve.tensor_tensor(p3[b], p3[b], rs3[b].unsqueeze(2).to_broadcast([P, TB, S]), ALU.mult).then_inc(sem("p3"), mark("p3", b))

            def evidence(b):
                src = filled(dve, ("wt3", b))
                dve.wait_ge(sem("wthigh"), at("wthigh", b))
                dve.tensor_tensor(wt3[b][:, 1, :], src[0:S, :], wt3[b][:, 0, :], ALU.subtract).then_inc(free(("wt3", b)), 1)

            def router(b):
                src = filled(dve, ("lg3", b))
                emptied(dve, ("anchor",))
                dve.tensor_tensor(lg3[b], src[:, 0:32].rearrange("p (t e) -> p t e", t=TB)[:, :, 0:NE],
                                  rb3[:, b, :].unsqueeze(1).to_broadcast([P, TB, NE]), ALU.add).then_inc(free(("lg3", b)), 1)
                emptied(dve, ("lg3", b))
                linked(dve.tensor_reduce(lm3[b], lg3[b], AX.X, ALU.max))
                dve.tensor_tensor(lg3[b], lg3[b], lm3[b].unsqueeze(2).to_broadcast([P, TB, NE]), ALU.subtract).then_inc(sem("lgs"), mark("lgs", b))
                dve.wait_ge(sem("lge"), at("lge", b))
                linked(dve.tensor_reduce(ls3[b], lg3[b], AX.X, ALU.add))
                linked(dve.reciprocal(ls3[b], ls3[b]))
                dve.tensor_tensor(lg3[b], lg3[b], ls3[b].unsqueeze(2).to_broadcast([P, TB, NE]), ALU.mult).then_inc(sem("rp3"), mark("rp3", b))
                dve.wait_ge(sem("rp3"), at("rp3", b))

            def hidden3(b, r, j):
                for ch in (2 * j, 2 * j + 1):
                    dve.wait_ge(sem("silu"), at("silu", "moe", b, r, ch))
                    if ch % 2:
                        emptied(dve, ("h3", b, r, j))
                    else:
                        dve.wait_ge(sem("uhigh"), at("uhigh", "moe", b, r, ch))
                    dve.tensor_tensor(hid3[:, 1, ch, :], hid32[:, ch % 2, :], hid3[:, 0, ch, :], ALU.subtract
                                      ).then_inc(sem("low"), mark("low", "moe", b, r, ch))

            def probs3(b):
                pass

            def experts3(b, r):
                for t in range(4):
                    src = filled(dve, ("ex3", b, r, t))
                    acc = xn[:, t, :]
                    linked(dve.tensor_copy(acc, src[:, 768:1024]))
                    for e in range(NE):
                        i = dve.scalar_tensor_tensor(out=acc, in0=src[:, e * C:(e + 1) * C], scalar=lg3[b][:, 4 * r + t, e:e + 1], in1=acc,
                                                     op0=ALU.mult, op1=ALU.add)
                        if e < NE - 1:
                            linked(i)
                    i.then_inc(free(("ex3", b, r, t)), 1)

            def routed3(b, r):
                src = filled(dve, ("rt3", b, r))
                dve.wait_ge(sem("rthigh"), at("rthigh", b, r))
                dve.tensor_tensor(rt3[:, 1], src.rearrange("p (c n) -> p c n", c=CC), rt3[:, 0], ALU.subtract).then_inc(free(("rt3", b, r)), 1)

            def gated3(b, r):
                dve.wait_ge(sem("ld_b3"), at("ld_b3", "all"))
                for g in range(2):
                    src = filled(dve, ("y3", b, r, g))
                    dve.tensor_tensor(gz_of(g).rearrange("p (t c) -> p t c", t=2), src[:, 512:1024].rearrange("p (t c) -> p t c", t=2),
                                      obias[:, 0, :].unsqueeze(1).to_broadcast([P, 2, C]), ALU.add).then_inc(sem("gz"), mark("gz", b, r, g))
                    y = xnf[:, g * 512:(g + 1) * 512]
                    dve.tensor_tensor(y.rearrange("p (t c) -> p t c", t=2), src[:, 0:512].rearrange("p (t c) -> p t c", t=2),
                                      obias[:, 1, :].unsqueeze(1).to_broadcast([P, 2, C]), ALU.add).then_inc(free(("y3", b, r, g)), 1)
                for g in range(2):
                    y = xnf[:, g * 512:(g + 1) * 512]
                    emptied(dve, ("y3", b, r, g))
                    dve.wait_ge(sem("tanh"), at("tanh", b, r, g))
                    linked(dve.scalar_tensor_tensor(out=y, in0=gz_of(g), scalar=1.0, in1=y, op0=ALU.add, op1=ALU.mult))
                    xs = x[:, b * TB + 4 * r + 2 * g:b * TB + 4 * r + 2 * g + 2, :].rearrange("p t c -> p (t c)")
                    dve.scalar_tensor_tensor(out=xs, in0=y, scalar=0.5, in1=xs, op0=ALU.mult, op1=ALU.add
                                             ).then_inc(sem("xu"), mark("xu", "moe", b, 2 * r + g))
                dve.wait_ge(sem("xu"), at("xu", "moe", b, 2 * r + 1))

            run = {"prep": prep, "mods": mod_stage, "ckv": ckv, "norm": ln, "turn": turn, "proj": proj, "attn": attn,
                   "post": post, "up": lambda m, b: mlp(m, b, False),
                   "down": lambda m, b: mlp(m, b, True), "prep3": prep3, "scores3": scores3, "evidence": evidence, "router": router,
                   "hidden3": hidden3, "probs3": probs3, "experts3": experts3, "routed3": routed3, "gated3": gated3}
            for s in sched:
                if s in relaxed:
                    norms_ahead.append(s[1:])
                else:
                    run[s[0]](*s[1:])

        @block.gpsimd
        def _(pool):
            def prep():
                pool.memset(identf[:], 0.0).then_inc(sem("ident"), mark("ident", "z"))
                pool.wait_ge(sem("ident"), at("ident", "z"))
                pool.affine_select(out=identf[:], in_=identf[:], compare_op=ALU.not_equal, fill=1.0, base=0,
                                   pattern=[[-1, P]], channel_multiplier=1).then_inc(sem("ident"), mark("ident", "f"))
                pool.wait_ge(sem("ident"), at("ident", "f"))
                pool.tensor_copy(identh[:], identf[:]).then_inc(sem("ident"), mark("ident", "h"))
                pool.wait_ge(sem("ident"), at("ident", "h"))
                pool.memset(vsf, 1.0).then_inc(sem("vones"), 1)
                pool.wait_ge(sem("vones"), 1)
                split_weights("x0", None)
                pool.wait_ge(sem("mv"), at("mv", "ctx"))
                pool.wait_ge(sem("mhalf"), 1)
                for v, eps in ((0, 1e-5), (1, 1e-6)):
                    pool.tensor_scalar(vare[0:S, 4 * v:4 * v + 2], mv[0:S, 0:2, 1], eps, None, ALU.add).then_inc(sem("vare"), mark("vare", "ctx", v))
                    pool.wait_ge(sem("vare"), at("vare", "ctx", v))
                    i = pool.tensor_tensor(rstd[0:S, 4 * v:4 * v + 2], vare[0:S, 4 * v:4 * v + 2], mhalf[0:S, 0:2], ALU.pow)
                i.then_inc(sem("rstd"), mark("rstd", "ctx"))
                pool.wait_ge(sem("rstd"), at("rstd", "ctx"))
                pool.wait_ge(sem("kzero"), at("kzero", 0))
                kv = ks[:].rearrange("p (a two) n -> p a two n", two=2)
                pool.memset(kv[ROWM:ROWM + 1, :, 0, :], 1.0)
                pool.memset(kv[64 + ROWM:64 + ROWM + 1, :, 1, :], 1.0).then_inc(sem("kzero"), mark("kzero", 1))
                pool.wait_ge(sem("kzero"), at("kzero", 1))

            def split_weights(name, after):
                parts = pieces_of(name)
                if after:
                    filled(pool, after)

                def place(n):
                    src = parts[n][0]
                    c, w = src.shape[1], src.shape[2]
                    return stage[:, stage_no[name, n] % 2, 0:c * w].rearrange("p (c n) -> p c n", c=c)

                def load(n):
                    k = stage_no[name, n] % 2
                    pool.dma_start(place(n), parts[n][0]).then_inc(sem(f"staged{k}"), mark(f"staged{k}", name, n, by=16))

                load(0)
                for n, (_, high, low) in enumerate(parts):
                    if n + 1 < len(parts):
                        load(n + 1)
                    k = stage_no[name, n] % 2
                    pool.wait_ge(sem(f"staged{k}"), at(f"staged{k}", name, n))
                    pool.tensor_copy(high, place(n)).then_inc(sem("wsplit"), mark("wsplit", name, n, 0))
                    pool.wait_ge(sem("wsplit"), at("wsplit", name, n, 0))
                    pool.tensor_tensor(low, place(n), high, ALU.subtract).then_inc(sem("sp_" + name), mark("sp_" + name, "all"))
                    pool.wait_ge(sem("sp_" + name), n + 1)

            stage_no = {}
            for name in ("x0", "s1", "x1", "m1", "w2", "t2", "m2", "moe", "ow"):
                for n in range(len(pieces_of(name))):
                    stage_no[name, n] = n + (name == "ow")

            def ln(i, b):
                pool.wait_ge(sem("mv"), at("mv", i, b))
                pool.tensor_scalar(vare[:], mv[:, :, 1], LN_EPS[i], None, ALU.add).then_inc(sem("vare"), mark("vare", i, b))
                pool.wait_ge(sem("vare"), at("vare", i, b))
                pool.tensor_tensor(rstd[:], vare[:], mhalf[:], ALU.pow).then_inc(sem("rstd"), mark("rstd", i, b))
                pool.wait_ge(sem("rstd"), at("rstd", i, b))
                prev = ln_calls.index(("ln", i, b)) - 1
                if prev >= 0:
                    filled(pool, (*ln_calls[prev], CC - 1))
                for t in range(TB) if ("norm", i, b) in relaxed else ():
                    pool.tensor_scalar(xn[:, t, :], x[:, b * TB + t, :], mv[:, t, 0:1], rstd[:, t:t + 1],
                                       ALU.subtract, ALU.mult).then_inc(sem(xn_sem(i, b)), mark(xn_sem(i, b), i, b, t))
                    pool.wait_ge(sem(xn_sem(i, b)), at(xn_sem(i, b), i, b, t))
                if i == 7:
                    return
                s = ["x0", "s1", "x1", "m1", "w2", "t2", "m2"][i]
                d = ATT.get(s) or MLP[s]
                row = obias[:, d.get("half", 2), :]
                if ("norm", i, b) not in relaxed:
                    pool.wait_ge(sem(xn_sem(i, b)), at(xn_sem(i, b), i, b, TB - 1))
                pool.wait_ge(sem("ld_" + s), at("ld_" + s, "all"))
                if d["gate"] is not None:
                    emptied(pool, ("gate", d["gate"]))
                    pool.tensor_tensor(gbias[:], row, gates[:, d["gate"], b, :], ALU.mult).then_inc(sem("gbias"), mark("gbias", s, b))
                    pool.wait_ge(sem("gbias"), at("gbias", s, b))
                    row = gbias[:]
                xs = x[:, b * TB:(b + 1) * TB, :]
                pool.tensor_tensor(xs, xs, row.unsqueeze(1).to_broadcast([P, TB, C]), ALU.add).then_inc(sem("xb"), mark("xb", s, b))
                pool.wait_ge(sem("xb"), at("xb", s, b))

            def proj(a, b):
                prev = call_before(a, b)
                if prev:
                    filled(pool, last_reader(*prev, HP - 1))
                else:
                    pool.wait_ge(sem("qzero"), 1)
                v = qs[:].rearrange("p a b -> p (a b)").bitcast(U32)
                pool.memset(v[ROWM:ROWM + 1, :], 0)
                pool.memset(v[64 + ROWM:64 + ROWM + 1, :], 0).then_inc(sem("mzero"), mark("mzero", a, b))
                pool.wait_ge(sem("mzero"), at("mzero", a, b))

            def attn_top(a, b):
                start, ahead = side_plan("top")
                for tasks in [start] + ahead:
                    for _, p, u in tasks:
                        n = 2 * p + u
                        emptied(pool, ("p1", a, b, p, 2 * u))
                        emptied(pool, ("p1", a, b, p, 2 * u + 1))
                        pool.wait_ge(sem("topm"), at("topm", a, b, p, u))
                        if n >= 4:
                            filled(pool, ("s", a, b, 2 * ((n - 4) // 2) + 1))
                        elif b:
                            filled(pool, ("s", a, b - 1, 2 * ((n + 12) // 2) + 1))
                        else:
                            filled(pool, last_reader(*call_before(a, b), HP - 1))
                            pool.wait_ge(sem("pv"), at("pv", *call_before(a, b), len(steps_of("win")) - 1))
                        pool.tensor_tensor(top_p[n % 4].rearrange("p (h r s) -> p h r s", h=2, r=4),
                                           top_s[n % 2].rearrange("p h (r s) -> p h r s", r=4),
                                           v8[:, n % 2, :, 0:1].rearrange("p (h r) o -> p h r o", h=2).to_broadcast([P, 2, 4, S]), ALU.subtract).then_inc(sem("topd"), mark("topd", a, b, p, u))
                        pool.wait_ge(sem("topd"), at("topd", a, b, p, u))
                        pool.wait_ge(sem("topw"), at("topw", a, b, p, u))
                        pool.tensor_scalar(top_w[n % 2], top_w[n % 2], TOPK_GONE / 2, None, ALU.is_le).then_inc(sem("topk"), mark("topk", a, b, p, u))
                        pool.wait_ge(sem("topk"), at("topk", a, b, p, u))
                        pool.wait_ge(sem("tope"), at("tope", a, b, p, u))
                        p_ = top_p[n % 4].rearrange("p (h s) -> p h s", h=2)
                        pool.tensor_tensor(p_, top_w[n % 2], p_, ALU.mult).then_inc(sem("topp"), mark("topp", a, b, p, u))
                        pool.wait_ge(sem("topp"), at("topp", a, b, p, u))

            names = [s[1] for s in sched if s[0] in ("attn", "down")] + ["moe" for s in sched if s[0] == "probs3"]
            for s in sched:
                for name, after in SPLIT_AT.get(s, []):
                    if name in names or name == "ow":
                        split_weights(name, after)
                if s[0] == "prep":
                    prep()
                elif s[0] == "norm":
                    ln(*s[1:])
                elif s[0] == "proj":
                    proj(*s[1:])
                elif s[0] == "attn" and ATT[s[1]]["kind"] == "top":
                    attn_top(*s[1:])

        @block.sync
        def _(sp):
            def rows(ap, n):
                return ap.rearrange("(c p) n -> p c n", p=P)

            def bc(ap):
                return ap.rearrange("(o n) -> o n", o=1).to_broadcast([P, ap.shape[0]])

            def load_att(a):
                d = ATT[a]
                for v, w in zip(att_views(a)[1:] if len(d["w"]) == 3 else att_views(a)[2:], d["w"][1:]):
                    sp.dma_start(v, rows(ins[w], 0)).then_inc(sem("ld_" + a), mark("ld_" + a, "w", by=16))
                name, lo = d["vb"]
                sp.dma_start(vbias[:, d["half"], :], bc(ins[name][lo:lo + C])).then_inc(sem("ld_" + a), mark("ld_" + a, "w", by=16))
                sp.dma_start(obias[:, d["half"], :], bc(ins[d["ob"]])).then_inc(sem("ld_" + a), mark("ld_" + a, "all", by=16))

            def load_mlp(m):
                d = MLP[m]
                sp.dma_start(obias[:, 2, :], bc(ins[d["ob"]])).then_inc(sem("ld_" + m), mark("ld_" + m, "all", by=16))

            def load_gates(layer):
                name = {1: "L1_xcond_b_mod", 2: "L2_xcond_b_ada"}[layer]
                for g, (ly, i) in enumerate(GATES):
                    if ly == layer:
                        for b in range(B):
                            sp.dma_start(gates[:, g, b, :], bc(ins[name][i * C:(i + 1) * C])
                                         ).then_inc(sem(f"ld_g{layer}"), mark(f"ld_g{layer}", "all", by=16))

            def prep():
                n = 0
                for name, lo, k in COLUMN_ROWS:
                    src = ins[name]
                    if len(src.shape) == 2:
                        src = src.rearrange("a n -> (a n)")
                    src = src[lo:lo + k * P].rearrange("(k p) -> k p", p=P)
                    sp.dma_start(crow[n:n + k, :], src).then_inc(sem("ld_cols"), mark("ld_cols", "all", by=16))
                    n += k
                sp.dma_start(cx, ins["ctx_1024"].rearrange("b s c -> s b c")).then_inc(sem("ld_ctx"), 16)
                for w in ("ssq", "sskv"):
                    sp.dma_start(mod_w[w], rows(ins[mod_in[w]], 0)).then_inc(sem("ld_ss"), 16)
                sp.dma_start(mod_w["mod1"], rows(ins[mod_in["mod1"]], 0)).then_inc(sem("ld_mod1"), 16)
                load_att("x0")
                load_gates(1)
                load_gates(2)
                if "s1" in [s[1] for s in sched if s[0] == "attn"]:
                    load_att("s1")

            def stack(t, a, b, m, n):
                j = split_no[(a, t, b, m)]
                emptied(sp, (t, a, b, m))
                sp.dma_start(scratch[j, :, :, 0:n].rearrange("s p n -> p s n"), st[:, j % 2, :, 0:n]
                             ).then_inc(sem(f"stout{j % 2}"), mark(f"stout{j % 2}", j, by=16))
                if m == 0:
                    stack_in(sp, t, a, b, m, n)

            def ckv(a):
                for m in range(CC):
                    stack("k", a, "c", m, B * S)

            def proj(a, b):
                for t, m in split_order(a):
                    stack(t, a, b, m, L)

            def attn(a, b):
                kind = ATT[a]["kind"]
                start, ahead = side_plan(kind)

                def side(tasks):
                    for t in tasks:
                        if t[0] == "t":
                            p = t[1]
                            emptied(sp, ("t", a, b, p))
                            for j in range(2):
                                sp.dma_start(qs[64 * j + ROWM:64 * j + ROWM + 1, p, :].rearrange("o (t n) -> o t n", t=TB),
                                             mt[TB * j:TB * (j + 1), p % MP, :]
                                             ).then_inc(sem(f"mrow{p % MP}"), mark(f"mrow{p % MP}", a, b, p, by=16))

                def pack(g):
                    sp.wait_ge(sem("on"), at("on", a, b, g))
                    for j in range(GH):
                        h = g * GH + j
                        sp.dma_start(ht[D * (h % 8):D * (h % 8) + D, b, h // 8, :], onorm[32 * j:32 * j + D, :]
                                     ).then_inc(sem(f"pack{g % 2}"), mark(f"pack{g % 2}", a, b, g, by=16))

                side(start)
                steps = steps_of(kind)
                per = len(steps) // (H // GH)
                for i, (p, j, kt) in enumerate(steps):
                    side(ahead[i])
                    if i > GH and i % per == 2:
                        pack(p // 2 - 1)
                pack(H // GH - 1)

            names = [s[1] for s in sched if s[0] == "attn"] + [s[1] for s in sched if s[0] == "down"]

            def post(a, b):
                if b < B - 1:
                    return
                nxt = {"x0": "x1", "s1": "w2", "x1": "t2"}.get(a)
                if nxt in names:
                    filled(sp, ("post", a, b, 1))
                    sp.wait_ge(sem("xb"), at("xb", a, b))
                    load_att(nxt)
                if a == "t2" and "prep3" in stages:
                    load_l3()

            def mod_stage(n):
                if n == 1:
                    filled(sp, ("gate", 1))
                    sp.dma_start(mod_w["ada2"], rows(ins[mod_in["ada2"]], 0)).then_inc(sem("ld_ada2"), 16)
                if n == 2 and "m1" in names:
                    filled(sp, ("gate", 4))
                    load_mlp("m1")

            def mlp(m, b, lowering):
                if not lowering:
                    return
                if m == "m1" and b == B - 1 and "m2" in names:
                    filled(sp, ("post", m, b, 1))
                    sp.wait_ge(sem("xb"), at("xb", m, b))
                    load_mlp("m2")
                if m == "m2" and b == B - 1 and "prep3" in stages:
                    sp.wait_ge(sem("sp_moe"), at("sp_moe", "all"))
                    ld3(w3v, rows(ins["L3_xcond_Wv"], 0))
                    filled(sp, ("post", m, b, 1))
                    sp.wait_ge(sem("xb"), at("xb", m, b))
                    load_l3b()

            def ld3(dst, src):
                sp.dma_start(dst, src).then_inc(sem("ld_l3"), mark("ld_l3", "all", by=16))

            def load_l3():
                filled(sp, ("post", "t2", B - 1, 1))
                for part, r0 in (("ev", C), ("an", 2 * C)):
                    for e in range(NE):
                        ld3(w3[part][:, :, e * RH:(e + 1) * RH], rows(ins["L3_xcond_e_w1"][e, r0:r0 + C, :], 0))
                    ld3(w3[part][:, :, NE * RH:NX], rows(ins["L3_xcond_gate_w1"][r0:r0 + C, :], 0))
                ld3(w3q, rows(ins["L3_xcond_Wq"], 0))
                ld3(w3k, rows(ins["L3_xcond_Wk"], 0))
                ld3(wr[:], rows(ins["L3_xcond_router_W"], 0))
                for i, name in enumerate(("L3_xcond_gate_b2", "L3_xcond_out_b")):
                    sp.dma_start(obias[:, i, :], bc(ins[name])).then_inc(sem("ld_b3"), mark("ld_b3", "all", by=16))

            def load_l3b():
                ld3(rbin, bc(ins["L3_xcond_router_b"]))
                ld3(b2e, ins["L3_xcond_e_b2"])

            out_v = out.rearrange("b (t p) c -> p (b t) c", p=P)

            def nothing(*_):
                pass

            hidden3 = probs3 = experts3 = routed3 = nothing

            def gated3(b, r):
                for q in (2 * r, 2 * r + 1):
                    sp.wait_ge(sem("xu"), at("xu", "moe", b, q))
                    lo = b * TB + 2 * q
                    sp.dma_start(out_v[:, lo:lo + 2, :], x[:, lo:lo + 2, :]).then_inc(sem("stored"), mark("stored", "all", by=16))

            run = {"prep": prep, "mods": mod_stage, "ckv": ckv, "norm": lambda i, b: None, "turn": lambda i, b: None,
                   "proj": proj, "attn": attn, "post": post, "up": lambda m, b: mlp(m, b, False),
                   "down": lambda m, b: mlp(m, b, True), "prep3": lambda part: None, "scores3": lambda b: None, "evidence": lambda b: None,
                   "router": lambda b: None, "hidden3": hidden3, "probs3": probs3, "experts3": experts3, "routed3": routed3, "gated3": gated3}
            for s in sched:
                run[s[0]](*s[1:])
            if "probs3" not in stages:
                last = next(s for s in reversed(sched) if s[0] in ("attn", "down"))
                for b in range(B):
                    for r in range(2):
                        sp.wait_ge(sem("xu"), at("xu", last[1], b, r))
                sp.dma_start(out_v, x[:]).then_inc(sem("stored"), mark("stored", "all", by=16))
            sp.wait_ge(sem("stored"), at("stored", "all"))
    return seen


_INS = ['x', 'ctx_1024', 'cond_1024',
        'L0_xcond_Wq', 'L0_xcond_bq', 'L0_xcond_Wkv', 'L0_xcond_bkv', 'L0_xcond_Wp', 'L0_xcond_bp',
        'L0_xcond_Wss_q', 'L0_xcond_bss_q', 'L0_xcond_Wss_kv', 'L0_xcond_bss_kv',
        'L1_xcond_W_mod', 'L1_xcond_b_mod', 'L1_xcond_W_qkv', 'L1_xcond_b_qkv', 'L1_xcond_W_proj', 'L1_xcond_b_proj',
        'L1_xcond_W_qc', 'L1_xcond_b_qc', 'L1_xcond_W_kvc', 'L1_xcond_b_kvc', 'L1_xcond_W_cproj', 'L1_xcond_b_cproj',
        'L1_xcond_W_mlp1', 'L1_xcond_b_mlp1', 'L1_xcond_W_mlp2', 'L1_xcond_b_mlp2',
        'L2_xcond_w_ada', 'L2_xcond_b_ada', 'L2_xcond_w_qkv', 'L2_xcond_b_qkv', 'L2_xcond_w_so', 'L2_xcond_b_so',
        'L2_xcond_w_q', 'L2_xcond_b_q', 'L2_xcond_w_kv', 'L2_xcond_b_kv', 'L2_xcond_w_co', 'L2_xcond_b_co',
        'L2_xcond_w_m1', 'L2_xcond_b_m1', 'L2_xcond_w_m2', 'L2_xcond_b_m2',
        'L3_xcond_ln_gamma', 'L3_xcond_ln_beta', 'L3_xcond_Wq', 'L3_xcond_Wk', 'L3_xcond_Wv',
        'L3_xcond_router_W', 'L3_xcond_router_b', 'L3_xcond_e_w1', 'L3_xcond_e_b1', 'L3_xcond_e_w2', 'L3_xcond_e_b2',
        'L3_xcond_gate_w1', 'L3_xcond_gate_b1', 'L3_xcond_gate_w2', 'L3_xcond_gate_b2', 'L3_xcond_out_w', 'L3_xcond_out_b']


def kernel(_stop=None, **inputs):
    import numpy as _np
    import concourse.bacc as _bacc
    from concourse.bass_utils import run_bass_kernel_spmd as _run

    marks = None
    for _ in range(2):
        nc = _bacc.Bacc("TRN2", target_bir_lowering=False, num_devices=1)
        arrays, aps = {}, {}
        for name in _INS:
            a = _np.ascontiguousarray(inputs[name])
            arrays[f"in_{name}_dram"] = a
            aps[name] = nc.dram_tensor(f"in_{name}_dram", a.shape, mybir.dt.from_np(a.dtype), kind="ExternalInput").ap()
        out = nc.dram_tensor("out_0_dram", (B, L, C), F32, kind="ExternalOutput").ap()
        marks = build(nc, aps, out, marks, _stop)
    r = _run(nc, [arrays], core_ids=[0])
    return r.results[0]["out_0_dram"]
```
